# Optimizing a Trainium2 kernel written in Bass

```python
import numpy as np
import jax
import jax.numpy as jnp

def _softmax(x, axis=-1):
    return jax.nn.softmax(x, axis=axis)

def _gelu(x):
    return jax.nn.gelu(x, approximate=True)

def _silu(x):
    return jax.nn.silu(x)

def _sigmoid(x):
    return jax.nn.sigmoid(x)

def _layernorm(x, axis=-1, eps=1e-05):
    m = jnp.mean(x, axis=axis, keepdims=True)
    v = jnp.var(x, axis=axis, keepdims=True)
    return (x - m) / jnp.sqrt(v + eps)

def _scatter_add(tgt, idx, src, axis=0):
    return tgt.at[idx].add(src)

def _segment_sum(src, seg, n):
    return jax.ops.segment_sum(src, seg, n)
kernel_name = 'mk_vit_tower_cls_d2_tok_img768_r4_2c892a'

def setup_inputs(seed: int=0):
    np.random.seed(seed)
    _w = jnp.asarray

    def _rec_inputs():
        import jax
        import jax.numpy as jnp
        _rk = jax.random.key(seed)
        x = 7.57192e-06 + 1.00007 * jax.random.normal(jax.random.fold_in(_rk, 1), (16, 3, 112, 112), jnp.float32)
        cls_tok = 0.02 * jax.random.normal(jax.random.fold_in(_rk, 5), (1, 1, 192), jnp.float32)
        return (x, cls_tok)
    x, cls_tok = _rec_inputs()

    def _L0_tok_setup():
        import jax, jax.numpy as jnp
        import numpy as np
        K = 4
        STRIDE = 4
        EPS = 1e-05
        SLOPE = 0.01

        def conv2d(x, w, b, stride):
            out = jax.lax.conv_general_dilated(x, w, (stride, stride), 'VALID', dimension_numbers=('NCHW', 'OIHW', 'NCHW'))
            return out + b[None, :, None, None]

        def batchnorm(x, g, b, m, v):
            inv = g / jnp.sqrt(v + EPS)
            return x * inv[None, :, None, None] + (b - m * inv)[None, :, None, None]

        def leaky_relu(x):
            return jnp.where(x >= 0, x, SLOPE * x)

        def deform_conv(x, offset, w, b):
            B, C, H, W = x.shape
            Ho, Wo = (offset.shape[2], offset.shape[3])
            KK = K * K
            off = offset.reshape(B, KK, 2, Ho, Wo)
            kh = jnp.repeat(jnp.arange(K), K).astype(x.dtype)
            kw = jnp.tile(jnp.arange(K), K).astype(x.dtype)
            base_y = (jnp.arange(Ho) * STRIDE).astype(x.dtype)
            base_x = (jnp.arange(Wo) * STRIDE).astype(x.dtype)
            py = base_y[None, None, :, None] + kh[None, :, None, None] + off[:, :, 0]
            px = base_x[None, None, None, :] + kw[None, :, None, None] + off[:, :, 1]
            y0 = jnp.floor(py)
            x0 = jnp.floor(px)
            wy = py - y0
            wx = px - x0

            def corner(yc, xc):
                yi = yc.astype(jnp.int32)
                xi = xc.astype(jnp.int32)
                valid = (yi >= 0) & (yi < H) & (xi >= 0) & (xi < W)
                yi = jnp.clip(yi, 0, H - 1)
                xi = jnp.clip(xi, 0, W - 1)
                v = jax.vmap(lambda img, a, c: img[:, a, c])(x, yi, xi)
                return v * valid[:, None].astype(x.dtype)
            v00 = corner(y0, x0)
            v01 = corner(y0, x0 + 1)
            v10 = corner(y0 + 1, x0)
            v11 = corner(y0 + 1, x0 + 1)
            wy_ = wy[:, None]
            wx_ = wx[:, None]
            sampled = v00 * (1 - wy_) * (1 - wx_) + v01 * (1 - wy_) * wx_ + v10 * wy_ * (1 - wx_) + v11 * wy_ * wx_
            out = jnp.einsum('bckhw,ock->bohw', sampled, w.reshape(w.shape[0], C, KK))
            return out + b[None, :, None, None]
        key = jax.random.key(seed)
        ks = jax.random.split(key, 16)
        f32 = jnp.float32
        inp = {'x': jax.random.normal(ks[0], (64, 3, 224, 224), f32), 'stem_w': jax.random.normal(ks[1], (96, 3, 4, 4), f32) * 0.1, 'stem_b': jax.random.normal(ks[2], (96,), f32) * 0.05, 'bn1_g': jax.random.uniform(ks[3], (96,), f32, 0.5, 1.5), 'bn1_b': jax.random.normal(ks[4], (96,), f32) * 0.05, 'bn1_m': jax.random.normal(ks[5], (96,), f32) * 0.05, 'bn1_v': jax.random.uniform(ks[6], (96,), f32, 0.5, 1.5), 'off_w': jax.random.normal(ks[7], (32, 96, 4, 4), f32) * 0.02, 'off_b': jax.random.normal(ks[8], (32,), f32) * 0.02, 'dcn_w': jax.random.normal(ks[9], (192, 96, 4, 4), f32) * 0.05, 'dcn_b': jax.random.normal(ks[10], (192,), f32) * 0.05, 'bn2_g': jax.random.uniform(ks[11], (192,), f32, 0.5, 1.5), 'bn2_b': jax.random.normal(ks[12], (192,), f32) * 0.05, 'bn2_m': jax.random.normal(ks[13], (192,), f32) * 0.05, 'bn2_v': jax.random.uniform(ks[14], (192,), f32, 0.5, 1.5)}
        return inp
    _L0_tok_all = _L0_tok_setup()
    _L0_tok_in = {k: v for k, v in _L0_tok_all.items() if k in ('stem_w', 'stem_b', 'bn1_g', 'bn1_b', 'bn1_m', 'bn1_v', 'off_w', 'off_b', 'dcn_w', 'dcn_b', 'bn2_g', 'bn2_b', 'bn2_m', 'bn2_v')}
    del _L0_tok_all

    def _L0_attn_setup():
        import jax, jax.numpy as jnp
        import numpy as np
        INIT_RANGE = 0.02
        key = jax.random.key(seed)
        ks = jax.random.split(key, 5)
        B, S, D, H, Dh = (4, 512, 192, 12, 64)
        residual = jax.random.normal(ks[0], (B, S, D), dtype=jnp.float32)
        W_Q = jax.random.normal(ks[1], (H, D, Dh), dtype=jnp.float32) * INIT_RANGE
        W_K = jax.random.normal(ks[2], (H, D, Dh), dtype=jnp.float32) * INIT_RANGE
        W_V = jax.random.normal(ks[3], (H, D, Dh), dtype=jnp.float32) * INIT_RANGE
        W_O = jax.random.normal(ks[4], (H, Dh, D), dtype=jnp.float32) * INIT_RANGE
        b_Q = jnp.zeros((H, Dh), dtype=jnp.float32)
        b_K = jnp.zeros((H, Dh), dtype=jnp.float32)
        b_V = jnp.zeros((H, Dh), dtype=jnp.float32)
        b_O = jnp.zeros((D,), dtype=jnp.float32)
        return {'residual': residual, 'W_Q': W_Q, 'W_K': W_K, 'W_V': W_V, 'W_O': W_O, 'b_Q': b_Q, 'b_K': b_K, 'b_V': b_V, 'b_O': b_O}
    _L0_attn_all = _L0_attn_setup()
    _L0_attn_in = {k: v for k, v in _L0_attn_all.items() if k in ('W_Q', 'W_K', 'W_V', 'W_O', 'b_Q', 'b_K', 'b_V', 'b_O')}
    del _L0_attn_all

    def _L0_ffn_setup():
        import jax, jax.numpy as jnp
        import numpy as np
        N_HEAD = 8 * 0 + 12
        TOP_K = 2
        GELU_C = 0.7978845608028654

        def _gelu(x):
            return 0.5 * x * (1.0 + jnp.tanh(GELU_C * (x + 0.044715 * x * x * x)))

        def _layernorm_global(x, w, b, eps=1e-12):
            m = jnp.mean(x)
            v = jnp.var(x, ddof=1)
            return (x - m) / jnp.sqrt(v + eps) * w + b

        def _attn(x, W1_w, W1_b, W2_w, W2_b):
            B, N, D = x.shape
            h = N_HEAD
            dh = D // h
            qkv = x @ W1_w + W1_b
            Q, K, V = jnp.split(qkv, 3, axis=-1)
            q = Q.reshape(B, N, h, dh).transpose(0, 2, 3, 1)
            k = K.reshape(B, N, h, dh).transpose(0, 2, 1, 3)
            v = V.reshape(B, N, h, dh).transpose(0, 2, 3, 1)
            w = jax.nn.softmax(q @ k / jnp.sqrt(jnp.asarray(N, x.dtype)), axis=-1)
            out = (w @ v).reshape(B, N, h * dh)
            return out @ W2_w + W2_b

        def _moe(x, r_w, r_b, fc_w, fc_b, proj_w, proj_b):
            B, N, D = x.shape
            scores = x @ r_w + r_b
            gate = jax.nn.softmax(jnp.mean(scores, axis=1), axis=-1)
            vals, idx = jax.lax.top_k(gate, TOP_K)
            hmid = _gelu(jnp.einsum('bnd,edf->benf', x, fc_w) + fc_b[None, :, None, :])
            outs = jnp.einsum('benf,efd->bend', hmid, proj_w) + proj_b[None, :, None, :]
            k_outs = jnp.take_along_axis(outs, idx[:, :, None, None], axis=1)
            return jnp.sum(vals[:, :, None, None] * k_outs, axis=1)
        key = jax.random.key(seed)
        ks = jax.random.split(key, 16)
        B, N, D, E = (2, 512, 192, 8)
        H = 4 * D
        s = 0.02
        return {'x': jax.random.normal(ks[0], (B, N, D), jnp.float32), 'W1_w': jax.random.normal(ks[1], (D, 3 * D), jnp.float32) * s, 'W1_b': jnp.zeros((3 * D,), jnp.float32), 'W2_w': jax.random.normal(ks[2], (D, D), jnp.float32) * s, 'W2_b': jnp.zeros((D,), jnp.float32), 'r_w': jax.random.normal(ks[3], (D, E), jnp.float32) * s, 'r_b': jnp.zeros((E,), jnp.float32), 'fc_w': jax.random.normal(ks[4], (E, D, H), jnp.float32) * s, 'fc_b': jnp.zeros((E, H), jnp.float32), 'proj_w': jax.random.normal(ks[5], (E, H, D), jnp.float32) * s, 'proj_b': jnp.zeros((E, D), jnp.float32), 'ln1_w': jnp.ones((D,), jnp.float32), 'ln1_b': jnp.zeros((D,), jnp.float32), 'ln2_w': jnp.ones((D,), jnp.float32), 'ln2_b': jnp.zeros((D,), jnp.float32)}
    _L0_ffn_all = _L0_ffn_setup()
    _L0_ffn_in = {k: v for k, v in _L0_ffn_all.items() if k in ('W1_w', 'W1_b', 'W2_w', 'W2_b', 'r_w', 'r_b', 'fc_w', 'fc_b', 'proj_w', 'proj_b', 'ln1_w', 'ln1_b', 'ln2_w', 'ln2_b')}
    del _L0_ffn_all

    def _L1_attn_setup():
        import jax, jax.numpy as jnp
        import numpy as np
        D_MODEL = 192
        D_STATE = 64
        D_CONV = 4
        EXPAND = 2
        HEADDIM = 64
        D_INNER = EXPAND * D_MODEL
        NHEADS = D_INNER // HEADDIM
        CONV_DIM = D_INNER + 2 * D_STATE
        D_IN_PROJ = 2 * D_INNER + 2 * D_STATE + NHEADS
        BATCH, SEQLEN = (2, 256)
        EPS = 1e-05

        def _forward(x, ln_w, ln_b, W_in, conv_w, conv_b, dt_bias, A_log, D, rms_w, W_out):
            b, l, _ = x.shape
            mu = jnp.mean(x, -1, keepdims=True)
            var = jnp.mean((x - mu) ** 2, -1, keepdims=True)
            xn = (x - mu) * jax.lax.rsqrt(var + EPS) * ln_w + ln_b
            zxbcdt = xn @ W_in
            z = zxbcdt[..., :D_INNER]
            xBC = zxbcdt[..., D_INNER:D_INNER + CONV_DIM]
            dt_raw = zxbcdt[..., -NHEADS:]
            xp = jnp.pad(xBC, ((0, 0), (D_CONV - 1, 0), (0, 0)))
            xBC = sum((xp[:, k:k + l, :] * conv_w[:, k] for k in range(D_CONV))) + conv_b
            xBC = jax.nn.silu(xBC)
            xh = xBC[..., :D_INNER].reshape(b, l, NHEADS, HEADDIM)
            Bm = xBC[..., D_INNER:D_INNER + D_STATE]
            Cm = xBC[..., D_INNER + D_STATE:]
            dt = jax.nn.softplus(dt_raw + dt_bias)
            A = -jnp.exp(A_log)
            decay = jnp.exp(dt * A)

            def step(h, inp):
                dec_t, dt_t, x_t, B_t, C_t = inp
                h = h * dec_t[..., None, None] + (dt_t[..., None] * x_t)[..., None] * B_t[:, None, None, :]
                y = jnp.einsum('bhpn,bn->bhp', h, C_t)
                return (h, y)
            h0 = jnp.zeros((b, NHEADS, HEADDIM, D_STATE), x.dtype)
            seq = (decay.transpose(1, 0, 2), dt.transpose(1, 0, 2), xh.transpose(1, 0, 2, 3), Bm.transpose(1, 0, 2), Cm.transpose(1, 0, 2))
            _, ys = jax.lax.scan(step, h0, seq)
            y = ys.transpose(1, 0, 2, 3) + D[None, None, :, None] * xh
            y = y.reshape(b, l, D_INNER)
            g = y * jax.nn.silu(z)
            g = g * jax.lax.rsqrt(jnp.mean(g * g, -1, keepdims=True) + EPS) * rms_w
            return g @ W_out + x
        key = jax.random.key(seed)
        ks = jax.random.split(key, 8)
        n = lambda i, shape, s: jax.random.normal(ks[i], shape, jnp.float32) * s
        return {'x': n(0, (BATCH, SEQLEN, D_MODEL), 1.0), 'ln_w': jnp.ones((D_MODEL,), jnp.float32), 'ln_b': jnp.zeros((D_MODEL,), jnp.float32), 'W_in': n(1, (D_MODEL, D_IN_PROJ), 0.02), 'conv_w': n(2, (CONV_DIM, D_CONV), 0.2), 'conv_b': jnp.zeros((CONV_DIM,), jnp.float32), 'dt_bias': n(3, (NHEADS,), 0.5), 'A_log': jnp.log(jnp.linspace(1.0, 16.0, NHEADS, dtype=jnp.float32)), 'D': jnp.ones((NHEADS,), jnp.float32), 'rms_w': jnp.ones((D_INNER,), jnp.float32), 'W_out': n(4, (D_INNER, D_MODEL), 0.02)}
    _L1_attn_all = _L1_attn_setup()
    _L1_attn_in = {k: v for k, v in _L1_attn_all.items() if k in ('ln_w', 'ln_b', 'W_in', 'conv_w', 'conv_b', 'dt_bias', 'A_log', 'D', 'rms_w', 'W_out')}
    del _L1_attn_all

    def _L1_ffn_setup():
        import jax, jax.numpy as jnp
        import numpy as np
        B, S, D, F, E = (8, 512, 192, 768, 16)
        CAP = 64
        EPS = 1e-06

        def _switch_moe_block(x, ln_w, w_router, wi, wo):
            var = jnp.mean(jnp.square(x.astype(jnp.float32)), axis=-1, keepdims=True)
            normed = (x * jax.lax.rsqrt(var + EPS)).astype(x.dtype) * ln_w
            logits = jnp.einsum('bsd,de->bse', normed.astype(jnp.float32), w_router.astype(jnp.float32))
            probs = jax.nn.softmax(logits, axis=-1)
            expert_idx = jnp.argmax(probs, axis=-1)
            onehot = jax.nn.one_hot(expert_idx, E, dtype=jnp.float32)
            priority = jnp.cumsum(onehot, axis=1)
            keep = onehot * (priority <= CAP)
            pos = (priority - 1.0).astype(jnp.int32)
            dispatch = keep[..., None] * jax.nn.one_hot(pos, CAP, dtype=jnp.float32)
            expert_in = jnp.einsum('bsec,bsd->becd', dispatch, normed)
            h = jax.nn.relu(jnp.einsum('becd,edf->becf', expert_in, wi))
            expert_out = jnp.einsum('becf,efd->becd', h, wo)
            combined = jnp.einsum('bsec,becd->bsd', dispatch, expert_out)
            routed = jnp.sum(dispatch, axis=(2, 3)) > 0
            next_states = jnp.where(routed[..., None], combined.astype(x.dtype), normed)
            router_prob = jnp.max(probs, axis=-1, keepdims=True).astype(x.dtype)
            return x + router_prob * next_states
        key = jax.random.key(seed)
        k_x, k_r, k_wi, k_wo = jax.random.split(key, 4)
        x = jax.random.normal(k_x, (B, S, D), dtype=jnp.float32)
        ln_w = jnp.ones((D,), dtype=jnp.float32)
        w_router = jax.random.normal(k_r, (D, E), dtype=jnp.float32) * 0.02
        wi = jax.random.normal(k_wi, (E, D, F), dtype=jnp.float32) * D ** (-0.5)
        wo = jax.random.normal(k_wo, (E, F, D), dtype=jnp.float32) * F ** (-0.5)
        return {'x': x, 'ln_w': ln_w, 'w_router': w_router, 'wi': wi, 'wo': wo}
    _L1_ffn_all = _L1_ffn_setup()
    _L1_ffn_in = {k: v for k, v in _L1_ffn_all.items() if k in ('ln_w', 'w_router', 'wi', 'wo')}
    del _L1_ffn_all
    return {'x': x, 'cls_tok': cls_tok, 'L0_tok_stem_w': _L0_tok_in['stem_w'], 'L0_tok_stem_b': _L0_tok_in['stem_b'], 'L0_tok_bn1_g': _L0_tok_in['bn1_g'], 'L0_tok_bn1_b': _L0_tok_in['bn1_b'], 'L0_tok_bn1_m': _L0_tok_in['bn1_m'], 'L0_tok_bn1_v': _L0_tok_in['bn1_v'], 'L0_tok_off_w': _L0_tok_in['off_w'], 'L0_tok_off_b': _L0_tok_in['off_b'], 'L0_tok_dcn_w': _L0_tok_in['dcn_w'], 'L0_tok_dcn_b': _L0_tok_in['dcn_b'], 'L0_tok_bn2_g': _L0_tok_in['bn2_g'], 'L0_tok_bn2_b': _L0_tok_in['bn2_b'], 'L0_tok_bn2_m': _L0_tok_in['bn2_m'], 'L0_tok_bn2_v': _L0_tok_in['bn2_v'], 'L0_attn_W_Q': _L0_attn_in['W_Q'], 'L0_attn_W_K': _L0_attn_in['W_K'], 'L0_attn_W_V': _L0_attn_in['W_V'], 'L0_attn_W_O': _L0_attn_in['W_O'], 'L0_attn_b_Q': _L0_attn_in['b_Q'], 'L0_attn_b_K': _L0_attn_in['b_K'], 'L0_attn_b_V': _L0_attn_in['b_V'], 'L0_attn_b_O': _L0_attn_in['b_O'], 'L0_ffn_W1_w': _L0_ffn_in['W1_w'], 'L0_ffn_W1_b': _L0_ffn_in['W1_b'], 'L0_ffn_W2_w': _L0_ffn_in['W2_w'], 'L0_ffn_W2_b': _L0_ffn_in['W2_b'], 'L0_ffn_r_w': _L0_ffn_in['r_w'], 'L0_ffn_r_b': _L0_ffn_in['r_b'], 'L0_ffn_fc_w': _L0_ffn_in['fc_w'], 'L0_ffn_fc_b': _L0_ffn_in['fc_b'], 'L0_ffn_proj_w': _L0_ffn_in['proj_w'], 'L0_ffn_proj_b': _L0_ffn_in['proj_b'], 'L0_ffn_ln1_w': _L0_ffn_in['ln1_w'], 'L0_ffn_ln1_b': _L0_ffn_in['ln1_b'], 'L0_ffn_ln2_w': _L0_ffn_in['ln2_w'], 'L0_ffn_ln2_b': _L0_ffn_in['ln2_b'], 'L1_attn_ln_w': _L1_attn_in['ln_w'], 'L1_attn_ln_b': _L1_attn_in['ln_b'], 'L1_attn_W_in': _L1_attn_in['W_in'], 'L1_attn_conv_w': _L1_attn_in['conv_w'], 'L1_attn_conv_b': _L1_attn_in['conv_b'], 'L1_attn_dt_bias': _L1_attn_in['dt_bias'], 'L1_attn_A_log': _L1_attn_in['A_log'], 'L1_attn_D': _L1_attn_in['D'], 'L1_attn_rms_w': _L1_attn_in['rms_w'], 'L1_attn_W_out': _L1_attn_in['W_out'], 'L1_ffn_ln_w': _L1_ffn_in['ln_w'], 'L1_ffn_w_router': _L1_ffn_in['w_router'], 'L1_ffn_wi': _L1_ffn_in['wi'], 'L1_ffn_wo': _L1_ffn_in['wo']}

def reference(x, cls_tok, L0_tok_stem_w, L0_tok_stem_b, L0_tok_bn1_g, L0_tok_bn1_b, L0_tok_bn1_m, L0_tok_bn1_v, L0_tok_off_w, L0_tok_off_b, L0_tok_dcn_w, L0_tok_dcn_b, L0_tok_bn2_g, L0_tok_bn2_b, L0_tok_bn2_m, L0_tok_bn2_v, L0_attn_W_Q, L0_attn_W_K, L0_attn_W_V, L0_attn_W_O, L0_attn_b_Q, L0_attn_b_K, L0_attn_b_V, L0_attn_b_O, L0_ffn_W1_w, L0_ffn_W1_b, L0_ffn_W2_w, L0_ffn_W2_b, L0_ffn_r_w, L0_ffn_r_b, L0_ffn_fc_w, L0_ffn_fc_b, L0_ffn_proj_w, L0_ffn_proj_b, L0_ffn_ln1_w, L0_ffn_ln1_b, L0_ffn_ln2_w, L0_ffn_ln2_b, L1_attn_ln_w, L1_attn_ln_b, L1_attn_W_in, L1_attn_conv_w, L1_attn_conv_b, L1_attn_dt_bias, L1_attn_A_log, L1_attn_D, L1_attn_rms_w, L1_attn_W_out, L1_ffn_ln_w, L1_ffn_w_router, L1_ffn_wi, L1_ffn_wo):
    import jax
    import jax.numpy as jnp

    def _L0_tok_ref(x, stem_w, stem_b, bn1_g, bn1_b, bn1_m, bn1_v, off_w, off_b, dcn_w, dcn_b, bn2_g, bn2_b, bn2_m, bn2_v):
        import jax, jax.numpy as jnp
        import numpy as np
        K = 4
        STRIDE = 4
        EPS = 1e-05
        SLOPE = 0.01

        def conv2d(x, w, b, stride):
            out = jax.lax.conv_general_dilated(x, w, (stride, stride), 'VALID', dimension_numbers=('NCHW', 'OIHW', 'NCHW'))
            return out + b[None, :, None, None]

        def batchnorm(x, g, b, m, v):
            inv = g / jnp.sqrt(v + EPS)
            return x * inv[None, :, None, None] + (b - m * inv)[None, :, None, None]

        def leaky_relu(x):
            return jnp.where(x >= 0, x, SLOPE * x)

        def deform_conv(x, offset, w, b):
            B, C, H, W = x.shape
            Ho, Wo = (offset.shape[2], offset.shape[3])
            KK = K * K
            off = offset.reshape(B, KK, 2, Ho, Wo)
            kh = jnp.repeat(jnp.arange(K), K).astype(x.dtype)
            kw = jnp.tile(jnp.arange(K), K).astype(x.dtype)
            base_y = (jnp.arange(Ho) * STRIDE).astype(x.dtype)
            base_x = (jnp.arange(Wo) * STRIDE).astype(x.dtype)
            py = base_y[None, None, :, None] + kh[None, :, None, None] + off[:, :, 0]
            px = base_x[None, None, None, :] + kw[None, :, None, None] + off[:, :, 1]
            y0 = jnp.floor(py)
            x0 = jnp.floor(px)
            wy = py - y0
            wx = px - x0

            def corner(yc, xc):
                yi = yc.astype(jnp.int32)
                xi = xc.astype(jnp.int32)
                valid = (yi >= 0) & (yi < H) & (xi >= 0) & (xi < W)
                yi = jnp.clip(yi, 0, H - 1)
                xi = jnp.clip(xi, 0, W - 1)
                v = jax.vmap(lambda img, a, c: img[:, a, c])(x, yi, xi)
                return v * valid[:, None].astype(x.dtype)
            v00 = corner(y0, x0)
            v01 = corner(y0, x0 + 1)
            v10 = corner(y0 + 1, x0)
            v11 = corner(y0 + 1, x0 + 1)
            wy_ = wy[:, None]
            wx_ = wx[:, None]
            sampled = v00 * (1 - wy_) * (1 - wx_) + v01 * (1 - wy_) * wx_ + v10 * wy_ * (1 - wx_) + v11 * wy_ * wx_
            out = jnp.einsum('bckhw,ock->bohw', sampled, w.reshape(w.shape[0], C, KK))
            return out + b[None, :, None, None]
        h = conv2d(x, stem_w, stem_b, 4)
        h = leaky_relu(batchnorm(h, bn1_g, bn1_b, bn1_m, bn1_v))
        offset = conv2d(h, off_w, off_b, 4)
        h = deform_conv(h, offset, dcn_w, dcn_b)
        h = leaky_relu(batchnorm(h, bn2_g, bn2_b, bn2_m, bn2_v))
        B, C, Ho, Wo = h.shape
        return h.reshape(B, C, Ho * Wo).transpose(0, 2, 1)

    def _L0_attn_ref(residual, W_Q, W_K, W_V, W_O, b_Q, b_K, b_V, b_O):
        import jax, jax.numpy as jnp
        import numpy as np
        INIT_RANGE = 0.02
        d_head = W_Q.shape[-1]
        q = jnp.einsum('bsd,hde->bshe', residual, W_Q) + b_Q
        k = jnp.einsum('bsd,hde->bshe', residual, W_K) + b_K
        v = jnp.einsum('bsd,hde->bshe', residual, W_V) + b_V
        scores = jnp.einsum('bqhe,bkhe->bhqk', q, k) / jnp.sqrt(jnp.float32(d_head))
        S = residual.shape[1]
        causal = jnp.tril(jnp.ones((S, S), dtype=bool))
        scores = jnp.where(causal, scores, -jnp.inf)
        pattern = jax.nn.softmax(scores, axis=-1)
        z = jnp.einsum('bkhe,bhqk->bqhe', v, pattern)
        attn_out = jnp.einsum('bqhe,hed->bqd', z, W_O) + b_O
        return attn_out

    def _L0_ffn_ref(x, W1_w, W1_b, W2_w, W2_b, r_w, r_b, fc_w, fc_b, proj_w, proj_b, ln1_w, ln1_b, ln2_w, ln2_b):
        import jax, jax.numpy as jnp
        import numpy as np
        N_HEAD = 8 * 0 + 12
        TOP_K = 2
        GELU_C = 0.7978845608028654

        def _gelu(x):
            return 0.5 * x * (1.0 + jnp.tanh(GELU_C * (x + 0.044715 * x * x * x)))

        def _layernorm_global(x, w, b, eps=1e-12):
            m = jnp.mean(x)
            v = jnp.var(x, ddof=1)
            return (x - m) / jnp.sqrt(v + eps) * w + b

        def _attn(x, W1_w, W1_b, W2_w, W2_b):
            B, N, D = x.shape
            h = N_HEAD
            dh = D // h
            qkv = x @ W1_w + W1_b
            Q, K, V = jnp.split(qkv, 3, axis=-1)
            q = Q.reshape(B, N, h, dh).transpose(0, 2, 3, 1)
            k = K.reshape(B, N, h, dh).transpose(0, 2, 1, 3)
            v = V.reshape(B, N, h, dh).transpose(0, 2, 3, 1)
            w = jax.nn.softmax(q @ k / jnp.sqrt(jnp.asarray(N, x.dtype)), axis=-1)
            out = (w @ v).reshape(B, N, h * dh)
            return out @ W2_w + W2_b

        def _moe(x, r_w, r_b, fc_w, fc_b, proj_w, proj_b):
            B, N, D = x.shape
            scores = x @ r_w + r_b
            gate = jax.nn.softmax(jnp.mean(scores, axis=1), axis=-1)
            vals, idx = jax.lax.top_k(gate, TOP_K)
            hmid = _gelu(jnp.einsum('bnd,edf->benf', x, fc_w) + fc_b[None, :, None, :])
            outs = jnp.einsum('benf,efd->bend', hmid, proj_w) + proj_b[None, :, None, :]
            k_outs = jnp.take_along_axis(outs, idx[:, :, None, None], axis=1)
            return jnp.sum(vals[:, :, None, None] * k_outs, axis=1)
        a = _attn(x, W1_w, W1_b, W2_w, W2_b)
        x = _layernorm_global(a + x, ln1_w, ln1_b)
        m = _moe(x, r_w, r_b, fc_w, fc_b, proj_w, proj_b)
        x = _layernorm_global(m + x, ln2_w, ln2_b)
        return x

    def _L1_attn_ref(x, ln_w, ln_b, W_in, conv_w, conv_b, dt_bias, A_log, D, rms_w, W_out):
        import jax, jax.numpy as jnp
        import numpy as np
        D_MODEL = 192
        D_STATE = 64
        D_CONV = 4
        EXPAND = 2
        HEADDIM = 64
        D_INNER = EXPAND * D_MODEL
        NHEADS = D_INNER // HEADDIM
        CONV_DIM = D_INNER + 2 * D_STATE
        D_IN_PROJ = 2 * D_INNER + 2 * D_STATE + NHEADS
        BATCH, SEQLEN = (2, 256)
        EPS = 1e-05

        def _forward(x, ln_w, ln_b, W_in, conv_w, conv_b, dt_bias, A_log, D, rms_w, W_out):
            b, l, _ = x.shape
            mu = jnp.mean(x, -1, keepdims=True)
            var = jnp.mean((x - mu) ** 2, -1, keepdims=True)
            xn = (x - mu) * jax.lax.rsqrt(var + EPS) * ln_w + ln_b
            zxbcdt = xn @ W_in
            z = zxbcdt[..., :D_INNER]
            xBC = zxbcdt[..., D_INNER:D_INNER + CONV_DIM]
            dt_raw = zxbcdt[..., -NHEADS:]
            xp = jnp.pad(xBC, ((0, 0), (D_CONV - 1, 0), (0, 0)))
            xBC = sum((xp[:, k:k + l, :] * conv_w[:, k] for k in range(D_CONV))) + conv_b
            xBC = jax.nn.silu(xBC)
            xh = xBC[..., :D_INNER].reshape(b, l, NHEADS, HEADDIM)
            Bm = xBC[..., D_INNER:D_INNER + D_STATE]
            Cm = xBC[..., D_INNER + D_STATE:]
            dt = jax.nn.softplus(dt_raw + dt_bias)
            A = -jnp.exp(A_log)
            decay = jnp.exp(dt * A)

            def step(h, inp):
                dec_t, dt_t, x_t, B_t, C_t = inp
                h = h * dec_t[..., None, None] + (dt_t[..., None] * x_t)[..., None] * B_t[:, None, None, :]
                y = jnp.einsum('bhpn,bn->bhp', h, C_t)
                return (h, y)
            h0 = jnp.zeros((b, NHEADS, HEADDIM, D_STATE), x.dtype)
            seq = (decay.transpose(1, 0, 2), dt.transpose(1, 0, 2), xh.transpose(1, 0, 2, 3), Bm.transpose(1, 0, 2), Cm.transpose(1, 0, 2))
            _, ys = jax.lax.scan(step, h0, seq)
            y = ys.transpose(1, 0, 2, 3) + D[None, None, :, None] * xh
            y = y.reshape(b, l, D_INNER)
            g = y * jax.nn.silu(z)
            g = g * jax.lax.rsqrt(jnp.mean(g * g, -1, keepdims=True) + EPS) * rms_w
            return g @ W_out + x
        return _forward(x, ln_w, ln_b, W_in, conv_w, conv_b, dt_bias, A_log, D, rms_w, W_out)

    def _L1_ffn_ref(x, ln_w, w_router, wi, wo):
        import jax, jax.numpy as jnp
        import numpy as np
        B, S, D, F, E = (8, 512, 192, 768, 16)
        CAP = 64
        EPS = 1e-06

        def _switch_moe_block(x, ln_w, w_router, wi, wo):
            var = jnp.mean(jnp.square(x.astype(jnp.float32)), axis=-1, keepdims=True)
            normed = (x * jax.lax.rsqrt(var + EPS)).astype(x.dtype) * ln_w
            logits = jnp.einsum('bsd,de->bse', normed.astype(jnp.float32), w_router.astype(jnp.float32))
            probs = jax.nn.softmax(logits, axis=-1)
            expert_idx = jnp.argmax(probs, axis=-1)
            onehot = jax.nn.one_hot(expert_idx, E, dtype=jnp.float32)
            priority = jnp.cumsum(onehot, axis=1)
            keep = onehot * (priority <= CAP)
            pos = (priority - 1.0).astype(jnp.int32)
            dispatch = keep[..., None] * jax.nn.one_hot(pos, CAP, dtype=jnp.float32)
            expert_in = jnp.einsum('bsec,bsd->becd', dispatch, normed)
            h = jax.nn.relu(jnp.einsum('becd,edf->becf', expert_in, wi))
            expert_out = jnp.einsum('becf,efd->becd', h, wo)
            combined = jnp.einsum('bsec,becd->bsd', dispatch, expert_out)
            routed = jnp.sum(dispatch, axis=(2, 3)) > 0
            next_states = jnp.where(routed[..., None], combined.astype(x.dtype), normed)
            router_prob = jnp.max(probs, axis=-1, keepdims=True).astype(x.dtype)
            return x + router_prob * next_states
        return _switch_moe_block(x, ln_w, w_router, wi, wo)
    h = _L0_tok_ref(x, L0_tok_stem_w, L0_tok_stem_b, L0_tok_bn1_g, L0_tok_bn1_b, L0_tok_bn1_m, L0_tok_bn1_v, L0_tok_off_w, L0_tok_off_b, L0_tok_dcn_w, L0_tok_dcn_b, L0_tok_bn2_g, L0_tok_bn2_b, L0_tok_bn2_m, L0_tok_bn2_v)
    h = jnp.concatenate([jnp.broadcast_to(cls_tok, (h.shape[0], 1, h.shape[2])), h], axis=1)
    h = h + _L0_attn_ref(_layernorm(h, axis=-1), L0_attn_W_Q, L0_attn_W_K, L0_attn_W_V, L0_attn_W_O, L0_attn_b_Q, L0_attn_b_K, L0_attn_b_V, L0_attn_b_O)
    h = h + _L0_ffn_ref(_layernorm(h, axis=-1), L0_ffn_W1_w, L0_ffn_W1_b, L0_ffn_W2_w, L0_ffn_W2_b, L0_ffn_r_w, L0_ffn_r_b, L0_ffn_fc_w, L0_ffn_fc_b, L0_ffn_proj_w, L0_ffn_proj_b, L0_ffn_ln1_w, L0_ffn_ln1_b, L0_ffn_ln2_w, L0_ffn_ln2_b)
    h = h + _L1_attn_ref(_layernorm(h, axis=-1), L1_attn_ln_w, L1_attn_ln_b, L1_attn_W_in, L1_attn_conv_w, L1_attn_conv_b, L1_attn_dt_bias, L1_attn_A_log, L1_attn_D, L1_attn_rms_w, L1_attn_W_out)
    h = h + _L1_ffn_ref(_layernorm(h, axis=-1), L1_ffn_ln_w, L1_ffn_w_router, L1_ffn_wi, L1_ffn_wo)
    return h

_drawn_inputs = setup_inputs


def setup_inputs(seed=0):
    import zlib

    import numpy as np

    out = dict(_drawn_inputs(seed))
    spreads = {'L0_attn_b_Q': (0.0, 0.8),
     'L0_attn_b_K': (0.0, 0.8),
     'L0_attn_b_V': (0.0, 0.1),
     'L0_attn_b_O': (0.0, 0.1),
     'L0_ffn_W1_b': (0.0, 0.8),
     'L0_ffn_W2_b': (0.0, 0.1),
     'L0_ffn_r_b': (0.0, 0.459),
     'L0_ffn_fc_b': (0.0, 0.8),
     'L0_ffn_proj_b': (0.0, 0.582),
     'L0_ffn_ln1_w': (1.0, 0.2),
     'L0_ffn_ln1_b': (0.0, 0.1),
     'L0_ffn_ln2_w': (1.0, 0.2),
     'L0_ffn_ln2_b': (0.0, 0.1),
     'L1_attn_ln_w': (1.0, 0.2),
     'L1_attn_ln_b': (0.0, 0.428),
     'L1_attn_conv_b': (0.0, 0.1),
     'L1_attn_D': (1.0, 0.6),
     'L1_attn_rms_w': (1.0, 0.2),
     'L1_ffn_ln_w': (1.0, 0.6)}
    factors = {'L0_attn_W_Q': 8.0,
     'L0_attn_W_K': 8.0,
     'L0_ffn_W1_w': 4.125,
     'L0_ffn_W2_w': 4.272,
     'L0_ffn_r_w': 2.974,
     'L0_ffn_fc_w': 4.434,
     'L0_ffn_proj_w': 4.06,
     'L1_attn_dt_bias': 8.0,
     'L1_attn_A_log': 8.0,
     'L1_ffn_w_router': 2.987,
     'L1_ffn_wi': 3.584,
     'L1_ffn_wo': 2.917}
    for name, (base, spread) in spreads.items():
        noise = np.random.default_rng([zlib.crc32(name.encode()), seed]).standard_normal(out[name].shape)
        drawn = base * np.exp(spread * noise) if base else spread * noise
        out[name] = jnp.asarray(drawn.astype(out[name].dtype))
    for name, factor in factors.items():
        out[name] = (out[name] * factor).astype(out[name].dtype)
    return out
```

```python
from contextlib import ExitStack

import numpy as np

import concourse.bass as bass
from concourse import mybir

F32 = mybir.dt.float32
I32 = mybir.dt.int32
U32 = mybir.dt.uint32
ALU = mybir.AluOpType
ACT = mybir.ActivationFunctionType
AX = mybir.AxisListType

IMAGES = 16
SIDE = 28
PIX = SIDE * SIDE
TAPS = 16
OUT_SIDE = 7
POS = OUT_SIDE * OUT_SIDE
SEQ = POS + 1
C1 = 96
D = 192
HD = 96
TOK = IMAGES * SEQ
PAIR = 2 * SEQ
TILES = TOK // PAIR
HALF_TOK = TOK // 2
ROWS = 4
CHUNK = ROWS * SIDE
CHUNKS = PIX // CHUNK
HALF = PIX // 2
HEADS = 12
DH = 64
F = 768
FC = F // 128
SLOT = 128
BANK = 512
D_IN = 384
D_ST = 64
M_HEADS = 6
KCONV = 4
PADSEQ = SEQ + KCONV - 1
NEG = -1e30


def expert_tiles(experts, assignments):
    return (assignments + experts * (SLOT - 1)) // SLOT


class Stage:

    def __init__(self, nc, name):
        self.nc, self.name, self.stack = nc, name, ExitStack()

    def __enter__(self):
        self.stack.__enter__()
        return self

    def __exit__(self, *a):
        return self.stack.__exit__(*a)

    def sb(self, name, shape, dt=F32):
        return self.stack.enter_context(self.nc.sbuf_tensor(f"{self.name}_{name}", shape, dt))

    def ps(self, name, shape, dt=F32):
        return self.stack.enter_context(self.nc.psum_tensor(f"{self.name}_{name}", shape, dt))

    def sem(self, name):
        return self.nc.alloc_semaphore(f"{self.name}_{name}")


class Step:

    def __init__(self, sem):
        self.sem, self.n = sem, 0

    def add(self, ins):
        ins.then_inc(self.sem, 1)
        self.n += 1
        return self.n


def link(eng, step, ins):
    eng.wait_ge(step.sem, step.add(ins))


def bcast(ap, axis, n):
    a = ap.unsqueeze(axis)
    shape = list(a.shape)
    shape[axis] = n
    return a.broadcast_to(shape)


def stem_stage(nc, K, W, h, samp, off_dram):
    NCH = 2 * IMAGES
    with Stage(nc, "stem") as s:
        im2col = samp[0:48, :, :].rearrange("p a b -> p (a b)")
        tmp = s.sb("tmp", [C1, 3, HALF])
        offs = s.sb("offs", [32, IMAGES, POS])
        ps = s.ps("ps", [C1, 4, BANK])
        pso = s.ps("pso", [32, 2, BANK])
        x_in = [s.sem(f"x_in{i}") for i in range(4)]
        vec = Step(s.sem("vec"))
        var_ready, rstd_ready, bn_ready = s.sem("var_ready"), s.sem("rstd_ready"), s.sem("bn_ready")
        conv_ready, scaled, leaky = s.sem("conv_ready"), s.sem("scaled"), s.sem("leaky")
        off_ready, off_based, off_out = s.sem("off_ready"), s.sem("off_based"), s.sem("off_out")
        cv, bnv = W["chan"], W["bnv"]
        QC = IMAGES * PIX // 4
        with nc.Block() as block:
            @block.sync
            def _(sp):
                for i in range(4):
                    sp.dma_start(im2col[:, i * QC:(i + 1) * QC], K["x"][:, i * QC:(i + 1) * QC]).then_inc(x_in[i], 16)
                sp.wait_ge(off_based, 2)
                sp.dma_start(off_dram.rearrange("b c p -> c b p"), offs[:]).then_inc(off_out, 16)
                sp.wait_ge(off_out, 16)

            @block.gpsimd
            def _(pool):
                pool.wait_ge(var_ready, 1)
                nc.gpsimd.tensor_tensor(bnv[:, 0, :], bnv[:, 0, :], W["mhalf"][0:C1, 0:3], ALU.pow).then_inc(rstd_ready, 1)

            @block.tensor
            def _(pe):
                pe.wait_ge(W["sem"]["stem_w"], 16)
                for n in range(NCH):
                    if n % 8 == 0:
                        pe.wait_ge(x_in[n // 8], 16)
                    if n >= 4:
                        pe.wait_ge(scaled, n - 3)
                    nc.tensor.matmul(ps[:, n % 4, 0:HALF], W["stem_w"][:], im2col[:, n * HALF:(n + 1) * HALF],
                                     start=True, stop=True).then_inc(conv_ready, 1)
                pe.wait_ge(W["sem"]["off_w"], 16)
                for half in range(2):
                    pe.wait_ge(leaky, (half + 1) * NCH // 2)
                    grid = h[:, half * 8:(half + 1) * 8, :].rearrange(
                        "p b (i r j s) -> p b i r j s", i=OUT_SIDE, r=4, j=OUT_SIDE)
                    for tap in range(TAPS):
                        mm = nc.tensor.matmul(pso[:, half, 0:8 * POS].rearrange("p (b i j) -> p b i j", b=8, i=OUT_SIDE),
                                              W["off_w"][:, tap, :], grid[:, :, :, tap // 4, :, tap % 4],
                                              start=tap == 0, stop=tap == TAPS - 1)
                    mm.then_inc(off_ready, 1)

            @block.scalar
            def _(act):
                act.wait_ge(bn_ready, 1)
                for n in range(NCH):
                    act.wait_ge(conv_ready, n + 1)
                    if n >= 3:
                        act.wait_ge(leaky, n - 2)
                    nc.scalar.activation(tmp[:, n % 3, :], ps[:, n % 4, 0:HALF], ACT.Identity,
                                         bias=bnv[:, 2, 0:1], scale=bnv[:, 1, 0:1]).then_inc(scaled, 1)

            @block.vector
            def _(dve):
                for name in ("chan", "tabs"):
                    dve.wait_ge(W["sem"][name], 16)
                nc.vector.memset(W["mhalf"][:], -0.5).then_inc(vec.sem, 1)
                vec.n += 1
                dve.wait_ge(vec.sem, vec.n)
                nc.vector.tensor_scalar(bnv[:, 0, :], cv[:, 3, :], 1e-5, None, ALU.add).then_inc(var_ready, 1)
                dve.wait_ge(rstd_ready, 1)
                link(dve, vec, nc.vector.tensor_tensor(bnv[:, 1, :], bnv[:, 0, :], cv[:, 0, :], ALU.mult))
                link(dve, vec, nc.vector.tensor_tensor(bnv[:, 2, :], cv[:, 4, :], cv[:, 2, :], ALU.subtract))
                link(dve, vec, nc.vector.tensor_tensor(bnv[:, 2, :], bnv[:, 2, :], bnv[:, 1, :], ALU.mult))
                nc.vector.tensor_tensor(bnv[:, 2, :], bnv[:, 2, :], cv[:, 1, :], ALU.add).then_inc(bn_ready, 1)
                for n in range(NCH):
                    dve.wait_ge(scaled, n + 1)
                    t = tmp[:, n % 3, :]
                    nc.vector.scalar_tensor_tensor(h[:, n // 2, (n % 2) * HALF:(n % 2 + 1) * HALF], t, 0.01, t,
                                                   ALU.mult, ALU.max).then_inc(leaky, 1)
                for half in range(2):
                    dve.wait_ge(off_ready, half + 1)
                    nc.vector.scalar_tensor_tensor(
                        offs[:, half * 8:(half + 1) * 8, :],
                        pso[:, half, 0:8 * POS].rearrange("p (b q) -> p b q", b=8), W["tabs"][0:32, 8:9],
                        bcast(W["tabs"][0:32, 16:16 + POS], 1, 8), ALU.add, ALU.add).then_inc(off_based, 1)


def sampling_stage(nc, K, W, h, samp, off_dram):
    RING = 4
    with Stage(nc, "smp") as s:
        pxy = s.sb("pxy", [CHUNK, 2, 2, PIX])
        xw = s.sb("xw", [CHUNK, 2, PIX])
        dist = s.sb("dist", [CHUNK, 2, PIX])
        rest = s.sb("rest", [CHUNK, PIX])
        S = s.sb("S", [CHUNK, RING, PIX])
        hT = s.sb("hT", [CHUNK, 2, CHUNKS, C1])
        psT = s.ps("psT", [CHUNK, 2, BANK])
        acc = s.ps("acc", [C1, 2, 2, BANK])
        loaded = [s.sem(f"loaded{i}") for i in range(2)]
        turned, hT_ready = s.sem("turned"), s.sem("hT_ready")
        dist_ready, S_ready, S_used = s.sem("dist_ready"), s.sem("S_ready"), s.sem("S_used")
        rest_ready, dist_used = s.sem("rest_ready"), s.sem("dist_used")
        sampled, kept = s.sem("sampled"), s.sem("kept")
        xlink = Step(s.sem("xlink"))
        tabs = W["tabs"]
        PER = CHUNKS + 1
        with nc.Block() as block:
            @block.sync
            def _(sp):
                for b in range(IMAGES):
                    if b >= 2:
                        sp.wait_ge(dist_ready, (b - 1) * PER)
                    sp.dma_start(pxy[:, b % 2, :, :].rearrange("p a q -> p (a q)"),
                                 off_dram[b].rearrange("c p -> (c p)").partition_broadcast(CHUNK)).then_inc(loaded[b % 2], 16)

            @block.tensor
            def _(pe):
                def turn(b):
                    if b >= 1:
                        pe.wait_ge(hT_ready, b * 2)
                    for c in range(CHUNKS):
                        mm = nc.tensor.transpose(psT[:, c // 4, (c % 4) * C1:(c % 4 + 1) * C1],
                                                 h[:, b, c * CHUNK:(c + 1) * CHUNK], W["ident"][0:C1, 0:C1])
                    mm.then_inc(turned, 1)

                pe.wait_ge(W["sem"]["ident"], 16)
                turn(0)
                for b in range(IMAGES):
                    if b + 1 < IMAGES:
                        turn(b + 1)
                    pe.wait_ge(hT_ready, 2 * (b + 1))
                    if b >= 2:
                        pe.wait_ge(kept, 2 * (b - 1))
                    for c in range(CHUNKS):
                        n = b * CHUNKS + c
                        pe.wait_ge(S_ready, n + 1)
                        for half in range(2):
                            mm = nc.tensor.matmul(acc[:, b % 2, half, 0:HALF], hT[:, b % 2, c, :],
                                                  S[:, n % RING, half * HALF:(half + 1) * HALF],
                                                  start=c == 0, stop=c == CHUNKS - 1)
                        mm.then_inc(S_used, 1)

            @block.scalar
            def _(act):
                def keep(b):
                    act.wait_ge(S_used, (b + 1) * CHUNKS)
                    for half in range(2):
                        nc.scalar.copy(samp[:, half * 8:(half + 1) * 8, b * POS:(b + 1) * POS],
                                       acc[:, b % 2, half, 0:HALF].rearrange("p (k q) -> p k q", k=8)).then_inc(kept, 1)

                def turned_back(b):
                    act.wait_ge(turned, b + 1)
                    if b >= 2:
                        act.wait_ge(S_used, (b - 1) * CHUNKS)
                    nc.scalar.copy(hT[:, b % 2, 0:4, :], psT[:, 0, 0:4 * C1].rearrange("p (c n) -> p c n", c=4)).then_inc(hT_ready, 1)
                    nc.scalar.copy(hT[:, b % 2, 4:7, :], psT[:, 1, 0:3 * C1].rearrange("p (c n) -> p c n", c=3)).then_inc(hT_ready, 1)

                turned_back(0)
                for b in range(IMAGES):
                    act.wait_ge(loaded[b % 2], 16 * (b // 2 + 1))
                    for j in range(PER):
                        n = b * PER + j
                        if n >= 2:
                            act.wait_ge(dist_used, n - 1)
                        axis, col = (1, 7) if j == 0 else (0, j - 1)
                        nc.scalar.activation(dist[:, n % 2, :], pxy[:, b % 2, axis, :], ACT.Abs,
                                             bias=tabs[0:CHUNK, col:col + 1], scale=1.0).then_inc(dist_ready, 1)
                        if j == 3 and b + 1 < IMAGES:
                            turned_back(b + 1)
                        if j == 4 and b >= 1:
                            keep(b - 1)
                keep(IMAGES - 1)

            @block.vector
            def _(dve):
                for b in range(IMAGES):
                    for j in range(PER):
                        n = b * PER + j
                        dve.wait_ge(dist_ready, n + 1)
                        d = dist[:, n % 2, :]
                        dst = xw[:, b % 2, :] if j == 0 else rest[:, :]
                        nc.vector.tensor_scalar(dst, d, -1.0, 1.0, ALU.mult, ALU.add).then_inc(dist_used, 1)
                        dve.wait_ge(dist_used, n + 1)
                        if j == 0:
                            link(dve, xlink, nc.vector.tensor_scalar(dst, dst, 0.0, None, ALU.max))
                        else:
                            m = b * CHUNKS + j - 1
                            if m >= RING:
                                dve.wait_ge(S_used, m - RING + 1)
                            nc.vector.scalar_tensor_tensor(S[:, m % RING, :], rest[:, :], 0.0, xw[:, b % 2, :],
                                                           ALU.max, ALU.mult).then_inc(S_ready, 1)
                            dve.wait_ge(S_ready, m + 1)


def patch_stage(nc, K, W, samp, H):
    with Stage(nc, "dcn") as s:
        tmp = s.sb("tmp", [C1, 4, HALF])
        hc = s.sb("hc", [HD, 2, IMAGES, SEQ])
        ps = s.ps("ps", [C1, 4, BANK])
        psT = s.ps("psT", [PAIR, 4, BANK])
        mm_ready, scaled, leaky, cls = s.sem("mm_ready"), s.sem("scaled"), s.sem("leaky"), s.sem("cls")
        turned, kept = s.sem("turned"), s.sem("kept")
        with nc.Block() as block:
            @block.tensor
            def _(pe):
                pe.wait_ge(W["sem"]["dcn_w"], 16)
                for n in range(4):
                    half, m = n // 2, n % 2
                    for tap in range(TAPS):
                        mm = nc.tensor.matmul(ps[:, n, 0:HALF], W["dcn_w"][:, tap, m * HD:(m + 1) * HD],
                                              samp[:, tap, half * HALF:(half + 1) * HALF],
                                              start=tap == 0, stop=tap == TAPS - 1)
                    mm.then_inc(mm_ready, 1)
                pe.wait_ge(cls, 1)
                for t in range(TILES):
                    pe.wait_ge(leaky, 2 if t < 4 else 4)
                    for m in range(2):
                        mm = nc.tensor.transpose(psT[:, t // 2, (t % 2) * D + m * HD:(t % 2) * D + (m + 1) * HD],
                                                 hc[:, m, 2 * t:2 * t + 2, :].rearrange("p b q -> p (b q)"), W["ident"][0:HD, 0:HD])
                    mm.then_inc(turned, 1)

            @block.scalar
            def _(act):
                for n in range(4):
                    act.wait_ge(mm_ready, n + 1)
                    m = n % 2
                    nc.scalar.activation(tmp[:, n, :], ps[:, n, 0:HALF], ACT.Identity,
                                         bias=W["bnv"][:, 2, 1 + m:2 + m], scale=W["bnv"][:, 1, 1 + m:2 + m]).then_inc(scaled, 1)
                for j in range(4):
                    act.wait_ge(turned, 2 * j + 2)
                    nc.scalar.copy(H[:, 2 * j:2 * j + 2, :], psT[:, j, 0:2 * D].rearrange("p (t d) -> p t d", t=2)).then_inc(kept, 1)

            @block.vector
            def _(dve):
                dve.wait_ge(W["sem"]["chan"], 16)
                nc.vector.tensor_copy(hc[:, :, :, 0], bcast(W["chan"][:, 5, 0:2], 2, IMAGES)).then_inc(cls, 1)
                for n in range(4):
                    half, m = n // 2, n % 2
                    dve.wait_ge(scaled, n + 1)
                    t = tmp[:, n, :].rearrange("p (b q) -> p b q", b=8)
                    nc.vector.scalar_tensor_tensor(hc[:, m, half * 8:(half + 1) * 8, 1:SEQ], t, 0.01, t,
                                                   ALU.mult, ALU.max).then_inc(leaky, 1)


def channels_stage(nc, W, name, src, dst):
    width, n = dst.shape[0], dst.shape[1]
    with Stage(nc, name) as s:
        ps = s.ps("ps", [width, 8, BANK])
        turned, kept_a, kept_v = s.sem("turned"), s.sem("kept_a"), s.sem("kept_v")
        groups = [(m, g) for g in range(2) for m in range(n)]
        with nc.Block() as block:
            @block.tensor
            def _(pe):
                for j, (m, g) in enumerate(groups):
                    for t in range(4):
                        mm = nc.tensor.transpose(ps[:, j, t * PAIR:(t + 1) * PAIR],
                                                 src[:, 4 * g + t, m * width:(m + 1) * width], W["ident"][0:PAIR, 0:PAIR])
                    mm.then_inc(turned, 1)

            @block.scalar
            def _(act):
                for j, (m, g) in enumerate(groups):
                    if j % 2 == 0:
                        act.wait_ge(turned, j + 1)
                        nc.scalar.copy(dst[:, m, g * HALF_TOK:(g + 1) * HALF_TOK], ps[:, j, 0:HALF_TOK]).then_inc(kept_a, 1)

            @block.vector
            def _(dve):
                for j, (m, g) in enumerate(groups):
                    if j % 2:
                        dve.wait_ge(turned, j + 1)
                        nc.vector.tensor_copy(dst[:, m, g * HALF_TOK:(g + 1) * HALF_TOK], ps[:, j, 0:HALF_TOK]).then_inc(kept_v, 1)


def norm_stage(nc, W, name, src, dst, eps, rms=False, gain=None, shift=None):
    with Stage(nc, name) as s:
        stat = s.sb("stat", [PAIR, TILES, 6])
        mv = s.sb("mv", [PAIR, TILES, 2])
        sq = s.sb("sq", [PAIR, TILES])
        rstd = s.sb("rstd", [PAIR, TILES])
        vec = Step(s.sem("vec"))
        var_ready, rstd_ready = s.sem("var_ready"), s.sem("rstd_ready")
        with nc.Block() as block:
            @block.vector
            def _(dve):
                for t in range(TILES):
                    vec.add(nc.vector.bn_stats(stat[:, t, :], src[:, t, :]))
                dve.wait_ge(vec.sem, vec.n)
                for t in range(TILES):
                    vec.add(nc.vector.bn_aggr(mv[:, t, :], stat[:, t, :]))
                dve.wait_ge(vec.sem, vec.n)
                if rms:
                    link(dve, vec, nc.vector.tensor_tensor(sq[:], mv[:, :, 0], mv[:, :, 0], ALU.mult))
                    link(dve, vec, nc.vector.tensor_tensor(sq[:], sq[:], mv[:, :, 1], ALU.add))
                    nc.vector.tensor_scalar(sq[:], sq[:], eps, None, ALU.add).then_inc(var_ready, 1)
                else:
                    nc.vector.tensor_scalar(sq[:], mv[:, :, 1], eps, None, ALU.add).then_inc(var_ready, 1)
                dve.wait_ge(rstd_ready, 1)
                for t in range(TILES):
                    if rms:
                        vec.add(nc.vector.tensor_scalar(dst[:, t, :], src[:, t, :], rstd[:, t:t + 1], None, ALU.mult))
                    else:
                        vec.add(nc.vector.tensor_scalar(dst[:, t, :], src[:, t, :], mv[:, t, 0:1], rstd[:, t:t + 1],
                                                        ALU.subtract, ALU.mult))
                for v, op in ((gain, ALU.mult), (shift, ALU.add)):
                    if v is not None:
                        dve.wait_ge(vec.sem, vec.n)
                        vec.add(nc.vector.tensor_tensor(dst[:], dst[:], bcast(v, 1, TILES), op))

            @block.gpsimd
            def _(pool):
                pool.wait_ge(var_ready, 1)
                nc.gpsimd.tensor_tensor(rstd[:], sq[:], W["mhalf"][0:PAIR, 0:TILES], ALU.pow).then_inc(rstd_ready, 1)


def global_norm_stage(nc, W, name, src, dst, gain, shift, add_to=None):
    N = TOK * D
    with Stage(nc, name) as s:
        stat = s.sb("stat", [PAIR, TILES, 6])
        mv = s.sb("mv", [PAIR, 2])
        m = s.sb("m", [PAIR, 4])
        ps = s.ps("ps", [PAIR, 2, BANK])
        vec = Step(s.sem("vec"))
        mean_in, mean_out, var_in, var_out = (s.sem(x) for x in ("mean_in", "mean_out", "var_in", "var_out"))
        sq_ready, rstd_ready = s.sem("sq_ready"), s.sem("rstd_ready")
        with nc.Block() as block:
            @block.tensor
            def _(pe):
                pe.wait_ge(mean_in, 1)
                nc.tensor.matmul(ps[:, 0, 0:1], W["ones"][0:PAIR, 0:PAIR], mv[:, 0:1], start=True, stop=True).then_inc(mean_out, 1)
                pe.wait_ge(var_in, 1)
                nc.tensor.matmul(ps[:, 1, 0:1], W["ones"][0:PAIR, 0:PAIR], m[:, 2:3], start=True, stop=True).then_inc(var_out, 1)

            @block.gpsimd
            def _(pool):
                pool.wait_ge(sq_ready, 1)
                nc.gpsimd.tensor_tensor(m[:, 3:4], m[:, 1:2], W["mhalf"][0:PAIR, 0:1], ALU.pow).then_inc(rstd_ready, 1)

            @block.vector
            def _(dve):
                for t in range(TILES):
                    vec.add(nc.vector.bn_stats(stat[:, t, :], src[:, t, :]))
                dve.wait_ge(vec.sem, vec.n)
                nc.vector.bn_aggr(mv[:], stat[:].rearrange("p t c -> p (t c)")).then_inc(mean_in, 1)
                dve.wait_ge(mean_out, 1)
                link(dve, vec, nc.vector.tensor_scalar(m[:, 0:1], ps[:, 0, 0:1], 1.0 / PAIR, None, ALU.mult))
                link(dve, vec, nc.vector.tensor_tensor(m[:, 1:2], mv[:, 0:1], m[:, 0:1], ALU.subtract))
                link(dve, vec, nc.vector.tensor_tensor(m[:, 1:2], m[:, 1:2], m[:, 1:2], ALU.mult))
                nc.vector.tensor_tensor(m[:, 2:3], mv[:, 1:2], m[:, 1:2], ALU.add).then_inc(var_in, 1)
                dve.wait_ge(var_out, 1)
                nc.vector.tensor_scalar(m[:, 1:2], ps[:, 1, 0:1], N / (N - 1.0) / PAIR, 1e-12, ALU.mult, ALU.add).then_inc(sq_ready, 1)
                dve.wait_ge(rstd_ready, 1)
                for t in range(TILES):
                    vec.add(nc.vector.tensor_scalar(dst[:, t, :], src[:, t, :], m[:, 0:1], m[:, 3:4], ALU.subtract, ALU.mult))
                dve.wait_ge(vec.sem, vec.n)
                link(dve, vec, nc.vector.tensor_tensor(dst[:], dst[:], bcast(gain, 1, TILES), ALU.mult))
                link(dve, vec, nc.vector.tensor_tensor(dst[:], dst[:], bcast(shift, 1, TILES), ALU.add))
                if add_to is not None:
                    link(dve, vec, nc.vector.tensor_tensor(add_to[:], add_to[:], dst[:], ALU.add))


def product_stage(nc, W, name, products, weights, add=False):
    with Stage(nc, name) as s:
        ps = s.ps("ps", [128, 8, BANK])
        ready, kept_a, kept_v = s.sem("ready"), s.sem("kept_a"), s.sem("kept_v")

        def bank(j, dst, row):
            free = dst.shape[1:]
            v = ps[row:row + dst.shape[0], j % 8, 0:int(np.prod(free))]
            return v if len(free) == 1 else v.rearrange("p (a b) -> p a b", a=free[0])

        def by_act(j):
            return j % 2 == 0 and not add

        with nc.Block() as block:
            @block.tensor
            def _(pe):
                for w in weights:
                    pe.wait_ge(W["sem"][w], 16)
                for j, (dst, bias, terms, row) in enumerate(products):
                    if j >= 8 and by_act(j):
                        pe.wait_ge(kept_a, (j - 8) // 2 + 1)
                    elif j >= 8:
                        pe.wait_ge(kept_v, j - 7 if add else (j - 8) // 2 + 1)
                    for i, (lhsT, rhs) in enumerate(terms):
                        n = int(np.prod(rhs.shape[1:]))
                        mm = nc.tensor.matmul(ps[row:row + dst.shape[0], j % 8, 0:n], lhsT, rhs,
                                              start=i == 0, stop=i == len(terms) - 1)
                    mm.then_inc(ready, 1)

            @block.scalar
            def _(act):
                for j, (dst, bias, terms, row) in enumerate(products):
                    if by_act(j):
                        act.wait_ge(ready, j + 1)
                        if bias is None:
                            nc.scalar.copy(dst, bank(j, dst, row)).then_inc(kept_a, 1)
                        else:
                            nc.scalar.activation(dst, bank(j, dst, row), ACT.Identity, bias=bias, scale=1.0).then_inc(kept_a, 1)

            @block.vector
            def _(dve):
                for j, (dst, bias, terms, row) in enumerate(products):
                    if not by_act(j):
                        dve.wait_ge(ready, j + 1)
                        if add:
                            nc.vector.tensor_tensor(dst, bank(j, dst, row), dst, ALU.add).then_inc(kept_v, 1)
                        elif bias is None:
                            nc.vector.tensor_copy(dst, bank(j, dst, row)).then_inc(kept_v, 1)
                        else:
                            nc.vector.tensor_scalar(dst, bank(j, dst, row), bias, None, ALU.add).then_inc(kept_v, 1)


def attention_core(nc, W, QT, KT, V, zT):
    G = 4

    def alike(g):
        h0 = 6 * (g // 2) + g % 2
        return slice(h0, h0 + 5, 2)

    with Stage(nc, "att") as s:
        sc = s.sb("sc", [PAIR, 2, HEADS, PAIR])
        pt = s.sb("pt", [PAIR, 2, HEADS, PAIR])
        mx = s.sb("mx", [PAIR, 2, HEADS])
        sm = s.sb("sm", [PAIR, 2, HEADS])
        psS = s.ps("psS", [PAIR, G, BANK])
        psP = s.ps("psP", [PAIR, 2, BANK])
        psZ = s.ps("psZ", [128, 2, BANK])
        scores, masked, vec, shifted = s.sem("scores"), s.sem("masked"), Step(s.sem("vec")), s.sem("shifted")
        exps, rec, probs, turned, pt_ready = (s.sem(x) for x in ("exps", "rec", "probs", "turned", "pt_ready"))
        z_ready, z_kept = s.sem("z_ready"), s.sem("z_kept")
        with nc.Block() as block:
            @block.tensor
            def _(pe):
                def score(t):
                    for g in range(G):
                        if t >= 1:
                            pe.wait_ge(masked, G * (t - 1) + g + 1)
                        for i in range(3):
                            hd = alike(g).start + 2 * i
                            r = 64 * (hd % 2)
                            mm = nc.tensor.matmul(psS[:, g, i * PAIR:(i + 1) * PAIR], QT[r:r + 64, hd // 2, tokens(t)],
                                                  KT[r:r + 64, hd // 2, tokens(t)], start=True, stop=True)
                        mm.then_inc(scores, 1)

                def turn(t):
                    pe.wait_ge(probs, t + 1)
                    for g in range(G):
                        if G * t + g >= 2:
                            pe.wait_ge(pt_ready, G * t + g - 1)
                        for i in range(3):
                            mm = nc.tensor.transpose(psP[:, g % 2, i * PAIR:(i + 1) * PAIR], sc[:, t % 2, 3 * g + i, :],
                                                     W["ident"][0:PAIR, 0:PAIR])
                        mm.then_inc(turned, 1)

                def weigh(t):
                    if t >= 1:
                        pe.wait_ge(z_kept, 2 * t)
                    for hd in range(HEADS):
                        if hd % 3 == 0:
                            pe.wait_ge(pt_ready, G * t + hd // 3 + 1)
                        r, pr = 64 * (hd % 2), hd // 2
                        mm = nc.tensor.matmul(psZ[r:r + 64, pr // 3, (pr % 3) * PAIR:(pr % 3 + 1) * PAIR],
                                              V[:, t, hd * DH:(hd + 1) * DH], pt[:, t % 2, hd, :], start=True, stop=True)
                    mm.then_inc(z_ready, 1)

                score(0)
                for t in range(TILES):
                    if t + 1 < TILES:
                        score(t + 1)
                    turn(t)
                    weigh(t)

            @block.vector
            def _(dve):
                def open_(t):
                    for g in range(G):
                        dve.wait_ge(scores, G * t + g + 1)
                        if t >= 2:
                            dve.wait_ge(turned, G * (t - 1))
                        nc.vector.tensor_tensor(sc[:, t % 2, alike(g), :],
                                                psS[:, g, 0:3 * PAIR].rearrange("p (h k) -> p h k", h=3),
                                                bcast(W["amask"][:], 1, 3), ALU.add).then_inc(masked, 1)
                    dve.wait_ge(masked, G * (t + 1))
                    link(dve, vec, nc.vector.tensor_reduce(mx[:, t % 2, :], sc[:, t % 2, :, :], AX.X, ALU.max))
                    nc.vector.tensor_tensor(sc[:, t % 2, :, :], sc[:, t % 2, :, :], bcast(mx[:, t % 2, :], 2, PAIR),
                                            ALU.subtract).then_inc(shifted, 1)

                def close(t):
                    dve.wait_ge(exps, t + 1)
                    if t >= 2:
                        dve.wait_ge(probs, t - 1)
                    link(dve, vec, nc.vector.tensor_reduce(sm[:, t % 2, :], sc[:, t % 2, :, :], AX.X, ALU.add))
                    nc.vector.reciprocal(sm[:, t % 2, :], sm[:, t % 2, :]).then_inc(rec, 1)

                def keep(t):
                    dve.wait_ge(z_ready, t + 1)
                    for j in range(2):
                        nc.vector.tensor_tensor(zT[:, 3 * j:3 * j + 3, t * PAIR:(t + 1) * PAIR],
                                                psZ[:, j, 0:3 * PAIR].rearrange("p (h q) -> p h q", h=3),
                                                bcast(W["qkvb"][:, 2, 3 * j:3 * j + 3], 2, PAIR), ALU.add).then_inc(z_kept, 1)

                dve.wait_ge(W["sem"]["amask"], 16)
                open_(0)
                for t in range(TILES):
                    if t + 1 < TILES:
                        open_(t + 1)
                    close(t)
                    if t >= 1:
                        keep(t - 1)
                keep(TILES - 1)

            @block.gpsimd
            def _(pool):
                for t in range(TILES):
                    pool.wait_ge(rec, t + 1)
                    nc.gpsimd.tensor_tensor(sc[:, t % 2, :, :], sc[:, t % 2, :, :], bcast(sm[:, t % 2, :], 2, PAIR),
                                            ALU.mult).then_inc(probs, 1)

            @block.scalar
            def _(act):
                def exp(t):
                    act.wait_ge(shifted, t + 1)
                    nc.scalar.activation(sc[:, t % 2, :, :], sc[:, t % 2, :, :], ACT.Exp, scale=DH ** -0.5).then_inc(exps, 1)

                exp(0)
                for t in range(TILES):
                    if t + 1 < TILES:
                        exp(t + 1)
                    for g in range(G):
                        act.wait_ge(turned, G * t + g + 1)
                        if t >= 2:
                            act.wait_ge(z_ready, t - 1)
                        nc.scalar.copy(pt[:, t % 2, 3 * g:3 * g + 3, :],
                                       psP[:, g % 2, 0:3 * PAIR].rearrange("p (h k) -> p h k", h=3)).then_inc(pt_ready, 1)


def tokens(t):
    return slice(t * PAIR, (t + 1) * PAIR)


def attention_layer(nc, W, H):
    with Stage(nc, "at") as s:
        xn = s.sb("xn", [PAIR, TILES, D])
        xT = s.sb("xT", [HD, 2, TOK])
        QT = s.sb("QT", [128, 6, TOK])
        KT = s.sb("KT", [128, 6, TOK])
        V = s.sb("V", [PAIR, TILES, HEADS * DH])
        zT = s.sb("zT", [128, 6, TOK])
        norm_stage(nc, W, "at_n", H, xn, 1e-5)
        channels_stage(nc, W, "at_c", xn, xT)
        prods = []
        for i, (name, dst) in enumerate((("wq", QT), ("wk", KT))):
            for m in range(6):
                for g in range(2):
                    c = slice(g * HALF_TOK, (g + 1) * HALF_TOK)
                    prods.append((dst[:, m, c], W["qkvb"][:, i, m:m + 1],
                                  [(W[name][:, k, m * 128:(m + 1) * 128], xT[:, k, c]) for k in range(2)], 0))
        for t in range(TILES):
            for g in range(2):
                c = slice(g * D_IN, (g + 1) * D_IN)
                prods.append((V[:, t, c], None, [(xT[:, k, tokens(t)], W["wv"][:, k, c]) for k in range(2)], 0))
        product_stage(nc, W, "at_p", prods, ["wq", "wk", "wv", "qkvb"])
        attention_core(nc, W, QT, KT, V, zT)
        prods = [(H[:, t, :], None, [(zT[:, p, tokens(t)], W["wo"][:, p, :]) for p in range(6)]
                  + [(W["ones"][0:1, 0:PAIR], W["rowb"][0:1, 0, :])], 0) for t in range(TILES)]
        product_stage(nc, W, "at_o", prods, ["wo", "rowb"], add=True)


def channel_attention(nc, W, xT, X, a_dram, Y, YT):
    with Stage(nc, "ca") as s:
        QK = s.sb("QK", [128, TILES, 2 * D])
        VT = s.sb("VT", [HD, 2, TOK])
        sc = s.sb("sc", [HD, 2 * IMAGES, HD])
        wT = s.sb("wT", [HD, 2 * IMAGES, HD])
        mx = s.sb("mx", [HD, 2 * IMAGES])
        A = s.sb("A", [HD, 2, IMAGES, SEQ])
        prods = []
        for t in range(TILES):
            for o in range(2):
                c = slice((2 * t + o) * SEQ, (2 * t + o + 1) * SEQ)
                prods.append((QK[64 * o:64 * o + SEQ, t, :], None,
                              [(xT[:, 0, c], W["w1"][:, 0, 0:2 * D]), (xT[0:HD, 1, c], W["w1"][0:HD, 1, 0:2 * D])], 64 * o))
        for m in range(2):
            for g in range(2):
                c = slice(g * HALF_TOK, (g + 1) * HALF_TOK)
                v = slice(2 * D + m * HD, 2 * D + (m + 1) * HD)
                prods.append((VT[:, m, c], None,
                              [(W["w1"][:, 0, v], xT[:, 0, c]), (W["w1"][0:HD, 1, v], xT[0:HD, 1, c])], 0))
        product_stage(nc, W, "ca_p", prods, ["w1"])
        with Stage(nc, "cb") as p:
            ps = p.ps("ps", [HD, 8, BANK])
            scores, masked, vec = s.sem("scores"), s.sem("masked"), Step(s.sem("vec"))
            shifted, exps, probs, turned, wT_ready, a_ready, a_kept, a_out, a_in = (
                s.sem(x) for x in ("shifted", "exps", "probs", "turned", "wT_ready", "a_ready", "a_kept", "a_out", "a_in"))

            def place(b, half):
                return 4 * (2 * (b // 4) + b % 2) + 2 * (b % 4 // 2) + half

            def four(j):
                return ps[:, j, 0:4 * HD].rearrange("p (h k) -> p h k", h=4)

            with nc.Block() as block:
                @block.tensor
                def _(pe):
                    for j in range(8):
                        for i in range(4):
                            b, c = 4 * (j // 2) + j % 2 + 2 * (i // 2), (i % 2) * HD
                            r = slice(64 * (b % 2), 64 * (b % 2) + SEQ)
                            mm = nc.tensor.matmul(ps[:, j, i * HD:(i + 1) * HD], QK[r, b // 2, c:c + HD],
                                                  QK[r, b // 2, D + c:D + c + HD], start=True, stop=True)
                        mm.then_inc(scores, 1)
                    pe.wait_ge(probs, 1)
                    for j in range(8):
                        for i in range(4):
                            mm = nc.tensor.transpose(ps[:, j, i * HD:(i + 1) * HD], sc[:, 4 * j + i, :], W["ident"][0:HD, 0:HD])
                        mm.then_inc(turned, 1)
                    pe.wait_ge(wT_ready, 8)
                    for j in range(4):
                        half, b0 = j // 2, 8 * (j % 2)
                        for b in range(b0, b0 + 8):
                            mm = nc.tensor.matmul(ps[:, j, (b - b0) * SEQ:(b - b0 + 1) * SEQ], wT[:, place(b, half), :],
                                                  VT[:, half, b * SEQ:(b + 1) * SEQ], start=True, stop=True)
                        mm.then_inc(a_ready, 1)

                @block.vector
                def _(dve):
                    dve.wait_ge(W["sem"]["cmask"], 16)
                    for j in range(8):
                        dve.wait_ge(scores, j + 1)
                        nc.vector.tensor_tensor(sc[:, 4 * j:4 * j + 4, :], four(j), bcast(W["cmask"][:], 1, 4), ALU.add).then_inc(masked, 1)
                    dve.wait_ge(masked, 8)
                    link(dve, vec, nc.vector.tensor_reduce(mx[:], sc[:], AX.X, ALU.max))
                    nc.vector.tensor_tensor(sc[:], sc[:], bcast(mx[:], 2, HD), ALU.subtract).then_inc(shifted, 1)
                    dve.wait_ge(exps, 1)
                    link(dve, vec, nc.vector.tensor_reduce(mx[:], sc[:], AX.X, ALU.add))
                    link(dve, vec, nc.vector.reciprocal(mx[:], mx[:]))
                    nc.vector.tensor_tensor(sc[:], sc[:], bcast(mx[:], 2, HD), ALU.mult).then_inc(probs, 1)
                    for j in range(4):
                        dve.wait_ge(a_ready, j + 1)
                        half, b0 = j // 2, 8 * (j % 2)
                        nc.vector.tensor_copy(A[:, half, b0:b0 + 8, :],
                                              ps[:, j, 0:8 * SEQ].rearrange("p (b q) -> p b q", b=8)).then_inc(a_kept, 1)

                @block.scalar
                def _(act):
                    act.wait_ge(shifted, 1)
                    nc.scalar.activation(sc[:], sc[:], ACT.Exp, scale=float(SEQ) ** -0.5).then_inc(exps, 1)
                    for j in range(8):
                        act.wait_ge(turned, j + 1)
                        nc.scalar.copy(wT[:, 4 * j:4 * j + 4, :], four(j)).then_inc(wT_ready, 1)

                @block.sync
                def _(sp):
                    sp.wait_ge(a_kept, 4)
                    for half in range(2):
                        sp.dma_start(a_dram.rearrange("b (h c) q -> h c b q", h=2)[half], A[:, half, :, :]).then_inc(a_out, 16)
                    sp.wait_ge(a_out, 32)
                    sp.dma_start(Y[:], a_dram.rearrange("b c q -> (b c q)").rearrange("(t p d) -> p t d", p=PAIR, d=D)).then_inc(a_in, 16)
                    sp.wait_ge(a_in, 16)
    channels_stage(nc, W, "cc", Y, YT)
    prods = [(X[:, t, :], None, [(YT[:, k, tokens(t)], W["w2"][:, k, :]) for k in range(2)]
              + [(W["ones"][0:1, 0:PAIR], W["rowb"][0:1, 1, :])], 0) for t in range(TILES)]
    product_stage(nc, W, "cd", prods, ["w2", "rowb"], add=True)


def routing_stage(nc, W, name, E, ranks, NT, xT, wr, wr_name, by_image, x, x_dram, gate, slot, tile_expert):
    TE = TILES * E
    MAXM = (TOK + SLOT - 1) // SLOT
    with Stage(nc, name) as s:
        lg = s.sb("lg", [PAIR, TILES, E])
        lr = s.sb("lr", [PAIR, TILES, E])
        ex = s.sb("ex", [PAIR, TILES, E])
        key = s.sb("key", [PAIR, TILES, E])
        oh = s.sb("oh", [PAIR, 2, TILES, E])
        both = s.sb("both", [PAIR, TILES, E])
        st = s.sb("st", [PAIR, 6, TILES])
        cnt = s.sb("cnt", [PAIR, E, MAXM])
        ne = s.sb("ne", [PAIR, 4, E])
        zero = s.sb("zero", [PAIR, E])
        rows = s.sb("rows", [PAIR, TILES, E])
        slotf = s.sb("slotf", [PAIR, TILES, 2])
        te = s.sb("te", [1, NT, E])
        tef = s.sb("tef", [1, NT])
        zrow = s.sb("zrow", [SLOT, D])
        psL = s.ps("psL", [PAIR, BANK])
        psM = s.ps("psM", [PAIR, BANK])
        psP = s.ps("psP", [PAIR, BANK])
        psN = s.ps("psN", [PAIR, BANK])
        logits, raw_kept, mean_ready, shifted, exps = (s.sem(x) for x in ("logits", "raw_kept", "mean_ready", "shifted", "exps"))
        chosen, counted, slots_ready, zeroed, cleared, scattered = (
            s.sem(x) for x in ("chosen", "counted", "slots_ready", "zeroed", "cleared", "scattered"))
        vec = Step(s.sem("vec"))
        xd = x_dram.rearrange("(n p) d -> n p d", p=SLOT)
        with nc.Block() as block:
            @block.tensor
            def _(pe):
                for n in (wr_name, "imean", "before"):
                    pe.wait_ge(W["sem"][n], 16)
                for t in range(TILES):
                    for k in range(2):
                        mm = nc.tensor.matmul(psL[:, t * E:(t + 1) * E], xT[0:HD, k, tokens(t)], wr[:, k, :],
                                              start=k == 0, stop=k == 1)
                mm.then_inc(logits, 1)
                if by_image:
                    pe.wait_ge(raw_kept, 1)
                    nc.tensor.matmul(psM[:, 0:TE], W["imean"][:], lr[:].rearrange("p t e -> p (t e)"),
                                     start=True, stop=True).then_inc(mean_ready, 1)
                pe.wait_ge(chosen, 1)
                pb = psP[:, 0:TE].rearrange("p (t e) -> p t e", t=TILES)
                nc.tensor.matmul(psP[:, 0:TE], W["before"][:], both[:].rearrange("p t e -> p (t e)"), start=True, stop=False)
                for t in range(TILES - 1):
                    nc.tensor.matmul(pb[:, t + 1:TILES, :], W["ones"][0:PAIR, 0:PAIR], bcast(both[:, t, :], 1, TILES - 1 - t),
                                     start=False, stop=t == TILES - 2)
                for t in range(TILES):
                    mm = nc.tensor.matmul(psN[:, 0:E], W["ones"][0:PAIR, 0:PAIR], both[:, t, :], start=t == 0, stop=t == TILES - 1)
                mm.then_inc(counted, 1)

            @block.scalar
            def _(act):
                act.wait_ge(shifted, 1)
                nc.scalar.activation(ex[:], lg[:], ACT.Exp, scale=1.0).then_inc(exps, 1)

            @block.sync
            def _(sp):
                sp.wait_ge(zeroed, 1)
                for n in range(NT):
                    sp.dma_start(xd[n], zrow[:]).then_inc(cleared, 16)

            @block.gpsimd
            def _(pool):
                nc.gpsimd.memset(zrow[:], 0.0).then_inc(zeroed, 1)
                pool.wait_ge(cleared, 16 * NT)
                pool.wait_ge(slots_ready, 1)
                for t in range(TILES):
                    for r in range(ranks):
                        nc.gpsimd.indirect_dma_start(
                            out=x_dram[:, :], out_offset=bass.IndirectOffsetOnAxis(ap=slot[:, t, r:r + 1], axis=0),
                            in_=x[:, t, :], in_offset=None).then_inc(scattered, 16)
                pool.wait_ge(scattered, 16 * TILES * ranks)

            @block.vector
            def _(dve):
                def do(ins):
                    link(dve, vec, ins)

                v3 = lambda p: p[:, 0:TE].rearrange("p (t e) -> p t e", t=TILES)
                dve.wait_ge(W["sem"]["iota"], 16)
                dve.wait_ge(logits, 1)
                if by_image:
                    nc.vector.tensor_copy(lr[:], v3(psL)).then_inc(raw_kept, 1)
                    dve.wait_ge(W["sem"]["colb"], 16)
                    dve.wait_ge(mean_ready, 1)
                    do(nc.vector.tensor_tensor(lr[:], v3(psM), bcast(W["colb"][:, 0:E], 1, TILES), ALU.add))
                else:
                    do(nc.vector.tensor_copy(lr[:], v3(psL)))
                do(nc.vector.tensor_reduce(st[:, 0, :], lr[:], AX.X, ALU.max))
                nc.vector.tensor_tensor(lg[:], lr[:], bcast(st[:, 0, :], 2, E), ALU.subtract).then_inc(shifted, 1)
                dve.wait_ge(exps, 1)
                do(nc.vector.tensor_reduce(st[:, 1, :], ex[:], AX.X, ALU.add))
                do(nc.vector.reciprocal(st[:, 2, :], st[:, 1, :]))
                iota = bcast(W["iota"][0:PAIR, 0:E], 1, TILES)
                do(nc.vector.memset(zero[:], 0.0))
                for r in range(ranks):
                    if r:
                        do(nc.vector.tensor_reduce(st[:, 0, :], lr[:], AX.X, ALU.max))
                    do(nc.vector.tensor_tensor(key[:], lr[:], bcast(st[:, 0, :], 2, E), ALU.is_lt))
                    do(nc.vector.scalar_tensor_tensor(key[:], key[:], 1000.0, iota, ALU.mult, ALU.add))
                    do(nc.vector.tensor_reduce(st[:, 3, :], key[:], AX.X, ALU.min))
                    do(nc.vector.tensor_tensor(oh[:, r, :, :], iota, bcast(st[:, 3, :], 2, E), ALU.is_equal))
                    do(nc.vector.tensor_tensor(key[:], oh[:, r, :, :], ex[:], ALU.mult))
                    do(nc.vector.tensor_reduce(st[:, 4, :], key[:], AX.X, ALU.add))
                    do(nc.vector.tensor_tensor(gate[:, :, r], st[:, 4, :], st[:, 2, :], ALU.mult))
                    if r + 1 < ranks:
                        do(nc.vector.scalar_tensor_tensor(lr[:], oh[:, r, :, :], NEG, lr[:], ALU.mult, ALU.add))
                if ranks == 2:
                    nc.vector.tensor_tensor(both[:], oh[:, 0, :, :], oh[:, 1, :, :], ALU.add).then_inc(chosen, 1)
                else:
                    nc.vector.tensor_copy(both[:], oh[:, 0, :, :]).then_inc(chosen, 1)
                dve.wait_ge(counted, 1)
                do(nc.vector.tensor_copy(ne[:, 0, :], psN[:, 0:E]))
                do(nc.vector.tensor_tensor(cnt[:], bcast(ne[:, 0, :], 2, MAXM), bcast(W["iota"][0:PAIR, 32:32 + MAXM], 1, E), ALU.is_gt))
                do(nc.vector.tensor_reduce(ne[:, 1, :], cnt[:], AX.X, ALU.add))
                do(nc.vector.tensor_tensor_scan(ne[:, 2, :], ne[:, 1, :], zero[:], 0.0, ALU.add, ALU.add))
                do(nc.vector.tensor_tensor(ne[:, 3, :], ne[:, 2, :], ne[:, 1, :], ALU.subtract))
                do(nc.vector.tensor_scalar(ne[:, 3, :], ne[:, 3, :], float(SLOT), None, ALU.mult))
                do(nc.vector.tensor_tensor(rows[:], v3(psP), bcast(ne[:, 3, :], 1, TILES), ALU.add))
                for r in range(ranks):
                    do(nc.vector.tensor_tensor(key[:], rows[:], oh[:, r, :, :], ALU.mult))
                    do(nc.vector.tensor_reduce(slotf[:, :, r], key[:], AX.X, ALU.add))
                do(nc.vector.tensor_tensor(te[:], bcast(W["iota"][0:1, 48:48 + NT], 2, E), bcast(ne[0:1, 2, :], 1, NT), ALU.is_ge))
                do(nc.vector.tensor_reduce(tef[:], te[:], AX.X, ALU.add))
                do(nc.vector.tensor_scalar(tile_expert[:, 0:NT], tef[:], float(E - 1), None, ALU.min))
                nc.vector.tensor_copy(slot[:, :, 0:ranks], slotf[:, :, 0:ranks]).then_inc(slots_ready, 1)


def expert_stage(nc, W, name, E, NT, func, w_up, w_down, b_down, tile_expert, x_dram, y_dram):
    assert NT % 2 == 0
    with Stage(nc, name) as s:
        wu = s.sb("wu", [HD + 1, 2, 2 * F])
        wd = s.sb("wd", [128, 2, FC * D])
        wb = s.sb("wb", [1, 2, D]) if b_down is not None else None
        xs = s.sb("xs", [SLOT, 2, D])
        xT = s.sb("xT", [HD + 1, 2, 2, SLOT])
        hm = s.sb("hm", [SLOT, F])
        hT = s.sb("hT", [128, FC, SLOT])
        ys = s.sb("ys", [SLOT, 2, D])
        psX = s.ps("psX", [HD, BANK])
        psU = s.ps("psU", [SLOT, 2, BANK])
        psH = s.ps("psH", [128, 2, BANK])
        psD = s.ps("psD", [SLOT, BANK])
        up_in, down_in, x_in, y_out = ([s.sem(f"{n}{i}") for i in range(2)] for n in ("up_in", "down_in", "x_in", "y_out"))
        ones_ready, x_turned, xT_ready, up_done, hm_ready = (
            s.sem(x) for x in ("ones_ready", "x_turned", "xT_ready", "up_done", "hm_ready"))
        h_turned, hT_ready, down_done, y_ready = (s.sem(x) for x in ("h_turned", "hT_ready", "down_done", "y_ready"))
        down_parts = 2 if b_down is not None else 1
        xd = x_dram.rearrange("(n p) d -> n p d", p=SLOT)
        yd = y_dram.rearrange("(n p) d -> n p d", p=SLOT)

        def each_tile(eng, step):
            for i in range(3):
                step(i, i % 2, i // 2, i == 0)
            with eng.Fori(1, NT // 2 - 1) as k:
                step(2 * k + 1, 1, k, False)
                step(2 * k + 2, 0, k + 1, False)
            step(NT - 1, 1, NT // 2 - 1, False)

        def wait_past(eng, sem, n):
            if not (isinstance(n, int) and n <= 0):
                eng.wait_ge(sem, n)

        with nc.Block() as block:
            @block.sync
            def _(sp):
                def load(i, p, u, first):
                    e = sp.value_load(tile_expert[0:1, bass.ds(i, 1)], min_val=0, max_val=E - 1)
                    if not first:
                        wait_past(sp, up_done, i - 1)
                    sp.dma_start(wu[:, p, :], w_up[bass.ds(e, 1), :, :].rearrange("o p f -> (o p) f")).then_inc(up_in[p], 16)
                    sp.dma_start(xs[:, p, :], xd[bass.ds(i, 1), :, :].rearrange("o p f -> (o p) f")).then_inc(x_in[p], 16)
                    if not first:
                        wait_past(sp, down_done, i - 1)
                    sp.dma_start(wd[:, p, :], w_down[bass.ds(e, 1), :, :].rearrange("o p f -> (o p) f")).then_inc(down_in[p], 16)
                    if b_down is not None:
                        sp.dma_start(wb[:, p, :], b_down[bass.ds(e, 1), :]).then_inc(down_in[p], 16)

                each_tile(sp, load)
                for q in y_out:
                    sp.wait_ge(q, 16 * (NT // 2))

            @block.tensor
            def _(pe):
                def turn_hidden(i):
                    pe.wait_ge(hm_ready, i + 1)
                    wait_past(pe, hT_ready, i)
                    for c in range(FC):
                        mm = nc.tensor.transpose(psH[:, c // 3, (c % 3) * SLOT:(c % 3 + 1) * SLOT],
                                                 hm[:, c * 128:(c + 1) * 128], W["ident"][:])
                    mm.then_inc(h_turned, 1)

                def down(i, p, u):
                    pe.wait_ge(down_in[p], (u + 1) * (16 * down_parts))
                    pe.wait_ge(hT_ready, i + 1)
                    wait_past(pe, y_ready, i)
                    for c in range(FC):
                        mm = nc.tensor.matmul(psD[:, 0:D], hT[:, c, :], wd[:, p, c * D:(c + 1) * D],
                                              start=c == 0, stop=c == FC - 1 and b_down is None)
                    if b_down is not None:
                        mm = nc.tensor.matmul(psD[:, 0:D], W["ones"][0:1, 0:SLOT], wb[:, p, :], start=False, stop=True)
                    mm.then_inc(down_done, 1)

                def step(i, p, u, first):
                    pe.wait_ge(x_in[p], (u + 1) * 16)
                    if not first:
                        pe.wait_ge(xT_ready, i)
                    for k in range(2):
                        mm = nc.tensor.transpose(psX[:, k * SLOT:(k + 1) * SLOT], xs[:, p, k * HD:(k + 1) * HD], W["ident"][:])
                    mm.then_inc(x_turned, 1)
                    if not first:
                        turn_hidden(i - 1)
                    pe.wait_ge(up_in[p], (u + 1) * 16)
                    pe.wait_ge(xT_ready, i + 1)
                    for j in range(2):
                        c = j * D_IN
                        nc.tensor.matmul(psU[:, j, 0:D_IN], xT[:, p, 0, :], wu[:, p, c:c + D_IN], start=True, stop=False)
                        mm = nc.tensor.matmul(psU[:, j, 0:D_IN], xT[0:HD, p, 1, :], wu[0:HD, p, F + c:F + c + D_IN],
                                              start=False, stop=True)
                    mm.then_inc(up_done, 1)
                    if not first:
                        down(i - 1, 1 - p, u - 1 + p)

                pe.wait_ge(ones_ready, 1)
                each_tile(pe, step)
                turn_hidden(NT - 1)
                down(NT - 1, 1, NT // 2 - 1)

            @block.vector
            def _(dve):
                def step(i, p, u, first):
                    dve.wait_ge(x_turned, i + 1)
                    if not first:
                        wait_past(dve, up_done, i - 1)
                    nc.vector.tensor_copy(xT[0:HD, p, :, :], psX[:, 0:2 * SLOT].rearrange("p (k n) -> p k n", k=2)).then_inc(xT_ready, 1)
                    if not first:
                        hidden(i - 1)

                def hidden(i):
                    dve.wait_ge(h_turned, i + 1)
                    wait_past(dve, down_done, i)
                    nc.vector.tensor_copy(hT[:].rearrange("p (a b) n -> p a (b n)", a=2), psH[:, :, 0:D_IN]).then_inc(hT_ready, 1)

                nc.vector.memset(xT[HD:HD + 1, :, :, :], 1.0).then_inc(ones_ready, 1)
                each_tile(dve, step)
                hidden(NT - 1)

            @block.scalar
            def _(act):
                def result(i, p, u):
                    act.wait_ge(down_done, i + 1)
                    wait_past(act, y_out[p], u * 16)
                    nc.scalar.copy(ys[:, p, :], psD[:, 0:D]).then_inc(y_ready, 1)
                    act.wait_ge(y_ready, i + 1)
                    act.dma_start(yd[bass.ds(i, 1), :, :].rearrange("o p f -> (o p) f"), ys[:, p, :]).then_inc(y_out[p], 16)

                def step(i, p, u, first):
                    act.wait_ge(up_done, i + 1)
                    wait_past(act, h_turned, i)
                    nc.scalar.activation(hm[:].rearrange("p (a n) -> p a n", a=2), psU[:, :, 0:D_IN], func).then_inc(hm_ready, 1)
                    if not first:
                        result(i - 1, 1 - p, u - 1 + p)

                each_tile(act, step)
                result(NT - 1, 1, NT // 2 - 1)


def combine_stage(nc, W, name, ranks, y_dram, gate, slot, dst, plus=None):
    with Stage(nc, name) as s:
        y = s.sb("y", [PAIR, ranks, TILES, D])
        got = s.sem("got")
        vec = Step(s.sem("vec"))
        with nc.Block() as block:
            @block.gpsimd
            def _(pool):
                for t in range(TILES):
                    for r in range(ranks):
                        nc.gpsimd.indirect_dma_start(
                            out=y[:, r, t, :], out_offset=None, in_=y_dram[:, :],
                            in_offset=bass.IndirectOffsetOnAxis(ap=slot[:, t, r:r + 1], axis=0)).then_inc(got, 16)

            @block.vector
            def _(dve):
                if plus is not None:
                    link(dve, vec, nc.vector.tensor_tensor(dst[:], dst[:], plus[:], ALU.add))
                dve.wait_ge(got, 16 * TILES * ranks)
                for r in range(ranks):
                    for t in range(TILES):
                        vec.add(nc.vector.scalar_tensor_tensor(dst[:, t, :], y[:, r, t, :], gate[:, t, r:r + 1], dst[:, t, :],
                                                               ALU.mult, ALU.add))
                    dve.wait_ge(vec.sem, vec.n)


def mamba_layer(nc, W, x, xn, xT, H):
    ZD = D_IN + M_HEADS
    with Stage(nc, "mb") as s:
        z = s.sb("z", [PAIR, TILES, ZD])
        xh = s.sb("xh", [PAIR, TILES, D_IN])
        L = s.sb("L", [PAIR, TILES * M_HEADS, PAIR])
        cc = s.sb("cc", [128, 5, TOK])
        dt = s.sb("dt", [PAIR, TILES, M_HEADS])
        dec = s.sb("dec", [PAIR, TILES, M_HEADS])
        with Stage(nc, "mc") as p:
            xbc = p.sb("xbc", [128, 5, IMAGES, PADSEQ])
            raw = p.sb("raw", [128, 5, TOK])
            prods = []
            for c in range(5):
                rows = 128 if c < 3 else D_ST
                w0 = ZD + (c * 128 if c < 3 else D_IN + (c - 3) * D_ST)
                for g in range(2):
                    prods.append((xbc[0:rows, c, 8 * g:8 * g + 8, KCONV - 1:PADSEQ], None,
                                  [(W["win"][:, k, w0:w0 + rows], xT[:, k, g * HALF_TOK:(g + 1) * HALF_TOK]) for k in range(2)], 0))
            for t in range(TILES):
                prods.append((z[:, t, :], None, [(xT[:, k, tokens(t)], W["win"][:, k, 0:ZD]) for k in range(2)], 0))
            product_stage(nc, W, "mp", prods, ["win"])

            t1, t2, t3 = (p.sb(n, [PAIR, TILES * M_HEADS]) for n in ("t1", "t2", "t3"))
            A = p.sb("A", [PAIR, M_HEADS])
            vec, conv = Step(p.sem("vec")), Step(p.sem("conv"))
            conv_done, silus = p.sem("conv_done"), p.sem("silus")
            a_ready, z_done, dt_absd, dt_exp, dec_in, dec_out = (
                p.sem(n) for n in ("a_ready", "z_done", "dt_absd", "dt_exp", "dec_in", "dec_out"))
            dtf = dt[:].rearrange("p t h -> p (t h)")
            decf = dec[:].rearrange("p t h -> p (t h)")
            with nc.Block() as block:
                @block.vector
                def _(dve):
                    def do(ins):
                        link(dve, vec, ins)

                    for n in ("mvec", "colb"):
                        dve.wait_ge(W["sem"][n], 16)
                    do(nc.vector.tensor_tensor(dt[:], z[:, :, D_IN:ZD], bcast(W["colb"][:, 16:22], 1, TILES), ALU.add))
                    do(nc.vector.tensor_scalar(t1[:], dtf, -1.0, None, ALU.mult))
                    nc.vector.tensor_tensor(t1[:], t1[:], dtf, ALU.min).then_inc(dt_absd, 1)
                    do(nc.vector.memset(xbc[:, :, :, 0:KCONV - 1], 0.0))
                    dve.wait_ge(dt_exp, 1)
                    do(nc.vector.tensor_scalar(t2[:], t1[:], 2.0, None, ALU.add))
                    do(nc.vector.reciprocal(t2[:], t2[:]))
                    do(nc.vector.tensor_tensor(t1[:], t1[:], t2[:], ALU.mult))
                    do(nc.vector.tensor_tensor(t2[:], t1[:], t1[:], ALU.mult))
                    do(nc.vector.tensor_scalar(t3[:], t2[:], 1.0 / 17, 1.0 / 15, ALU.mult, ALU.add))
                    for odd in (13, 11, 9, 7, 5, 3, 1):
                        do(nc.vector.tensor_tensor(t3[:], t3[:], t2[:], ALU.mult))
                        do(nc.vector.tensor_scalar(t3[:], t3[:], 1.0 / odd, None, ALU.add))
                    do(nc.vector.scalar_tensor_tensor(t3[:], t3[:], 2.0, t1[:], ALU.mult, ALU.mult))
                    do(nc.vector.scalar_tensor_tensor(dtf, dtf, 0.0, t3[:], ALU.max, ALU.add))
                    dve.wait_ge(a_ready, 1)
                    nc.vector.scalar_tensor_tensor(dec[:], dt[:], -1.0, bcast(A[:], 1, TILES), ALU.mult, ALU.mult).then_inc(dec_in, 1)
                    for k in range(KCONV):
                        for c in range(5):
                            r = 128 if c < 3 else D_ST
                            src = xbc[0:r, c, :, k:k + SEQ]
                            dst = raw[0:r, c, :].rearrange("p (b q) -> p b q", b=IMAGES)
                            tap = W["mvec"][0:r, c, k:k + 1]
                            if k:
                                dve.wait_ge(conv.sem, 5 * (k - 1) + c + 1)
                            conv.add(nc.vector.tensor_scalar(dst, src, tap, None, ALU.mult) if k == 0 else
                                     nc.vector.scalar_tensor_tensor(dst, src, tap, dst, ALU.mult, ALU.add))

                @block.scalar
                def _(act):
                    act.wait_ge(W["sem"]["colb"], 16)
                    nc.scalar.activation(A[:], W["colb"][:, 24:30], ACT.Exp).then_inc(a_ready, 1)
                    act.wait_ge(dt_absd, 1)
                    nc.scalar.activation(t1[:], t1[:], ACT.Exp).then_inc(dt_exp, 1)
                    act.wait_ge(dec_in, 1)
                    nc.scalar.activation(decf, decf, ACT.Exp).then_inc(dec_out, 1)
                    for t in range(TILES):
                        nc.scalar.activation(z[:, t, 0:D_IN], z[:, t, 0:D_IN], ACT.Silu).then_inc(z_done, 1)
                    for c in range(5):
                        r = 128 if c < 3 else D_ST
                        act.wait_ge(conv.sem, 5 * (KCONV - 1) + c + 1)
                        nc.scalar.activation(cc[0:r, c, :], raw[0:r, c, :], ACT.Silu, bias=W["mvec"][0:r, c, 4:5], scale=1.0).then_inc(silus, 1)

        with Stage(nc, "md") as p:
            decT = p.sb("decT", [M_HEADS, TOK])
            d0 = p.sb("d0", [PAIR, TILES, M_HEADS, PAIR])
            d1 = p.sb("d1", [PAIR, TILES * M_HEADS, PAIR])
            psD = p.ps("psD", [M_HEADS, 2, BANK])
            psB = p.ps("psB", [PAIR, 2, BANK])
            psX = p.ps("psX", [PAIR, 2, BANK])
            psG = p.ps("psG", [PAIR, 2, BANK])
            dec_turned, decT_ready, spread, masked, scanned = (p.sem(n) for n in ("dec_turned", "decT_ready", "spread", "masked", "scanned"))
            x_turned, x_kept, g_ready, d1_ready, weighted = (p.sem(n) for n in ("x_turned", "x_kept", "g_ready", "d1_ready", "weighted"))
            with nc.Block() as block:
                @block.tensor
                def _(pe):
                    for t in range(TILES):
                        mm = nc.tensor.transpose(psD[:, t // 4, (t % 4) * PAIR:(t % 4 + 1) * PAIR], dec[:, t, :], W["ident"][0:PAIR, 0:PAIR])
                    mm.then_inc(dec_turned, 1)
                    for t in range(TILES):
                        mm = nc.tensor.matmul(psG[:, t // 4, (t % 4) * PAIR:(t % 4 + 1) * PAIR], cc[0:D_ST, 3, tokens(t)],
                                              cc[0:D_ST, 4, tokens(t)], start=True, stop=True)
                    mm.then_inc(g_ready, 1)
                    pe.wait_ge(decT_ready, 2)
                    pe.wait_ge(W["sem"]["sel"], 16)
                    for hd in range(M_HEADS):
                        for g in range(2):
                            n = 2 * hd + g
                            if n >= 2:
                                pe.wait_ge(masked, n - 1)
                            nc.tensor.matmul(psB[:, g, 0:HALF_TOK], W["sel"][:, hd, :], decT[:, g * HALF_TOK:(g + 1) * HALF_TOK],
                                             start=True, stop=True).then_inc(spread, 1)
                    for t in range(TILES):
                        if t >= 2:
                            pe.wait_ge(x_kept, t - 1)
                        for c in range(3):
                            mm = nc.tensor.transpose(psX[:, t % 2, c * 128:(c + 1) * 128], cc[:, c, tokens(t)], W["ident"][:])
                        mm.then_inc(x_turned, 1)

                @block.scalar
                def _(act):
                    act.wait_ge(dec_turned, 1)
                    for g in range(2):
                        nc.scalar.copy(decT[:, g * HALF_TOK:(g + 1) * HALF_TOK], psD[:, g, 0:HALF_TOK]).then_inc(decT_ready, 1)
                    for t in range(TILES):
                        act.wait_ge(x_turned, t + 1)
                        nc.scalar.copy(xh[:, t, :], psX[:, t % 2, 0:D_IN]).then_inc(x_kept, 1)

                @block.gpsimd
                def _(pool):
                    nc.gpsimd.tensor_tensor(d1[:], bcast(W["ident"][0:PAIR, 0:PAIR], 1, TILES * M_HEADS),
                                            bcast(dt[:].rearrange("p t h -> p (t h)"), 2, PAIR), ALU.mult).then_inc(d1_ready, 1)

                @block.vector
                def _(dve):
                    dve.wait_ge(W["sem"]["lmask"], 16)
                    for hd in range(M_HEADS):
                        for g in range(2):
                            n = 2 * hd + g
                            dve.wait_ge(spread, n + 1)
                            nc.vector.tensor_tensor(d0[:, 4 * g:4 * g + 4, hd, :], psB[:, g, 0:HALF_TOK].rearrange("p (t i) -> p t i", t=4),
                                                    bcast(W["lmask"][:], 1, 4), ALU.mult).then_inc(masked, 1)
                    dve.wait_ge(masked, 2 * M_HEADS)
                    dve.wait_ge(d1_ready, 1)
                    nc.vector.tensor_tensor_scan(L[:].rearrange("p a i -> p (a i)"), d0[:].rearrange("p t h i -> p (t h i)"),
                                                 d1[:].rearrange("p a i -> p (a i)"), 0.0, ALU.mult, ALU.add).then_inc(scanned, 1)
                    dve.wait_ge(scanned, 1)
                    dve.wait_ge(g_ready, 1)
                    for t in range(TILES):
                        Lt = L[:, t * M_HEADS:(t + 1) * M_HEADS, :]
                        nc.vector.tensor_tensor(Lt, bcast(psG[:, t // 4, (t % 4) * PAIR:(t % 4 + 1) * PAIR], 1, M_HEADS), Lt,
                                                ALU.mult).then_inc(weighted, 1)

        with Stage(nc, "me") as p:
            g = p.sb("g", [PAIR, TILES, D_IN])
            sq = p.sb("sq", [PAIR, TILES, D_IN])
            ms = p.sb("ms", [PAIR, 3, TILES])
            gT = p.sb("gT", [128, 3, TOK])
            y_ready, y_read, vec = p.sem("y_ready"), p.sem("y_read"), Step(p.sem("vec"))
            dx_ready, var_ready, rstd_ready = p.sem("dx_ready"), p.sem("var_ready"), p.sem("rstd_ready")
            with Stage(nc, "my") as q:
                psY = q.ps("psY", [PAIR, 4, BANK])
                with nc.Block() as block:
                    @block.tensor
                    def _(pe):
                        for t in range(TILES):
                            if t >= 4:
                                pe.wait_ge(y_read, t - 3)
                            for hd in range(M_HEADS):
                                mm = nc.tensor.matmul(psY[:, t % 4, hd * DH:(hd + 1) * DH], L[:, t * M_HEADS + hd, :],
                                                      xh[:, t, hd * DH:(hd + 1) * DH], start=True, stop=True)
                            mm.then_inc(y_ready, 1)

                    @block.gpsimd
                    def _(pool):
                        pool.wait_ge(var_ready, 1)
                        nc.gpsimd.tensor_tensor(ms[:, 2, :], ms[:, 1, :], W["mhalf"][0:PAIR, 0:TILES], ALU.pow).then_inc(rstd_ready, 1)

                    @block.vector
                    def _(dve):
                        dve.wait_ge(W["sem"]["rowp"], 16)
                        link(dve, vec, nc.vector.tensor_tensor(g[:], xh[:], bcast(W["rowp"][:, 0, :], 1, TILES), ALU.mult))
                        for t in range(TILES):
                            dve.wait_ge(y_ready, t + 1)
                            nc.vector.tensor_tensor(g[:, t, :], psY[:, t % 4, 0:D_IN], g[:, t, :], ALU.add).then_inc(y_read, 1)
                        dve.wait_ge(y_read, TILES)
                        link(dve, vec, nc.vector.tensor_tensor(g[:], g[:], z[:, :, 0:D_IN], ALU.mult))
                        link(dve, vec, nc.vector.tensor_tensor(sq[:], g[:], g[:], ALU.mult))
                        link(dve, vec, nc.vector.tensor_reduce(ms[:, 0, :], sq[:], AX.X, ALU.add))
                        nc.vector.tensor_scalar(ms[:, 1, :], ms[:, 0, :], 1.0 / D_IN, 1e-5, ALU.mult, ALU.add).then_inc(var_ready, 1)
                        dve.wait_ge(rstd_ready, 1)
                        for t in range(TILES):
                            vec.add(nc.vector.scalar_tensor_tensor(g[:, t, :], g[:, t, :], ms[:, 2, t:t + 1], W["rowp"][:, 1, :], ALU.mult, ALU.mult))
                        dve.wait_ge(vec.sem, vec.n)
                        vec.add(nc.vector.tensor_tensor(H[:], H[:], x[:], ALU.add))
            channels_stage(nc, W, "mf", g, gT)
            prods = [(H[:, t, :], None, [(gT[:, k, tokens(t)], W["wout"][:, k, :]) for k in range(3)], 0) for t in range(TILES)]
            product_stage(nc, W, "mg", prods, ["wout"], add=True)


E0, E1 = 8, 16
NT0 = expert_tiles(E0, 2 * TOK) // 2 * 2 + 2 * (expert_tiles(E0, 2 * TOK) % 2)
NT1 = expert_tiles(E1, TOK) // 2 * 2 + 2 * (expert_tiles(E1, TOK) % 2)

RESIDENT = {
    "stem_w": (48, C1), "chan": (C1, 6, 3), "tabs": (128, 72), "ident": (128, 128), "off_w": (C1, TAPS, 32),
    "dcn_w": (C1, TAPS, D), "wq": (HD, 2, HEADS * DH), "wk": (HD, 2, HEADS * DH), "qkvb": (128, 3, 6),
    "amask": (PAIR, PAIR), "wv": (HD, 2, HEADS * DH), "wo": (128, 6, D), "rowb": (1, 2, D), "w1": (HD + 1, 2, 3 * D),
    "cmask": (HD, HD), "w2": (HD, 2, D), "imean": (PAIR, PAIR), "before": (PAIR, PAIR), "iota": (128, 80),
    "wr0": (HD, 2, E0), "sel": (M_HEADS, M_HEADS, PAIR), "lmask": (PAIR, PAIR), "mvec": (128, 5, 5),
    "wr1": (HD, 2, E1), "win": (HD, 2, 2 * D_IN + 2 * D_ST + M_HEADS), "wout": (128, 3, D),
}
LATE = {"w1", "w2", "win", "wout", "mvec", "rowd", "rowp"}
SPREAD = {"colb": 32, "rowd": 7 * D, "rowp": 2 * D_IN}
STREAMED = {"x": (48, IMAGES * PIX), "up0": (E0, HD + 1, 2 * F), "down0": (E0, 128, FC * D), "bdown0": (E0, D),
            "up1": (E1, HD + 1, 2 * F), "down1": (E1, 128, FC * D)}


def vit_tower(nc, K, out):
    W = {"sem": {}}
    with ExitStack() as top:
        def sb(name, shape, dt=F32):
            return top.enter_context(nc.sbuf_tensor(name, list(shape), dt))

        def place(late):
            for name, shape in RESIDENT.items():
                if (name in LATE) == late:
                    W[name] = sb(name, shape)
                    W["sem"][name] = nc.alloc_semaphore(f"in_{name}")
            for name, n in SPREAD.items():
                if (name in LATE) == late:
                    W[name] = sb(name, (PAIR, n))
                    W["sem"][name] = nc.alloc_semaphore(f"in_{name}")

        def fetch(act, late):
            for name in RESIDENT:
                if (name in LATE) == late:
                    act.dma_start(W[name][:], K[name]).then_inc(W["sem"][name], 16)
            for name in SPREAD:
                if (name in LATE) == late:
                    act.dma_start(W[name][:], K[name].partition_broadcast(PAIR)).then_inc(W["sem"][name], 16)

        place(False)
        W["mhalf"], W["ones"], W["bnv"] = sb("mhalf", (128, 8)), sb("ones", (128, 128)), sb("bnv", (C1, 3, 3))
        H = sb("H", (PAIR, TILES, D))
        off_dram = nc.dram_tensor("points", (IMAGES, 32, POS), F32, kind="Internal").ap()
        a_dram = nc.dram_tensor("channel_rows", (IMAGES, D, SEQ), F32, kind="Internal").ap()
        xs0, ys0 = (nc.dram_tensor(n, (NT0 * SLOT, D), F32, kind="Internal").ap() for n in ("rows0", "results0"))
        xs1, ys1 = (nc.dram_tensor(n, (NT1 * SLOT, D), F32, kind="Internal").ap() for n in ("rows1", "results1"))
        ones_done = nc.alloc_semaphore("ones_done")

        with nc.Block() as block:
            @block.scalar
            def _(act):
                fetch(act, False)

            @block.vector
            def _(dve):
                nc.vector.memset(W["ones"][:], 1.0).then_inc(ones_done, 1)
                dve.wait_ge(ones_done, 1)

        with nc.cleanup_on_exit(), Stage(nc, "pe") as s:
            h = s.sb("h", [C1, IMAGES, PIX])
            samp = s.sb("samp", [C1, TAPS, IMAGES * POS])
            stem_stage(nc, K, W, h, samp, off_dram)
            sampling_stage(nc, K, W, h, samp, off_dram)
            patch_stage(nc, K, W, samp, H)
        place(True)
        with nc.Block() as block:
            @block.scalar
            def _(act):
                fetch(act, True)
        W["rowd"] = W["rowd"][:].rearrange("p (a d) -> p a d", d=D)
        W["rowp"] = W["rowp"][:].rearrange("p (a d) -> p a d", d=D_IN)
        with nc.cleanup_on_exit():
            attention_layer(nc, W, H)
        with nc.cleanup_on_exit(), Stage(nc, "l0") as s:
            X = s.sb("X", [PAIR, TILES, D])
            xT = s.sb("xT", [HD + 1, 2, TOK])
            Y = s.sb("Y", [PAIR, TILES, D])
            YT = s.sb("YT", [HD, 2, TOK])
            gate, slot, te = s.sb("gate", [PAIR, TILES, 2]), s.sb("slot", [PAIR, TILES, 2], U32), s.sb("te", [1, 32], I32)
            ones_row = s.sem("ones_row")
            norm_stage(nc, W, "l0_n", H, X, 1e-5)
            channels_stage(nc, W, "l0_c", X, xT[0:HD, :, :])
            with nc.Block() as block:
                @block.vector
                def _(dve):
                    nc.vector.memset(xT[HD:HD + 1, :, :], 1.0).then_inc(ones_row, 1)
                    dve.wait_ge(ones_row, 1)
                    dve.wait_ge(W["sem"]["rowd"], 16)
            channel_attention(nc, W, xT, X, a_dram, Y, YT)
            global_norm_stage(nc, W, "l0_g", X, Y, W["rowd"][:, 0, :], W["rowd"][:, 1, :])
            channels_stage(nc, W, "l0_d", Y, YT)
            routing_stage(nc, W, "l0_r", E0, 2, NT0, YT, W["wr0"], "wr0", True, Y, xs0, gate, slot, te)
            expert_stage(nc, W, "l0_e", E0, NT0, ACT.Gelu_apprx_tanh, K["up0"], K["down0"], K["bdown0"], te, xs0, ys0)
            combine_stage(nc, W, "l0_m", 2, ys0, gate, slot, Y)
            global_norm_stage(nc, W, "l0_h", Y, X, W["rowd"][:, 2, :], W["rowd"][:, 3, :], add_to=H)
        with nc.cleanup_on_exit(), Stage(nc, "l1") as s:
            X = s.sb("X", [PAIR, TILES, D])
            XN = s.sb("XN", [PAIR, TILES, D])
            xT = s.sb("xT", [HD, 2, TOK])
            norm_stage(nc, W, "l1_a", H, X, 1e-5)
            norm_stage(nc, W, "l1_b", X, XN, 1e-5, gain=W["rowd"][:, 4, :], shift=W["rowd"][:, 5, :])
            channels_stage(nc, W, "l1_c", XN, xT)
            mamba_layer(nc, W, X, XN, xT, H)
        with nc.cleanup_on_exit(), Stage(nc, "l2") as s:
            X = s.sb("X", [PAIR, TILES, D])
            XN = s.sb("XN", [PAIR, TILES, D])
            xT = s.sb("xT", [HD, 2, TOK])
            gate, slot, te = s.sb("gate", [PAIR, TILES, 2]), s.sb("slot", [PAIR, TILES, 2], U32), s.sb("te", [1, 32], I32)
            norm_stage(nc, W, "l2_a", H, X, 1e-5)
            norm_stage(nc, W, "l2_b", X, XN, 1e-6, rms=True, gain=W["rowd"][:, 6, :])
            channels_stage(nc, W, "l2_c", XN, xT)
            routing_stage(nc, W, "l2_r", E1, 1, NT1, xT, W["wr1"], "wr1", False, XN, xs1, gate, slot, te)
            expert_stage(nc, W, "l2_e", E1, NT1, ACT.Relu, K["up1"], K["down1"], None, te, xs1, ys1)
            combine_stage(nc, W, "l2_m", 1, ys1, gate, slot, H, plus=X)
        out_done = nc.alloc_semaphore("out_done")
        with nc.Block() as block:
            @block.sync
            def _(sp):
                for q in W["sem"].values():
                    sp.wait_ge(q, 16)
                sp.dma_start(out.rearrange("(t o) q d -> (o q) t d", o=2), H[:]).then_inc(out_done, 16)
                sp.wait_ge(out_done, 16)


def layouts(a):
    f = np.float32

    def halves(w):
        return w.reshape(2, HD, -1).transpose(1, 0, 2)

    def biased(w, b):
        lo = np.concatenate([w[:HD], b[None]], 0)
        hi = np.concatenate([w[HD:], np.zeros_like(b)[None]], 0)
        return np.stack([lo, hi], 1)

    K = {}
    x = a["x"].reshape(IMAGES, 3, SIDE, 4, SIDE, 4)
    K["x"] = x.transpose(1, 3, 5, 0, 2, 4).reshape(48, IMAGES * PIX)
    K["stem_w"] = a["L0_tok_stem_w"].reshape(C1, 48).T
    chan = np.zeros((C1, 6, 3), f)
    for i, n in enumerate("gbmv"):
        chan[:, i, 0] = a[f"L0_tok_bn1_{n}"]
        chan[:, i, 1:] = a[f"L0_tok_bn2_{n}"].reshape(2, HD).T
    chan[:, 4, 0] = a["L0_tok_stem_b"]
    chan[:, 4, 1:] = a["L0_tok_dcn_b"].reshape(2, HD).T
    chan[:, 5, 0:2] = a["cls_tok"].reshape(2, HD).T
    K["chan"] = chan
    by_axis = lambda v: np.ascontiguousarray(v.reshape((TAPS, 2) + v.shape[1:]).swapaxes(0, 1)).reshape(v.shape)
    K["off_w"] = by_axis(a["L0_tok_off_w"]).reshape(32, C1, TAPS).transpose(1, 2, 0)
    tabs = np.zeros((128, 72), f)
    p = np.arange(CHUNK)
    for c in range(CHUNKS):
        tabs[:CHUNK, c] = -(ROWS * c + p // SIDE)
    tabs[:CHUNK, 7] = -(p % SIDE)
    tabs[:32, 8] = by_axis(a["L0_tok_off_b"])
    pos, tap = np.arange(POS), np.arange(TAPS)
    tabs[0:16, 16:16 + POS] = 4 * (pos // OUT_SIDE)[None] + (tap // 4)[:, None]
    tabs[16:32, 16:16 + POS] = 4 * (pos % OUT_SIDE)[None] + (tap % 4)[:, None]
    K["tabs"] = tabs
    K["ident"] = np.eye(128, dtype=f)
    K["dcn_w"] = a["L0_tok_dcn_w"].reshape(D, C1, TAPS).transpose(1, 2, 0)
    for n, w in (("wq", "Q"), ("wk", "K"), ("wv", "V")):
        K[n] = halves(a[f"L0_attn_W_{w}"].transpose(1, 0, 2).reshape(D, HEADS * DH))
    K["qkvb"] = np.stack([a[f"L0_attn_b_{n}"].reshape(6, 128).T for n in "QKV"], 1)
    K["wo"] = a["L0_attn_W_O"].reshape(6, 128, D).transpose(1, 0, 2)
    K["rowb"] = np.stack([a["L0_attn_b_O"], a["L0_ffn_W2_b"]])[None]
    K["w1"] = biased(a["L0_ffn_W1_w"], a["L0_ffn_W1_b"])
    K["w2"] = halves(a["L0_ffn_W2_w"])
    q = np.arange(PAIR)
    same = q[:, None] // SEQ == q[None] // SEQ
    K["amask"] = np.where(same & (q[None] <= q[:, None]), 0, NEG).astype(f)
    c = np.arange(HD)
    K["cmask"] = np.where(c[:, None] // 16 == c[None] // 16, 0, NEG).astype(f)
    K["imean"] = (same / SEQ).astype(f)
    K["before"] = (q[:, None] < q[None]).astype(f)
    iota = np.zeros((128, 80), f)
    iota[:, 0:32] = np.arange(32)
    iota[:, 32:40] = SLOT * np.arange(8)
    iota[:, 48:80] = np.arange(32)
    K["iota"] = iota
    K["wr0"], K["wr1"] = halves(a["L0_ffn_r_w"]), halves(a["L1_ffn_w_router"])
    K["sel"] = np.repeat(np.eye(M_HEADS, dtype=f)[:, :, None], PAIR, 2)
    K["lmask"] = (same & (q[None] > q[:, None])).astype(f)
    conv = np.concatenate([a["L1_attn_conv_w"], a["L1_attn_conv_b"][:, None]], 1)
    mvec = np.zeros((128, 5, 5), f)
    mvec[:, 0:3] = conv[:D_IN].reshape(3, 128, 5).transpose(1, 0, 2)
    mvec[:D_ST, 3:5] = conv[D_IN:].reshape(2, D_ST, 5).transpose(1, 0, 2)
    K["mvec"] = mvec
    w = a["L1_attn_W_in"]
    K["win"] = halves(np.concatenate([w[:, :D_IN], w[:, -M_HEADS:], w[:, D_IN:-M_HEADS]], 1))
    K["wout"] = a["L1_attn_W_out"].reshape(3, 128, D).transpose(1, 0, 2)
    colb = np.zeros(32, f)
    colb[0:8], colb[16:22], colb[24:30] = a["L0_ffn_r_b"], a["L1_attn_dt_bias"], a["L1_attn_A_log"]
    K["colb"] = colb
    K["rowd"] = np.concatenate([a[n] for n in ("L0_ffn_ln1_w", "L0_ffn_ln1_b", "L0_ffn_ln2_w", "L0_ffn_ln2_b",
                                               "L1_attn_ln_w", "L1_attn_ln_b", "L1_ffn_ln_w")])
    K["rowp"] = np.concatenate([np.repeat(a["L1_attn_D"], DH), a["L1_attn_rms_w"]])

    def up(w, b):
        w = w.reshape(-1, 2, HD, F).transpose(0, 2, 1, 3)
        row = np.stack([b, np.zeros_like(b)], 1)[:, None]
        return np.concatenate([w, row], 1).reshape(-1, HD + 1, 2 * F)

    def down(w):
        return w.reshape(-1, FC, 128, D).transpose(0, 2, 1, 3).reshape(-1, 128, FC * D)

    K["up0"], K["down0"], K["bdown0"] = up(a["L0_ffn_fc_w"], a["L0_ffn_fc_b"]), down(a["L0_ffn_proj_w"]), a["L0_ffn_proj_b"]
    K["up1"], K["down1"] = up(a["L1_ffn_wi"], np.zeros((E1, F), f)), down(a["L1_ffn_wo"])
    return {n: np.ascontiguousarray(v) for n, v in K.items()}


def kernel(**inputs):
    import concourse.bacc as bacc
    from concourse.bass_utils import run_bass_kernel_spmd

    nc = bacc.Bacc("TRN2", target_bir_lowering=False, num_devices=1)
    arrays = layouts({n: np.asarray(v) for n, v in inputs.items()})
    K = {n: nc.dram_tensor(f"in_{n}", v.shape, mybir.dt.from_np(v.dtype), kind="ExternalInput").ap() for n, v in arrays.items()}
    out = nc.dram_tensor("out", (IMAGES, SEQ, D), F32, kind="ExternalOutput").ap()
    vit_tower(nc, K, out)
    r = run_bass_kernel_spmd(nc, [{f"in_{n}": v for n, v in arrays.items()}], core_ids=[0])
    return r.results[0]["out"]
```

```python
from contextlib import ExitStack

import numpy as np

import concourse.bass as bass
from concourse import mybir

F32 = mybir.dt.float32
I32 = mybir.dt.int32
U32 = mybir.dt.uint32
ALU = mybir.AluOpType
ACT = mybir.ActivationFunctionType
AX = mybir.AxisListType

IMAGES = 16
SIDE = 28
PIX = SIDE * SIDE
TAPS = 16
OUT_SIDE = 7
POS = OUT_SIDE * OUT_SIDE
SEQ = POS + 1
C1 = 96
D = 192
HD = 96
TOK = IMAGES * SEQ
PAIR = 2 * SEQ
TILES = TOK // PAIR
HALF_TOK = TOK // 2
ROWS = 4
CHUNK = ROWS * SIDE
CHUNKS = PIX // CHUNK
HALF = PIX // 2
HEADS = 12
DH = 64
F = 768
FC = F // 128
SLOT = 128
BANK = 512
D_IN = 384
D_ST = 64
M_HEADS = 6
KCONV = 4
PADSEQ = SEQ + KCONV - 1
ROW = D + 2
NO_ROW = 4096
NEG = -1e30


def expert_tiles(experts, assignments):
    return (assignments + experts * (SLOT - 1)) // SLOT


class Stage:

    def __init__(self, nc, name):
        self.nc, self.name, self.stack = nc, name, ExitStack()

    def __enter__(self):
        self.stack.__enter__()
        return self

    def __exit__(self, *a):
        return self.stack.__exit__(*a)

    def sb(self, name, shape, dt=F32):
        return self.stack.enter_context(self.nc.sbuf_tensor(f"{self.name}_{name}", shape, dt))

    def ps(self, name, shape, dt=F32):
        return self.stack.enter_context(self.nc.psum_tensor(f"{self.name}_{name}", shape, dt))

    def sem(self, name):
        return self.nc.alloc_semaphore(f"{self.name}_{name}")


class Step:

    def __init__(self, sem):
        self.sem, self.n = sem, 0

    def add(self, ins):
        ins.then_inc(self.sem, 1)
        self.n += 1
        return self.n


def link(eng, step, ins):
    eng.wait_ge(step.sem, step.add(ins))


def bcast(ap, axis, n):
    a = ap.unsqueeze(axis)
    shape = list(a.shape)
    shape[axis] = n
    return a.broadcast_to(shape)


def stem_stage(nc, K, W, h, samp, off_dram, all_near):
    NCH = 2 * IMAGES
    with Stage(nc, "stem") as s:
        im2col = samp[:].rearrange("p a b -> p (a b)")[:, 0:IMAGES // 2 * PIX]
        tmp = s.sb("tmp", [C1, 3, HALF])
        offs = s.sb("offs", [32, IMAGES, POS])
        ps = s.ps("ps", [C1, 4, BANK])
        pso = s.ps("pso", [128, BANK])
        psum4 = s.ps("psum4", [32, BANK])
        parts = s.sb("parts", [128, 8 * POS])
        starts = [0, 1, 2, 4, IMAGES // 2]
        x_in = [s.sem(f"x_in{i}") for i in range(4)]
        off_part, off_kept = s.sem("off_part"), s.sem("off_kept")
        near = s.sb("near", [32, 8 * POS])
        near_n = s.sb("near_n", [32, 2])
        psn = s.ps("psn", [1, BANK])
        near_ready, near_summed, near_out = s.sem("near_ready"), s.sem("near_summed"), s.sem("near_out")
        vec = Step(s.sem("vec"))
        var_ready, rstd_ready, bn_ready = s.sem("var_ready"), s.sem("rstd_ready"), s.sem("bn_ready")
        conv_ready, scaled, leaky = s.sem("conv_ready"), s.sem("scaled"), s.sem("leaky")
        off_ready, off_based, off_out = s.sem("off_ready"), s.sem("off_based"), s.sem("off_out")
        cv, bnv = W["chan"], W["bnv"]
        with nc.Block() as block:
            @block.sync
            def _(sp):
                for i in range(4):
                    c = slice(starts[i] * PIX, starts[i + 1] * PIX)
                    sp.dma_start(im2col[:, c], K["x"][:, c]).then_inc(x_in[i], 16)
                sp.wait_ge(off_based, 2)
                sp.dma_start(off_dram.rearrange("b c p -> c b p"), offs[:]).then_inc(off_out, 16)
                sp.wait_ge(off_out, 16)

            @block.gpsimd
            def _(pool):
                pool.wait_ge(var_ready, 1)
                nc.gpsimd.tensor_tensor(bnv[:, 0, :], bnv[:, 0, :], W["mhalf"][0:C1, 0:3], ALU.pow).then_inc(rstd_ready, 1)

            @block.tensor
            def _(pe):
                pe.wait_ge(W["sem"]["stem_w"], 16)
                for n in range(NCH):
                    if n < IMAGES and n % 2 == 0 and n // 2 in starts:
                        pe.wait_ge(x_in[starts.index(n // 2)], 16)
                    if n >= 4:
                        pe.wait_ge(scaled, n - 3)
                    nc.tensor.matmul(ps[:, n % 4, 0:HALF], W["stem_w"][:, n // IMAGES, :],
                                     im2col[:, n % IMAGES * HALF:(n % IMAGES + 1) * HALF],
                                     start=True, stop=True).then_inc(conv_ready, 1)
                for name in ("off_w", "stack4"):
                    pe.wait_ge(W["sem"][name], 16)
                for half in range(2):
                    pe.wait_ge(leaky, (half + 1) * NCH // 2)
                    grid = h[:, half * 8:(half + 1) * 8, :].rearrange(
                        "p b (i r j s) -> p b i r j s", i=OUT_SIDE, r=4, j=OUT_SIDE)
                    if half:
                        pe.wait_ge(off_part, 1)
                    for tap in range(TAPS):
                        q = 32 * (tap % 4)
                        mm = nc.tensor.matmul(pso[q:q + 32, 0:8 * POS].rearrange("p (b i j) -> p b i j", b=8, i=OUT_SIDE),
                                              W["off_w"][:, tap, :], grid[:, :, :, tap // 4, :, tap % 4],
                                              start=tap < 4, stop=tap >= TAPS - 4)
                    mm.then_inc(off_ready, 1)
                    pe.wait_ge(off_part, half + 1)
                    if half:
                        pe.wait_ge(near_ready, 1)
                    nc.tensor.matmul(psum4[:, 0:8 * POS], W["stack4"][:], parts[:], start=True, stop=True).then_inc(off_kept, 1)
                pe.wait_ge(near_ready, 2)
                for half in range(2):
                    mm = nc.tensor.matmul(psn[:, 0:1], near_n[:, half:half + 1], W["ones"][0:32, 0:1], start=half == 0, stop=half == 1)
                mm.then_inc(near_summed, 1)

            @block.scalar
            def _(act):
                act.wait_ge(bn_ready, 1)
                for n in range(NCH):
                    act.wait_ge(conv_ready, n + 1)
                    if n >= 3:
                        act.wait_ge(leaky, n - 2)
                    nc.scalar.activation(tmp[:, n % 3, :], ps[:, n % 4, 0:HALF], ACT.Identity,
                                         bias=bnv[:, 2, 0:1], scale=bnv[:, 1, 0:1]).then_inc(scaled, 1)
                for half in range(2):
                    act.wait_ge(off_ready, half + 1)
                    if half:
                        act.wait_ge(off_kept, 1)
                    nc.scalar.copy(parts[:], pso[:, 0:8 * POS]).then_inc(off_part, 1)

            @block.vector
            def _(dve):
                for name in ("chan", "tabs"):
                    dve.wait_ge(W["sem"][name], 16)
                nc.vector.memset(W["mhalf"][:], -0.5).then_inc(vec.sem, 1)
                vec.n += 1
                dve.wait_ge(vec.sem, vec.n)
                nc.vector.tensor_scalar(bnv[:, 0, :], cv[:, 3, :], 1e-5, None, ALU.add).then_inc(var_ready, 1)
                dve.wait_ge(rstd_ready, 1)
                link(dve, vec, nc.vector.tensor_tensor(bnv[:, 1, :], bnv[:, 0, :], cv[:, 0, :], ALU.mult))
                link(dve, vec, nc.vector.tensor_tensor(bnv[:, 2, :], cv[:, 4, :], cv[:, 2, :], ALU.subtract))
                link(dve, vec, nc.vector.tensor_tensor(bnv[:, 2, :], bnv[:, 2, :], bnv[:, 1, :], ALU.mult))
                nc.vector.tensor_tensor(bnv[:, 2, :], bnv[:, 2, :], cv[:, 1, :], ALU.add).then_inc(bn_ready, 1)
                for n in range(NCH):
                    dve.wait_ge(scaled, n + 1)
                    t = tmp[:, n % 3, :]
                    nc.vector.scalar_tensor_tensor(h[:, n // 2, (n % 2) * HALF:(n % 2 + 1) * HALF], t, 0.01, t,
                                                   ALU.mult, ALU.max).then_inc(leaky, 1)
                for half in range(2):
                    dve.wait_ge(off_kept, half + 1)
                    nc.vector.scalar_tensor_tensor(
                        offs[:, half * 8:(half + 1) * 8, :],
                        psum4[:, 0:8 * POS].rearrange("p (b q) -> p b q", b=8), W["tabs"][0:32, 8:9],
                        bcast(W["tabs"][0:32, 16:16 + POS], 1, 8), ALU.add, ALU.add).then_inc(off_based, 1)
                    link(dve, vec, nc.vector.tensor_scalar(near[:], psum4[:, 0:8 * POS], W["tabs"][0:32, 8:9], None, ALU.add))
                    link(dve, vec, nc.vector.tensor_tensor(near[:], near[:], near[:], ALU.mult))
                    link(dve, vec, nc.vector.tensor_scalar(near[:], near[:], float(ROWS) ** 2, None, ALU.is_lt))
                    nc.vector.tensor_reduce(near_n[:, half:half + 1], near[:], AX.X, ALU.add).then_inc(near_ready, 1)
                    if half == 0:
                        dve.wait_ge(near_ready, 1)
                dve.wait_ge(near_summed, 1)
                nc.vector.tensor_scalar(all_near[:], psn[:, 0:1], 32.0 * IMAGES * POS, None, ALU.is_ge).then_inc(near_out, 1)
                dve.wait_ge(near_out, 1)


def sampling_stage(nc, K, W, h, samp, off_dram):
    RING = 4
    with Stage(nc, "smp") as s:
        pxy = s.sb("pxy", [CHUNK, 2, 2, PIX])
        xw = s.sb("xw", [CHUNK, 2, PIX])
        dist = s.sb("dist", [CHUNK, 2, PIX])
        rest = s.sb("rest", [CHUNK, PIX])
        S = s.sb("S", [CHUNK, RING, PIX])
        hT = s.sb("hT", [CHUNK, 2, CHUNKS, C1])
        psT = s.ps("psT", [CHUNK, 2, BANK])
        acc = s.ps("acc", [C1, 2, 2, BANK])
        loaded = [s.sem(f"loaded{i}") for i in range(2)]
        turned, hT_ready = s.sem("turned"), s.sem("hT_ready")
        dist_ready, S_ready, S_used = s.sem("dist_ready"), s.sem("S_ready"), s.sem("S_used")
        rest_ready, dist_used = s.sem("rest_ready"), s.sem("dist_used")
        sampled, kept = s.sem("sampled"), s.sem("kept")
        xlink = Step(s.sem("xlink"))
        tabs = W["tabs"]
        PER = CHUNKS + 1
        with nc.Block() as block:
            @block.sync
            def _(sp):
                for b in range(IMAGES):
                    if b >= 2:
                        sp.wait_ge(dist_ready, (b - 1) * PER)
                    sp.dma_start(pxy[:, b % 2, :, :].rearrange("p a q -> p (a q)"),
                                 off_dram[b].rearrange("c p -> (c p)").partition_broadcast(CHUNK)).then_inc(loaded[b % 2], 16)

            @block.tensor
            def _(pe):
                def turn(b):
                    if b >= 1:
                        pe.wait_ge(hT_ready, b * 2)
                    for c in range(CHUNKS):
                        mm = nc.tensor.transpose(psT[:, c // 4, (c % 4) * C1:(c % 4 + 1) * C1],
                                                 h[:, b, c * CHUNK:(c + 1) * CHUNK], W["ident"][0:C1, 0:C1])
                    mm.then_inc(turned, 1)

                pe.wait_ge(W["sem"]["ident"], 16)
                turn(0)
                for b in range(IMAGES):
                    if b + 1 < IMAGES:
                        turn(b + 1)
                    pe.wait_ge(hT_ready, 2 * (b + 1))
                    if b >= 2:
                        pe.wait_ge(kept, 2 * (b - 1))
                    for c in range(CHUNKS):
                        n = b * CHUNKS + c
                        pe.wait_ge(S_ready, n + 1)
                        for half in range(2):
                            mm = nc.tensor.matmul(acc[:, b % 2, half, 0:HALF], hT[:, b % 2, c, :],
                                                  S[:, n % RING, half * HALF:(half + 1) * HALF],
                                                  start=c == 0, stop=c == CHUNKS - 1)
                        mm.then_inc(S_used, 1)

            @block.scalar
            def _(act):
                def keep(b):
                    act.wait_ge(S_used, (b + 1) * CHUNKS)
                    for half in range(2):
                        nc.scalar.copy(samp[:, half * 8:(half + 1) * 8, b * POS:(b + 1) * POS],
                                       acc[:, b % 2, half, 0:HALF].rearrange("p (k q) -> p k q", k=8)).then_inc(kept, 1)

                def turned_back(b):
                    act.wait_ge(turned, b + 1)
                    if b >= 2:
                        act.wait_ge(S_used, (b - 1) * CHUNKS)
                    nc.scalar.copy(hT[:, b % 2, 0:4, :], psT[:, 0, 0:4 * C1].rearrange("p (c n) -> p c n", c=4)).then_inc(hT_ready, 1)
                    nc.scalar.copy(hT[:, b % 2, 4:7, :], psT[:, 1, 0:3 * C1].rearrange("p (c n) -> p c n", c=3)).then_inc(hT_ready, 1)

                turned_back(0)
                for b in range(IMAGES):
                    act.wait_ge(loaded[b % 2], 16 * (b // 2 + 1))
                    for j in range(PER):
                        n = b * PER + j
                        if n >= 2:
                            act.wait_ge(dist_used, n - 1)
                        axis, col = (1, 7) if j == 0 else (0, j - 1)
                        nc.scalar.activation(dist[:, n % 2, :], pxy[:, b % 2, axis, :], ACT.Abs,
                                             bias=tabs[0:CHUNK, col:col + 1], scale=1.0).then_inc(dist_ready, 1)
                        if j == 3 and b + 1 < IMAGES:
                            turned_back(b + 1)
                        if j == 4 and b >= 1:
                            keep(b - 1)
                keep(IMAGES - 1)

            @block.vector
            def _(dve):
                for b in range(IMAGES):
                    for j in range(PER):
                        n = b * PER + j
                        dve.wait_ge(dist_ready, n + 1)
                        d = dist[:, n % 2, :]
                        dst = xw[:, b % 2, :] if j == 0 else rest[:, :]
                        nc.vector.tensor_scalar(dst, d, -1.0, 1.0, ALU.mult, ALU.add).then_inc(dist_used, 1)
                        dve.wait_ge(dist_used, n + 1)
                        if j == 0:
                            link(dve, xlink, nc.vector.tensor_scalar(dst, dst, 0.0, None, ALU.max))
                        else:
                            m = b * CHUNKS + j - 1
                            if m >= RING:
                                dve.wait_ge(S_used, m - RING + 1)
                            nc.vector.scalar_tensor_tensor(S[:, m % RING, :], rest[:, :], 0.0, xw[:, b % 2, :],
                                                           ALU.max, ALU.mult).then_inc(S_ready, 1)
                            dve.wait_ge(S_ready, m + 1)


def near_sampling_stage(nc, K, W, h, samp, off_dram, hc):
    GROUP = 4
    PART = 2 * TAPS // GROUP
    RING = 6
    near = lambda c: range(max(c - 1, 0), min(c + 2, CHUNKS))
    cols = lambda c: slice(near(c)[0] * OUT_SIDE, (near(c)[-1] + 1) * OUT_SIDE)
    with Stage(nc, "nsm") as s:
        pxy = s.sb("pxy", [CHUNK, 3, 2, TAPS, POS])
        xw = s.sb("xw", [CHUNK, 2, TAPS, POS])
        xdist = s.sb("xdist", [CHUNK, TAPS, POS])
        dist = s.sb("dist", [CHUNK, 4, TAPS, 3 * OUT_SIDE])
        rest = s.sb("rest", [CHUNK, 3, TAPS, 3 * OUT_SIDE])
        S = s.sb("S", [CHUNK, RING, TAPS, 3 * OUT_SIDE])
        hT = s.sb("hT", [CHUNK, 2, CHUNKS, C1])
        psT = s.ps("psT", [CHUNK, 2, BANK])
        acc = s.ps("acc", [C1, 2, 2, BANK])
        psD = s.ps("psD", [C1, 2, BANK])
        tmp = s.sb("tmp", [C1, 2, GROUP * POS])
        row = TAPS * OUT_SIDE
        loaded = [s.sem(f"loaded{i}") for i in range(3)]
        turned, hT_act, hT_dve = s.sem("turned"), s.sem("hT_act"), s.sem("hT_dve")
        xdist_ready, xrest_ready, xw_ready = s.sem("xdist_ready"), s.sem("xrest_ready"), s.sem("xw_ready")
        dist_ready, rest_ready, S_ready, row_done, kept = (
            s.sem(x) for x in ("dist_ready", "rest_ready", "S_ready", "row_done", "kept"))
        mm_ready, scaled, leaky = s.sem("mm_ready"), s.sem("scaled"), s.sem("leaky")
        tabs = W["tabs"]
        with nc.Block() as block:
            @block.sync
            def _(sp):
                for b in range(IMAGES):
                    if b >= 3:
                        sp.wait_ge(dist_ready, (b - 2) * CHUNKS)
                        sp.wait_ge(xdist_ready, b - 2)
                    sp.dma_start(pxy[:, b % 3].rearrange("p a k q -> p (a k q)"),
                                 off_dram[b].rearrange("c p -> (c p)").partition_broadcast(CHUNK)).then_inc(loaded[b % 3], 16)

            @block.tensor
            def _(pe):
                def turn(b):
                    if b >= 1:
                        pe.wait_ge(hT_act, b)
                        pe.wait_ge(hT_dve, b)
                    for c in range(CHUNKS):
                        mm = nc.tensor.transpose(psT[:, c // 4, (c % 4) * C1:(c % 4 + 1) * C1],
                                                 h[:, b, c * CHUNK:(c + 1) * CHUNK], W["ident"][0:C1, 0:C1])
                    mm.then_inc(turned, 1)

                def patch(g, first, last):
                    pe.wait_ge(kept, 2 * GROUP * (g + 1))
                    for n in range(first, last):
                        m, tap = n // TAPS, n % TAPS
                        if tap == 0 and g:
                            pe.wait_ge(scaled, 2 * (g - 1) + m + 1)
                        mm = nc.tensor.matmul(psD[:, m, 0:GROUP * POS], W["dcn_w"][:, tap, m * HD:(m + 1) * HD],
                                              samp[:, tap, g * GROUP * POS:(g + 1) * GROUP * POS], start=tap == 0, stop=tap == TAPS - 1)
                        if tap == TAPS - 1:
                            mm.then_inc(mm_ready, 1)

                for name in ("ident", "dcn_w"):
                    pe.wait_ge(W["sem"][name], 16)
                turn(0)
                for b in range(IMAGES):
                    if b + 1 < IMAGES:
                        turn(b + 1)
                    pe.wait_ge(hT_act, b + 1)
                    pe.wait_ge(hT_dve, b + 1)
                    if b >= 2:
                        pe.wait_ge(kept, 2 * (b - 1))
                    for i in range(OUT_SIDE):
                        pe.wait_ge(S_ready, b * CHUNKS + near(i)[-1] + 1)
                        for c in near(i):
                            q = (i - near(c)[0]) * OUT_SIDE
                            mm = nc.tensor.matmul(acc[:, b % 2, i // 4, (i % 4) * row:(i % 4 + 1) * row], hT[:, b % 2, c, :],
                                                  S[:, (b * CHUNKS + c) % RING, :, q:q + OUT_SIDE],
                                                  start=c == near(i)[0], stop=c == near(i)[-1])
                        mm.then_inc(row_done, 1)
                        if b >= GROUP:
                            n = b % GROUP * PART
                            patch(b // GROUP - 1, n + PART * i // OUT_SIDE, n + PART * (i + 1) // OUT_SIDE)
                patch(IMAGES // GROUP - 1, 0, 2 * TAPS)

            @block.scalar
            def _(act):
                def keep(b, half):
                    rows = 4 - half
                    act.wait_ge(row_done, b * CHUNKS + 4 + 3 * half)
                    nc.scalar.copy(samp[:, :, b * POS + 4 * half * OUT_SIDE:b * POS + (4 * half + rows) * OUT_SIDE].rearrange("p k (i j) -> p i k j", i=rows),
                                   acc[:, b % 2, half, 0:rows * row].rearrange("p (i k j) -> p i k j", i=rows, k=TAPS)).then_inc(kept, 1)

                def turned_back(b):
                    act.wait_ge(turned, b + 1)
                    if b >= 2:
                        act.wait_ge(row_done, (b - 1) * CHUNKS)
                    nc.scalar.copy(hT[:, b % 2, 0:4, :], psT[:, 0, 0:4 * C1].rearrange("p (c n) -> p c n", c=4)).then_inc(hT_act, 1)

                def xpart(b):
                    act.wait_ge(loaded[b % 3], 16 * (b // 3 + 1))
                    if b >= 1:
                        act.wait_ge(xw_ready, b)
                    nc.scalar.activation(xdist[:], pxy[:, b % 3, 1], ACT.Abs, bias=tabs[0:CHUNK, 7:8], scale=1.0).then_inc(xdist_ready, 1)

                turned_back(0)
                xpart(0)
                for b in range(IMAGES):
                    for c in range(CHUNKS):
                        n = b * CHUNKS + c
                        if n >= 4:
                            act.wait_ge(rest_ready, n - 3)
                        w = cols(c)
                        nc.scalar.activation(dist[:, n % 4, :, 0:w.stop - w.start], pxy[:, b % 3, 0, :, w], ACT.Abs,
                                             bias=tabs[0:CHUNK, c:c + 1], scale=1.0).then_inc(dist_ready, 1)
                        if c == 1 and b + 1 < IMAGES:
                            xpart(b + 1)
                        if c == 5 and b + 1 < IMAGES:
                            turned_back(b + 1)
                        if c == 5 and b >= 1:
                            keep(b - 1, 0)
                        if c == 6 and b >= 1:
                            keep(b - 1, 1)
                keep(IMAGES - 1, 0)
                keep(IMAGES - 1, 1)

            @block.gpsimd
            def _(pool):
                for b in range(IMAGES):
                    pool.wait_ge(xdist_ready, b + 1)
                    if b >= 2:
                        pool.wait_ge(S_ready, (b - 1) * CHUNKS)
                    nc.gpsimd.tensor_scalar(xw[:, b % 2], xdist[:], -1.0, 1.0, ALU.mult, ALU.add).then_inc(xrest_ready, 1)
                    pool.wait_ge(xrest_ready, b + 1)
                    nc.gpsimd.tensor_scalar(xw[:, b % 2], xw[:, b % 2], 0.0, None, ALU.max).then_inc(xw_ready, 1)

            @block.vector
            def _(dve):
                def turned_back(b):
                    dve.wait_ge(turned, b + 1)
                    if b >= 2:
                        dve.wait_ge(row_done, (b - 1) * CHUNKS)
                    nc.vector.tensor_copy(hT[:, b % 2, 4:7, :], psT[:, 1, 0:3 * C1].rearrange("p (c n) -> p c n", c=3)).then_inc(hT_dve, 1)

                def remainder(n):
                    c = n % CHUNKS
                    w = cols(c).stop - cols(c).start
                    dve.wait_ge(dist_ready, n + 1)
                    if n >= 3:
                        dve.wait_ge(S_ready, n - 2)
                    nc.vector.tensor_scalar(rest[:, n % 3, :, 0:w], dist[:, n % 4, :, 0:w], -1.0, 1.0, ALU.mult, ALU.add).then_inc(rest_ready, 1)

                def activate(j):
                    g, m = j // 2, j % 2
                    dve.wait_ge(mm_ready, j + 1)
                    nc.vector.tensor_scalar(tmp[:, m, :], psD[:, m, 0:GROUP * POS], W["bnv"][:, 1, 1 + m:2 + m], W["bnv"][:, 2, 1 + m:2 + m],
                                            ALU.mult, ALU.add).then_inc(scaled, 1)
                    dve.wait_ge(scaled, j + 1)
                    v = tmp[:, m, :].rearrange("p (b q) -> p b q", b=GROUP)
                    nc.vector.scalar_tensor_tensor(hc[:, m, g * GROUP:(g + 1) * GROUP, 1:SEQ], v, 0.01, v, ALU.mult, ALU.max).then_inc(leaky, 1)
                    dve.wait_ge(leaky, j + 1)

                turned_back(0)
                remainder(0)
                remainder(1)
                for n in range(IMAGES * CHUNKS):
                    b, c = n // CHUNKS, n % CHUNKS
                    if n + 2 < IMAGES * CHUNKS:
                        remainder(n + 2)
                    if c == 0:
                        dve.wait_ge(xw_ready, b + 1)
                    if n >= RING:
                        dve.wait_ge(row_done, min(n - RING + 1, (n - RING) // CHUNKS * CHUNKS + CHUNKS - 1) + 1)
                    dve.wait_ge(rest_ready, n + 1)
                    w = cols(c)
                    nc.vector.scalar_tensor_tensor(S[:, n % RING, :, 0:w.stop - w.start], rest[:, n % 3, :, 0:w.stop - w.start], 0.0,
                                                   xw[:, b % 2, :, w], ALU.max, ALU.mult).then_inc(S_ready, 1)
                    if c == 4 and b + 1 < IMAGES:
                        turned_back(b + 1)
                    if c == 5 and b > GROUP and b % 2 == 0:
                        activate(b // 2 - GROUP // 2 - 1)
                for j in range((IMAGES - GROUP) // 2 - 1, 2 * IMAGES // GROUP):
                    activate(j)


def patch_stage(nc, K, W, samp, hc):
    with Stage(nc, "dcn") as s:
        tmp = s.sb("tmp", [C1, 4, HALF])
        ps = s.ps("ps", [C1, 4, BANK])
        mm_ready, scaled, leaky = s.sem("mm_ready"), s.sem("scaled"), s.sem("leaky")
        with nc.Block() as block:
            @block.tensor
            def _(pe):
                pe.wait_ge(W["sem"]["dcn_w"], 16)
                for n in range(4):
                    half, m = n // 2, n % 2
                    for tap in range(TAPS):
                        mm = nc.tensor.matmul(ps[:, n, 0:HALF], W["dcn_w"][:, tap, m * HD:(m + 1) * HD],
                                              samp[:, tap, half * HALF:(half + 1) * HALF],
                                              start=tap == 0, stop=tap == TAPS - 1)
                    mm.then_inc(mm_ready, 1)

            @block.scalar
            def _(act):
                for n in range(4):
                    act.wait_ge(mm_ready, n + 1)
                    m = n % 2
                    nc.scalar.activation(tmp[:, n, :], ps[:, n, 0:HALF], ACT.Identity,
                                         bias=W["bnv"][:, 2, 1 + m:2 + m], scale=W["bnv"][:, 1, 1 + m:2 + m]).then_inc(scaled, 1)

            @block.vector
            def _(dve):
                for n in range(4):
                    half, m = n // 2, n % 2
                    dve.wait_ge(scaled, n + 1)
                    t = tmp[:, n, :].rearrange("p (b q) -> p b q", b=8)
                    nc.vector.scalar_tensor_tensor(hc[:, m, half * 8:(half + 1) * 8, 1:SEQ], t, 0.01, t,
                                                   ALU.mult, ALU.max).then_inc(leaky, 1)


def token_stage(nc, W, hc, H):
    with Stage(nc, "tok") as s:
        psT = s.ps("psT", [PAIR, 4, BANK])
        cls, turned, kept, kept_v = s.sem("cls"), s.sem("turned"), s.sem("kept"), s.sem("kept_v")
        with nc.Block() as block:
            @block.tensor
            def _(pe):
                pe.wait_ge(W["sem"]["ident"], 16)
                pe.wait_ge(cls, 1)
                for t in range(TILES):
                    for m in range(2):
                        mm = nc.tensor.transpose(psT[:, t // 2, (t % 2) * D + m * HD:(t % 2) * D + (m + 1) * HD],
                                                 hc[:, m, 2 * t:2 * t + 2, :].rearrange("p b q -> p (b q)"), W["ident"][0:HD, 0:HD])
                    mm.then_inc(turned, 1)

            @block.scalar
            def _(act):
                for j in (0, 2):
                    act.wait_ge(turned, 2 * j + 2)
                    nc.scalar.copy(H[:, 2 * j:2 * j + 2, :], psT[:, j, 0:2 * D].rearrange("p (t d) -> p t d", t=2)).then_inc(kept, 1)

            @block.vector
            def _(dve):
                dve.wait_ge(W["sem"]["chan"], 16)
                nc.vector.tensor_copy(hc[:, :, :, 0], bcast(W["chan"][:, 5, 0:2], 2, IMAGES)).then_inc(cls, 1)
                for j in (1, 3):
                    dve.wait_ge(turned, 2 * j + 2)
                    nc.vector.tensor_copy(H[:, 2 * j:2 * j + 2, :], psT[:, j, 0:2 * D].rearrange("p (t d) -> p t d", t=2)).then_inc(kept_v, 1)


def channels_stage(nc, W, name, src, dst):
    width, n = dst.shape[0], dst.shape[1]
    with Stage(nc, name) as s:
        ps = s.ps("ps", [width, 8, BANK])
        turned, kept_a, kept_v = s.sem("turned"), s.sem("kept_a"), s.sem("kept_v")
        groups = [(m, g) for g in range(2) for m in range(n)]
        with nc.Block() as block:
            @block.tensor
            def _(pe):
                for j, (m, g) in enumerate(groups):
                    for t in range(4):
                        mm = nc.tensor.transpose(ps[:, j, t * PAIR:(t + 1) * PAIR],
                                                 src[:, 4 * g + t, m * width:(m + 1) * width], W["ident"][0:PAIR, 0:PAIR])
                    mm.then_inc(turned, 1)

            @block.scalar
            def _(act):
                for j, (m, g) in enumerate(groups):
                    if j % 2 == 0:
                        act.wait_ge(turned, j + 1)
                        nc.scalar.copy(dst[:, m, g * HALF_TOK:(g + 1) * HALF_TOK], ps[:, j, 0:HALF_TOK]).then_inc(kept_a, 1)

            @block.vector
            def _(dve):
                for j, (m, g) in enumerate(groups):
                    if j % 2:
                        dve.wait_ge(turned, j + 1)
                        nc.vector.tensor_copy(dst[:, m, g * HALF_TOK:(g + 1) * HALF_TOK], ps[:, j, 0:HALF_TOK]).then_inc(kept_v, 1)


def norm_stage(nc, W, name, src, dst, eps, rms=False, gain=None, shift=None):
    with Stage(nc, name) as s:
        stat = s.sb("stat", [PAIR, TILES, 6])
        mv = s.sb("mv", [PAIR, TILES, 2])
        sq = s.sb("sq", [PAIR, TILES])
        rstd = s.sb("rstd", [PAIR, TILES])
        vec = Step(s.sem("vec"))
        var_ready, rstd_ready = s.sem("var_ready"), s.sem("rstd_ready")
        with nc.Block() as block:
            @block.vector
            def _(dve):
                for t in range(TILES):
                    vec.add(nc.vector.bn_stats(stat[:, t, :], src[:, t, :]))
                dve.wait_ge(vec.sem, vec.n)
                for t in range(TILES):
                    vec.add(nc.vector.bn_aggr(mv[:, t, :], stat[:, t, :]))
                dve.wait_ge(vec.sem, vec.n)
                if rms:
                    link(dve, vec, nc.vector.tensor_tensor(sq[:], mv[:, :, 0], mv[:, :, 0], ALU.mult))
                    link(dve, vec, nc.vector.tensor_tensor(sq[:], sq[:], mv[:, :, 1], ALU.add))
                    nc.vector.tensor_scalar(sq[:], sq[:], eps, None, ALU.add).then_inc(var_ready, 1)
                else:
                    nc.vector.tensor_scalar(sq[:], mv[:, :, 1], eps, None, ALU.add).then_inc(var_ready, 1)
                dve.wait_ge(rstd_ready, 1)
                for t in range(TILES):
                    if rms:
                        vec.add(nc.vector.tensor_scalar(dst[:, t, :], src[:, t, :], rstd[:, t:t + 1], None, ALU.mult))
                    else:
                        vec.add(nc.vector.tensor_scalar(dst[:, t, :], src[:, t, :], mv[:, t, 0:1], rstd[:, t:t + 1],
                                                        ALU.subtract, ALU.mult))
                for v, op in ((gain, ALU.mult), (shift, ALU.add)):
                    if v is not None:
                        dve.wait_ge(vec.sem, vec.n)
                        vec.add(nc.vector.tensor_tensor(dst[:], dst[:], bcast(v, 1, TILES), op))

            @block.gpsimd
            def _(pool):
                pool.wait_ge(var_ready, 1)
                nc.gpsimd.tensor_tensor(rstd[:], sq[:], W["mhalf"][0:PAIR, 0:TILES], ALU.pow).then_inc(rstd_ready, 1)


def global_norm_stage(nc, W, name, src, dst, gain, shift, add_to=None):
    N = TOK * D
    with Stage(nc, name) as s:
        stat = s.sb("stat", [PAIR, TILES, 6])
        mv = s.sb("mv", [PAIR, 2])
        m = s.sb("m", [PAIR, 4])
        ps = s.ps("ps", [PAIR, 2, BANK])
        vec = Step(s.sem("vec"))
        mean_in, mean_out, var_in, var_out = (s.sem(x) for x in ("mean_in", "mean_out", "var_in", "var_out"))
        sq_ready, rstd_ready = s.sem("sq_ready"), s.sem("rstd_ready")
        with nc.Block() as block:
            @block.tensor
            def _(pe):
                pe.wait_ge(mean_in, 1)
                nc.tensor.matmul(ps[:, 0, 0:1], W["ones"][0:PAIR, 0:PAIR], mv[:, 0:1], start=True, stop=True).then_inc(mean_out, 1)
                pe.wait_ge(var_in, 1)
                nc.tensor.matmul(ps[:, 1, 0:1], W["ones"][0:PAIR, 0:PAIR], m[:, 2:3], start=True, stop=True).then_inc(var_out, 1)

            @block.gpsimd
            def _(pool):
                pool.wait_ge(sq_ready, 1)
                nc.gpsimd.tensor_tensor(m[:, 3:4], m[:, 1:2], W["mhalf"][0:PAIR, 0:1], ALU.pow).then_inc(rstd_ready, 1)

            @block.vector
            def _(dve):
                for t in range(TILES):
                    vec.add(nc.vector.bn_stats(stat[:, t, :], src[:, t, :]))
                dve.wait_ge(vec.sem, vec.n)
                nc.vector.bn_aggr(mv[:], stat[:].rearrange("p t c -> p (t c)")).then_inc(mean_in, 1)
                dve.wait_ge(mean_out, 1)
                link(dve, vec, nc.vector.tensor_scalar(m[:, 0:1], ps[:, 0, 0:1], 1.0 / PAIR, None, ALU.mult))
                link(dve, vec, nc.vector.tensor_tensor(m[:, 1:2], mv[:, 0:1], m[:, 0:1], ALU.subtract))
                link(dve, vec, nc.vector.tensor_tensor(m[:, 1:2], m[:, 1:2], m[:, 1:2], ALU.mult))
                nc.vector.tensor_tensor(m[:, 2:3], mv[:, 1:2], m[:, 1:2], ALU.add).then_inc(var_in, 1)
                dve.wait_ge(var_out, 1)
                nc.vector.tensor_scalar(m[:, 1:2], ps[:, 1, 0:1], N / (N - 1.0) / PAIR, 1e-12, ALU.mult, ALU.add).then_inc(sq_ready, 1)
                dve.wait_ge(rstd_ready, 1)
                for t in range(TILES):
                    vec.add(nc.vector.tensor_scalar(dst[:, t, :], src[:, t, :], m[:, 0:1], m[:, 3:4], ALU.subtract, ALU.mult))
                dve.wait_ge(vec.sem, vec.n)
                link(dve, vec, nc.vector.tensor_tensor(dst[:], dst[:], bcast(gain, 1, TILES), ALU.mult))
                link(dve, vec, nc.vector.tensor_tensor(dst[:], dst[:], bcast(shift, 1, TILES), ALU.add))
                if add_to is not None:
                    link(dve, vec, nc.vector.tensor_tensor(add_to[:], add_to[:], dst[:], ALU.add))


def product_stage(nc, W, name, products, weights, add=False, on_pool=None):
    with Stage(nc, name) as s:
        ps = s.ps("ps", [128, 8, BANK])
        ready, kept_a, kept_v = s.sem("ready"), s.sem("kept_a"), s.sem("kept_v")

        def bank(j, dst, row):
            free = dst.shape[1:]
            v = ps[row:row + dst.shape[0], j % 8, 0:int(np.prod(free))]
            return v if len(free) == 1 else v.rearrange("p (a b) -> p a b", a=free[0])

        def by_act(j):
            return j % 2 == 0 and not add

        with nc.Block() as block:
            if on_pool is not None:
                block.gpsimd(on_pool)

            @block.tensor
            def _(pe):
                for w in weights:
                    pe.wait_ge(W["sem"][w], 16)
                for j, (results, terms) in enumerate(products):
                    if j >= 8 and by_act(j):
                        pe.wait_ge(kept_a, (j - 8) // 2 + 1)
                    elif j >= 8:
                        pe.wait_ge(kept_v, j - 7 if add else (j - 8) // 2 + 1)
                    lo = min(row for _, row, _ in results)
                    for i, (lhsT, rhs) in enumerate(terms):
                        m, n = int(np.prod(lhsT.shape[1:])), int(np.prod(rhs.shape[1:]))
                        mm = nc.tensor.matmul(ps[lo:lo + m, j % 8, 0:n], lhsT, rhs, start=i == 0, stop=i == len(terms) - 1)
                    mm.then_inc(ready, 1)

            @block.scalar
            def _(act):
                for j, (results, _) in enumerate(products):
                    if by_act(j):
                        act.wait_ge(ready, j + 1)
                        for dst, row, bias in results:
                            if bias is None:
                                last = nc.scalar.copy(dst, bank(j, dst, row))
                            else:
                                last = nc.scalar.activation(dst, bank(j, dst, row), ACT.Identity, bias=bias, scale=1.0)
                        last.then_inc(kept_a, 1)

            @block.vector
            def _(dve):
                for j, (results, _) in enumerate(products):
                    if not by_act(j):
                        dve.wait_ge(ready, j + 1)
                        for dst, row, bias in results:
                            if add:
                                last = nc.vector.tensor_tensor(dst, bank(j, dst, row), dst, ALU.add)
                            elif bias is None:
                                last = nc.vector.tensor_copy(dst, bank(j, dst, row))
                            else:
                                last = nc.vector.tensor_scalar(dst, bank(j, dst, row), bias, None, ALU.add)
                        last.then_inc(kept_v, 1)


def attention_core(nc, W, QT, KT, V, zT):
    G, AHEAD, BUF = 3, 2, 4
    with Stage(nc, "att") as s:
        sc = s.sb("sc", [PAIR, BUF, HEADS, PAIR])
        pt = s.sb("pt", [PAIR, 2, HEADS, PAIR])
        mx = s.sb("mx", [PAIR, BUF, HEADS])
        sm = s.sb("sm", [PAIR, BUF, HEADS])
        psS = s.ps("psS", [PAIR, G, BANK])
        psP = s.ps("psP", [PAIR, G, BANK])
        psZ = s.ps("psZ", [128, 2, BANK])
        scores, masked, vec, shifted = s.sem("scores"), s.sem("masked"), Step(s.sem("vec")), s.sem("shifted")
        exps, rec, probs, turned, pt_ready = (s.sem(x) for x in ("exps", "rec", "probs", "turned", "pt_ready"))
        z_ready, z_kept = s.sem("z_ready"), s.sem("z_kept")

        def staged(first, later):
            for t in range(TILES + AHEAD):
                if t < TILES:
                    first(t)
                if t >= AHEAD:
                    later(t - AHEAD)

        with nc.Block() as block:
            @block.tensor
            def _(pe):
                def score(t):
                    for g in range(G):
                        if t >= 1:
                            pe.wait_ge(masked, G * (t - 1) + g + 1)
                        for i in range(4):
                            hd = 4 * g + i
                            mm = nc.tensor.matmul(psS[:, g, i * PAIR:(i + 1) * PAIR], QT[:, hd // 2, tokens(t)],
                                                  KT[:, hd, tokens(t)], start=True, stop=True)
                        mm.then_inc(scores, 1)

                def finish(t):
                    pe.wait_ge(probs, t + 1)
                    for g in range(G):
                        if t >= 1:
                            pe.wait_ge(pt_ready, G * (t - 1) + g + 1)
                        for i in range(4):
                            mm = nc.tensor.transpose(psP[:, g, i * PAIR:(i + 1) * PAIR], sc[:, t % BUF, 4 * g + i, :],
                                                     W["ident"][0:PAIR, 0:PAIR])
                        mm.then_inc(turned, 1)
                    if t >= 1:
                        pe.wait_ge(z_kept, 2 * t)
                    for hd in range(HEADS):
                        if hd % 4 == 0:
                            pe.wait_ge(pt_ready, G * t + hd // 4 + 1)
                        r, pr = 64 * (hd % 2), hd // 2
                        mm = nc.tensor.matmul(psZ[r:r + 64, pr // 3, (pr % 3) * PAIR:(pr % 3 + 1) * PAIR],
                                              V[:, t, hd * DH:(hd + 1) * DH], pt[:, t % 2, hd, :], start=True, stop=True)
                    mm.then_inc(z_ready, 1)

                staged(score, finish)

            @block.vector
            def _(dve):
                def open_(t):
                    b = t % BUF
                    for g in range(G):
                        dve.wait_ge(scores, G * t + g + 1)
                        if t >= BUF:
                            dve.wait_ge(turned, G * (t - BUF + 1))
                        nc.vector.tensor_tensor(sc[:, b, 4 * g:4 * g + 4, :],
                                                psS[:, g, 0:4 * PAIR].rearrange("p (h k) -> p h k", h=4),
                                                bcast(W["amask"][:], 1, 4), ALU.add).then_inc(masked, 1)
                    dve.wait_ge(masked, G * (t + 1))
                    link(dve, vec, nc.vector.tensor_reduce(mx[:, b, :], sc[:, b, :, :], AX.X, ALU.max))
                    nc.vector.tensor_tensor(sc[:, b, :, :], sc[:, b, :, :], bcast(mx[:, b, :], 2, PAIR),
                                            ALU.subtract).then_inc(shifted, 1)

                def sums(t):
                    b = t % BUF
                    dve.wait_ge(exps, t + 1)
                    link(dve, vec, nc.vector.tensor_reduce(sm[:, b, :], sc[:, b, :, :], AX.X, ALU.add))
                    nc.vector.reciprocal(sm[:, b, :], sm[:, b, :]).then_inc(rec, 1)

                def keep(t):
                    dve.wait_ge(z_ready, t + 1)
                    for j in range(2):
                        nc.vector.tensor_tensor(zT[:, 3 * j:3 * j + 3, tokens(t)],
                                                psZ[:, j, 0:3 * PAIR].rearrange("p (h q) -> p h q", h=3),
                                                bcast(W["qkvb"][:, 2, 3 * j:3 * j + 3], 2, PAIR), ALU.add).then_inc(z_kept, 1)

                dve.wait_ge(W["sem"]["amask"], 16)
                for t in range(TILES + AHEAD + 1):
                    if t < TILES:
                        open_(t)
                    if 1 <= t <= TILES:
                        sums(t - 1)
                    if t > AHEAD:
                        keep(t - AHEAD - 1)

            @block.gpsimd
            def _(pool):
                for t in range(TILES):
                    pool.wait_ge(rec, t + 1)
                    b = t % BUF
                    nc.gpsimd.tensor_tensor(sc[:, b, :, :], sc[:, b, :, :], bcast(sm[:, b, :], 2, PAIR),
                                            ALU.mult).then_inc(probs, 1)

            @block.scalar
            def _(act):
                def exp(t):
                    act.wait_ge(shifted, t + 1)
                    nc.scalar.activation(sc[:, t % BUF, :, :], sc[:, t % BUF, :, :], ACT.Exp, scale=DH ** -0.5).then_inc(exps, 1)

                def keep(t):
                    for g in range(G):
                        act.wait_ge(turned, G * t + g + 1)
                        if t >= 2:
                            act.wait_ge(z_ready, t - 1)
                        nc.scalar.copy(pt[:, t % 2, 4 * g:4 * g + 4, :],
                                       psP[:, g, 0:4 * PAIR].rearrange("p (h k) -> p h k", h=4)).then_inc(pt_ready, 1)

                staged(exp, keep)


def tokens(t):
    return slice(t * PAIR, (t + 1) * PAIR)


def attention_layer(nc, W, H):
    with Stage(nc, "at") as s:
        xn = s.sb("xn", [PAIR, TILES, D])
        xT = s.sb("xT", [HD, 2, TOK])
        QT = s.sb("QT", [128, 6, TOK])
        KT = s.sb("KT", [128, HEADS, TOK])
        zeroed = s.sem("zeroed")
        V = s.sb("V", [PAIR, TILES, HEADS * DH])
        zT = s.sb("zT", [128, 6, TOK])

        def zero_other_heads(pool):
            for hd in range(HEADS):
                r = 64 * (1 - hd % 2)
                nc.gpsimd.memset(KT[r:r + 64, hd, :], 0.0).then_inc(zeroed, 1)
            pool.wait_ge(zeroed, HEADS)

        norm_stage(nc, W, "at_n", H, xn, 1e-5)
        channels_stage(nc, W, "at_c", xn, xT)
        prods = []
        for m in range(6):
            for g in range(2):
                c = slice(g * HALF_TOK, (g + 1) * HALF_TOK)
                w = slice(m * 128, (m + 1) * 128)
                prods.append(([(QT[:, m, c], 0, W["qkvb"][:, 0, m:m + 1])], [(W["wq"][:, k, w], xT[:, k, c]) for k in range(2)]))
                prods.append(([(KT[r:r + 64, 2 * m + r // 64, c], r, W["qkvb"][r:r + 64, 1, m:m + 1]) for r in (0, 64)],
                              [(W["wk"][:, k, w], xT[:, k, c]) for k in range(2)]))
        for t in range(TILES):
            for g in range(2):
                c = slice(g * D_IN, (g + 1) * D_IN)
                prods.append(([(V[:, t, c], 0, None)], [(xT[:, k, tokens(t)], W["wv"][:, k, c]) for k in range(2)]))
        product_stage(nc, W, "at_p", prods, ["wq", "wk", "wv", "qkvb"], on_pool=zero_other_heads)
        attention_core(nc, W, QT, KT, V, zT)
        prods = [([(H[:, t, :], 0, None)], [(zT[:, p, tokens(t)], W["wo"][:, p, :]) for p in range(6)]
                  + [(W["ones"][0:1, 0:PAIR], W["rowb"][0:1, 0, :])]) for t in range(TILES)]
        product_stage(nc, W, "at_o", prods, ["wo", "rowb"], add=True)


def channel_attention(nc, W, xT, X, a_dram, Y, YT):
    with Stage(nc, "ca") as s:
        QK = s.sb("QK", [128, TILES, 2 * D])
        VT = s.sb("VT", [HD, 2, TOK])
        sc = s.sb("sc", [HD, 2 * IMAGES, HD])
        wT = s.sb("wT", [HD, 2 * IMAGES, HD])
        mx = s.sb("mx", [HD, 2 * IMAGES])
        A = s.sb("A", [HD, 2, IMAGES, SEQ])
        prods = []
        for t in range(TILES):
            for o in range(2):
                c = slice((2 * t + o) * SEQ, (2 * t + o + 1) * SEQ)
                prods.append(([(QK[64 * o:64 * o + SEQ, t, :], 64 * o, None)],
                              [(xT[:, 0, c], W["w1"][:, 0, 0:2 * D]), (xT[0:HD, 1, c], W["w1"][0:HD, 1, 0:2 * D])]))
        for m in range(2):
            for g in range(2):
                c = slice(g * HALF_TOK, (g + 1) * HALF_TOK)
                v = slice(2 * D + m * HD, 2 * D + (m + 1) * HD)
                prods.append(([(VT[:, m, c], 0, None)],
                              [(W["w1"][:, 0, v], xT[:, 0, c]), (W["w1"][0:HD, 1, v], xT[0:HD, 1, c])]))
        product_stage(nc, W, "ca_p", prods, ["w1"])
        with Stage(nc, "cb") as p:
            ps = p.ps("ps", [HD, 8, BANK])
            scores, masked, vec = s.sem("scores"), s.sem("masked"), Step(s.sem("vec"))
            shifted, exps, probs, turned, wT_ready, a_ready, a_kept, a_out, a_in = (
                s.sem(x) for x in ("shifted", "exps", "probs", "turned", "wT_ready", "a_ready", "a_kept", "a_out", "a_in"))

            def place(b, half):
                return 4 * (2 * (b // 4) + b % 2) + 2 * (b % 4 // 2) + half

            def four(j):
                return ps[:, j, 0:4 * HD].rearrange("p (h k) -> p h k", h=4)

            with nc.Block() as block:
                @block.tensor
                def _(pe):
                    for j in range(8):
                        for i in range(4):
                            b, c = 4 * (j // 2) + j % 2 + 2 * (i // 2), (i % 2) * HD
                            r = slice(64 * (b % 2), 64 * (b % 2) + SEQ)
                            mm = nc.tensor.matmul(ps[:, j, i * HD:(i + 1) * HD], QK[r, b // 2, c:c + HD],
                                                  QK[r, b // 2, D + c:D + c + HD], start=True, stop=True)
                        mm.then_inc(scores, 1)
                    pe.wait_ge(probs, 1)
                    for j in range(8):
                        for i in range(4):
                            mm = nc.tensor.transpose(ps[:, j, i * HD:(i + 1) * HD], sc[:, 4 * j + i, :], W["ident"][0:HD, 0:HD])
                        mm.then_inc(turned, 1)
                    pe.wait_ge(wT_ready, 8)
                    for j in range(4):
                        half, b0 = j // 2, 8 * (j % 2)
                        for b in range(b0, b0 + 8):
                            mm = nc.tensor.matmul(ps[:, j, (b - b0) * SEQ:(b - b0 + 1) * SEQ], wT[:, place(b, half), :],
                                                  VT[:, half, b * SEQ:(b + 1) * SEQ], start=True, stop=True)
                        mm.then_inc(a_ready, 1)

                @block.vector
                def _(dve):
                    dve.wait_ge(W["sem"]["cmask"], 16)
                    for j in range(8):
                        dve.wait_ge(scores, j + 1)
                        nc.vector.tensor_tensor(sc[:, 4 * j:4 * j + 4, :], four(j), bcast(W["cmask"][:], 1, 4), ALU.add).then_inc(masked, 1)
                    dve.wait_ge(masked, 8)
                    link(dve, vec, nc.vector.tensor_reduce(mx[:], sc[:], AX.X, ALU.max))
                    nc.vector.tensor_tensor(sc[:], sc[:], bcast(mx[:], 2, HD), ALU.subtract).then_inc(shifted, 1)
                    dve.wait_ge(exps, 1)
                    link(dve, vec, nc.vector.tensor_reduce(mx[:], sc[:], AX.X, ALU.add))
                    link(dve, vec, nc.vector.reciprocal(mx[:], mx[:]))
                    nc.vector.tensor_tensor(sc[:], sc[:], bcast(mx[:], 2, HD), ALU.mult).then_inc(probs, 1)
                    for j in range(4):
                        dve.wait_ge(a_ready, j + 1)
                        half, b0 = j // 2, 8 * (j % 2)
                        nc.vector.tensor_copy(A[:, half, b0:b0 + 8, :],
                                              ps[:, j, 0:8 * SEQ].rearrange("p (b q) -> p b q", b=8)).then_inc(a_kept, 1)

                @block.scalar
                def _(act):
                    act.wait_ge(shifted, 1)
                    nc.scalar.activation(sc[:], sc[:], ACT.Exp, scale=float(SEQ) ** -0.5).then_inc(exps, 1)
                    for j in range(8):
                        act.wait_ge(turned, j + 1)
                        nc.scalar.copy(wT[:, 4 * j:4 * j + 4, :], four(j)).then_inc(wT_ready, 1)

                @block.sync
                def _(sp):
                    sp.wait_ge(a_kept, 4)
                    for half in range(2):
                        sp.dma_start(a_dram.rearrange("b (h c) q -> h c b q", h=2)[half], A[:, half, :, :]).then_inc(a_out, 16)
                    sp.wait_ge(a_out, 32)
                    sp.dma_start(Y[:], a_dram.rearrange("b c q -> (b c q)").rearrange("(t p d) -> p t d", p=PAIR, d=D)).then_inc(a_in, 16)
                    sp.wait_ge(a_in, 16)
    channels_stage(nc, W, "cc", Y, YT)
    prods = [([(X[:, t, :], 0, None)], [(YT[:, k, tokens(t)], W["w2"][:, k, :]) for k in range(2)]
              + [(W["ones"][0:1, 0:PAIR], W["rowb"][0:1, 1, :])]) for t in range(TILES)]
    product_stage(nc, W, "cd", prods, ["w2", "rowb"], add=True)


def routing_stage(nc, W, name, E, ranks, NT, usual, xT, wr, wr_name, by_image, x, rows, slot, tile_expert):
    TE = TILES * E
    MAXM = (TOK + SLOT - 1) // SLOT
    with Stage(nc, name) as s:
        lg = s.sb("lg", [PAIR, TILES, E])
        lr = s.sb("lr", [PAIR, TILES, E])
        ex = s.sb("ex", [PAIR, TILES, E])
        key = s.sb("key", [PAIR, TILES, E])
        oh = s.sb("oh", [PAIR, 2, TILES, E])
        both = s.sb("both", [PAIR, TILES, E])
        st = s.sb("st", [PAIR, 6, TILES])
        cnt = s.sb("cnt", [PAIR, E, MAXM])
        ne = s.sb("ne", [PAIR, 4, E])
        zero = s.sb("zero", [PAIR, E])
        place = s.sb("place", [PAIR, TILES, E])
        slotf = s.sb("slotf", [PAIR, TILES, 2])
        te = s.sb("te", [1, NT, E])
        tef = s.sb("tef", [1, NT])
        psL = s.ps("psL", [PAIR, BANK])
        psM = s.ps("psM", [PAIR, BANK])
        psP = s.ps("psP", [PAIR, BANK])
        psN = s.ps("psN", [PAIR, BANK])
        logits, raw_kept, mean_ready, shifted, exps = (s.sem(x) for x in ("logits", "raw_kept", "mean_ready", "shifted", "exps"))
        chosen, counted, slots_ready, copied = (s.sem(x) for x in ("chosen", "counted", "slots_ready", "copied"))
        vec = Step(s.sem("vec"))
        with nc.Block() as block:
            @block.tensor
            def _(pe):
                for n in (wr_name, "imean", "before"):
                    pe.wait_ge(W["sem"][n], 16)
                for t in range(TILES):
                    for k in range(2):
                        mm = nc.tensor.matmul(psL[:, t * E:(t + 1) * E], xT[0:HD, k, tokens(t)], wr[:, k, :],
                                              start=k == 0, stop=k == 1)
                mm.then_inc(logits, 1)
                if by_image:
                    pe.wait_ge(raw_kept, 1)
                    nc.tensor.matmul(psM[:, 0:TE], W["imean"][:], lr[:].rearrange("p t e -> p (t e)"),
                                     start=True, stop=True).then_inc(mean_ready, 1)
                pe.wait_ge(chosen, 1)
                pb = psP[:, 0:TE].rearrange("p (t e) -> p t e", t=TILES)
                nc.tensor.matmul(psP[:, 0:TE], W["before"][:], both[:].rearrange("p t e -> p (t e)"), start=True, stop=False)
                for t in range(TILES - 1):
                    nc.tensor.matmul(pb[:, t + 1:TILES, :], W["ones"][0:PAIR, 0:PAIR], bcast(both[:, t, :], 1, TILES - 1 - t),
                                     start=False, stop=t == TILES - 2)
                for t in range(TILES):
                    mm = nc.tensor.matmul(psN[:, 0:E], W["ones"][0:PAIR, 0:PAIR], both[:, t, :], start=t == 0, stop=t == TILES - 1)
                mm.then_inc(counted, 1)

            @block.scalar
            def _(act):
                act.wait_ge(W["sem"]["iota"], 16)
                for k in range(ranks):
                    nc.scalar.copy(rows[:, :, k, 0:D], x[:]).then_inc(copied, 1)
                    nc.scalar.activation(rows[:, :, k, D], W["iota"][0:PAIR, 80:80 + TILES], ACT.Identity,
                                         bias=W["iota"][0:PAIR, 80 + TILES + k:81 + TILES + k], scale=float(ranks)).then_inc(copied, 1)
                act.wait_ge(shifted, 1)
                nc.scalar.activation(ex[:], lg[:], ACT.Exp, scale=1.0).then_inc(exps, 1)

            @block.vector
            def _(dve):
                def do(ins):
                    link(dve, vec, ins)

                v3 = lambda p: p[:, 0:TE].rearrange("p (t e) -> p t e", t=TILES)
                dve.wait_ge(W["sem"]["iota"], 16)
                dve.wait_ge(logits, 1)
                if by_image:
                    nc.vector.tensor_copy(lr[:], v3(psL)).then_inc(raw_kept, 1)
                    dve.wait_ge(W["sem"]["colb"], 16)
                    dve.wait_ge(mean_ready, 1)
                    do(nc.vector.tensor_tensor(lr[:], v3(psM), bcast(W["colb"][:, 0:E], 1, TILES), ALU.add))
                else:
                    do(nc.vector.tensor_copy(lr[:], v3(psL)))
                do(nc.vector.tensor_reduce(st[:, 0, :], lr[:], AX.X, ALU.max))
                nc.vector.tensor_tensor(lg[:], lr[:], bcast(st[:, 0, :], 2, E), ALU.subtract).then_inc(shifted, 1)
                dve.wait_ge(exps, 1)
                do(nc.vector.tensor_reduce(st[:, 1, :], ex[:], AX.X, ALU.add))
                do(nc.vector.reciprocal(st[:, 2, :], st[:, 1, :]))
                iota = bcast(W["iota"][0:PAIR, 0:E], 1, TILES)
                do(nc.vector.memset(zero[:], 0.0))
                for r in range(ranks):
                    if r:
                        do(nc.vector.tensor_reduce(st[:, 0, :], lr[:], AX.X, ALU.max))
                    do(nc.vector.tensor_tensor(key[:], lr[:], bcast(st[:, 0, :], 2, E), ALU.is_lt))
                    do(nc.vector.scalar_tensor_tensor(key[:], key[:], 1000.0, iota, ALU.mult, ALU.add))
                    do(nc.vector.tensor_reduce(st[:, 3, :], key[:], AX.X, ALU.min))
                    do(nc.vector.tensor_tensor(oh[:, r, :, :], iota, bcast(st[:, 3, :], 2, E), ALU.is_equal))
                    do(nc.vector.tensor_tensor(key[:], oh[:, r, :, :], ex[:], ALU.mult))
                    do(nc.vector.tensor_reduce(st[:, 4, :], key[:], AX.X, ALU.add))
                    do(nc.vector.tensor_tensor(rows[:, :, r, D + 1], st[:, 4, :], st[:, 2, :], ALU.mult))
                    if r + 1 < ranks:
                        do(nc.vector.scalar_tensor_tensor(lr[:], oh[:, r, :, :], NEG, lr[:], ALU.mult, ALU.add))
                if ranks == 2:
                    nc.vector.tensor_tensor(both[:], oh[:, 0, :, :], oh[:, 1, :, :], ALU.add).then_inc(chosen, 1)
                else:
                    nc.vector.tensor_copy(both[:], oh[:, 0, :, :]).then_inc(chosen, 1)
                dve.wait_ge(counted, 1)
                do(nc.vector.tensor_copy(ne[:, 0, :], psN[:, 0:E]))
                do(nc.vector.tensor_tensor(cnt[:], bcast(ne[:, 0, :], 2, MAXM), bcast(W["iota"][0:PAIR, 32:32 + MAXM], 1, E), ALU.is_gt))
                do(nc.vector.tensor_reduce(ne[:, 1, :], cnt[:], AX.X, ALU.add))
                do(nc.vector.tensor_tensor_scan(ne[:, 2, :], ne[:, 1, :], zero[:], 0.0, ALU.add, ALU.add))
                do(nc.vector.tensor_tensor(ne[:, 3, :], ne[:, 2, :], ne[:, 1, :], ALU.subtract))
                do(nc.vector.tensor_scalar(ne[:, 3, :], ne[:, 3, :], float(SLOT), None, ALU.mult))
                do(nc.vector.tensor_tensor(place[:], v3(psP), bcast(ne[:, 3, :], 1, TILES), ALU.add))
                for r in range(ranks):
                    do(nc.vector.tensor_tensor(key[:], place[:], oh[:, r, :, :], ALU.mult))
                    do(nc.vector.tensor_reduce(slotf[:, :, r], key[:], AX.X, ALU.add))
                do(nc.vector.tensor_tensor(te[:], bcast(W["iota"][0:1, 48:48 + NT], 2, E), bcast(ne[0:1, 2, :], 1, NT), ALU.is_ge))
                do(nc.vector.tensor_reduce(tef[:], te[:], AX.X, ALU.add))
                do(nc.vector.tensor_scalar(tile_expert[:, 0:NT], tef[:], float(E - 1), None, ALU.min))
                do(nc.vector.tensor_scalar(tile_expert[:, NT:NT + 1], ne[0:1, 2, E - 1:E], usual + 0.5, None, ALU.is_gt))
                nc.vector.tensor_copy(slot[:, :, 0:ranks], slotf[:, :, 0:ranks]).then_inc(slots_ready, 1)


def expert_stage(nc, W, name, E, ranks, NT, usual, func, w_up, w_down, b_down, tile_expert, rows, slot, x_dram, cleared, y_dram):
    assert NT % 2 == 0 and usual % 2 == 0
    tokens_in = ranks * TOK
    with Stage(nc, name) as s:
        wu = s.sb("wu", [HD + 1, 2, 2 * F])
        wd = s.sb("wd", [128, 2, FC * D])
        wb = s.sb("wb", [1, 2, D]) if b_down is not None else None
        xs = s.sb("xs", [SLOT, 2, ROW])
        gate = s.sb("gate", [SLOT, 2])
        target = s.sb("target", [SLOT, 2], U32)
        xT = s.sb("xT", [HD + 1, 2, 2, SLOT])
        hm = s.sb("hm", [SLOT, F])
        hT = s.sb("hT", [128, FC, SLOT])
        ys = s.sb("ys", [SLOT, 2, D])
        psX = s.ps("psX", [HD, BANK])
        psU = s.ps("psU", [SLOT, 2, BANK])
        psH = s.ps("psH", [128, 2, BANK])
        psD = s.ps("psD", [SLOT, BANK])
        up_in, down_in, x_in, y_out = ([s.sem(f"{n}{i}") for i in range(2)] for n in ("up_in", "down_in", "x_in", "y_out"))
        ones_ready, x_turned, xT_ready, up_done, hm_ready = (
            s.sem(x) for x in ("ones_ready", "x_turned", "xT_ready", "up_done", "hm_ready"))
        h_turned, hT_ready, down_done, y_ready = (s.sem(x) for x in ("h_turned", "hT_ready", "down_done", "y_ready"))
        scattered, aside = s.sem("scattered"), s.sem("aside")
        down_parts = 2 if b_down is not None else 1
        xd = x_dram.rearrange("(n p) d -> n p d", p=SLOT)
        more = nc.values_load(tile_expert[0:1, NT:NT + 1], min_val=0, max_val=1)

        def each_tile(eng, step, finish):
            for i in range(3):
                step(i, i % 2, i // 2, i == 0)
            with eng.Fori(1, usual // 2 - 1) as k:
                step(2 * k + 1, 1, k, False)
                step(2 * k + 2, 0, k + 1, False)
            step(usual - 1, 1, usual // 2 - 1, False)
            with eng.If(more > 0):
                with eng.Fori(usual // 2, NT // 2) as k:
                    step(2 * k, 0, k, False)
                    step(2 * k + 1, 1, k, False)
                finish(NT)
            with eng.Else():
                finish(usual)

        def wait_past(eng, sem, n):
            if not (isinstance(n, int) and n <= 0):
                eng.wait_ge(sem, n)

        with nc.Block() as block:
            @block.sync
            def _(sp):
                def load(i, p, u, first):
                    e = sp.value_load(tile_expert[0:1, bass.ds(i, 1)], min_val=0, max_val=E - 1)
                    if first:
                        sp.dma_start(wu[:, p, :], w_up[bass.ds(e, 1), :, :].rearrange("o p f -> (o p) f")).then_inc(up_in[p], 16)
                        sp.wait_ge(scattered, 16 * TILES * ranks)
                        sp.dma_start(xs[:, p, :], xd[bass.ds(i, 1), :, :].rearrange("o p f -> (o p) f")).then_inc(x_in[p], 16)
                    else:
                        wait_past(sp, up_done, i - 1)
                        wait_past(sp, aside, i - 1)
                        sp.dma_start(xs[:, p, :], xd[bass.ds(i, 1), :, :].rearrange("o p f -> (o p) f")).then_inc(x_in[p], 16)
                        sp.dma_start(wu[:, p, :], w_up[bass.ds(e, 1), :, :].rearrange("o p f -> (o p) f")).then_inc(up_in[p], 16)

                each_tile(sp, load, lambda n: None)

            @block.tensor
            def _(pe):
                def turn_hidden(i):
                    pe.wait_ge(hm_ready, i + 1)
                    wait_past(pe, hT_ready, i)
                    for c in range(FC):
                        mm = nc.tensor.transpose(psH[:, c // 3, (c % 3) * SLOT:(c % 3 + 1) * SLOT],
                                                 hm[:, c * 128:(c + 1) * 128], W["ident"][:])
                    mm.then_inc(h_turned, 1)

                def down(i, p, u):
                    pe.wait_ge(down_in[p], (u + 1) * (16 * down_parts))
                    pe.wait_ge(hT_ready, i + 1)
                    wait_past(pe, y_ready, i)
                    for c in range(FC):
                        mm = nc.tensor.matmul(psD[:, 0:D], hT[:, c, :], wd[:, p, c * D:(c + 1) * D],
                                              start=c == 0, stop=c == FC - 1 and b_down is None)
                    if b_down is not None:
                        mm = nc.tensor.matmul(psD[:, 0:D], W["ones"][0:1, 0:SLOT], wb[:, p, :], start=False, stop=True)
                    mm.then_inc(down_done, 1)

                def step(i, p, u, first):
                    pe.wait_ge(x_in[p], (u + 1) * 16)
                    if not first:
                        pe.wait_ge(xT_ready, i)
                    for k in range(2):
                        mm = nc.tensor.transpose(psX[:, k * SLOT:(k + 1) * SLOT], xs[:, p, k * HD:(k + 1) * HD], W["ident"][:])
                    mm.then_inc(x_turned, 1)
                    if not first:
                        turn_hidden(i - 1)
                    pe.wait_ge(up_in[p], (u + 1) * 16)
                    pe.wait_ge(xT_ready, i + 1)
                    for j in range(2):
                        c = j * D_IN
                        nc.tensor.matmul(psU[:, j, 0:D_IN], xT[:, p, 0, :], wu[:, p, c:c + D_IN], start=True, stop=False)
                        mm = nc.tensor.matmul(psU[:, j, 0:D_IN], xT[0:HD, p, 1, :], wu[0:HD, p, F + c:F + c + D_IN],
                                              start=False, stop=True)
                    mm.then_inc(up_done, 1)
                    if not first:
                        down(i - 1, 1 - p, u - 1 + p)

                pe.wait_ge(ones_ready, 1)
                def finish(n):
                    turn_hidden(n - 1)
                    down(n - 1, 1, n // 2 - 1)

                each_tile(pe, step, finish)

            @block.vector
            def _(dve):
                def step(i, p, u, first):
                    dve.wait_ge(x_turned, i + 1)
                    if not first:
                        wait_past(dve, up_done, i - 1)
                    nc.vector.tensor_copy(xT[0:HD, p, :, :], psX[:, 0:2 * SLOT].rearrange("p (k n) -> p k n", k=2)).then_inc(xT_ready, 1)
                    if not first:
                        hidden(i - 1)
                    wait_past(dve, y_out[p], u * 16)
                    nc.vector.tensor_scalar(target[:, p:p + 1], xs[:, p, D:D + 1], float(NO_ROW), None, ALU.add)
                    nc.vector.tensor_copy(gate[:, p:p + 1], xs[:, p, D + 1:D + 2]).then_inc(aside, 1)

                def hidden(i):
                    dve.wait_ge(h_turned, i + 1)
                    wait_past(dve, down_done, i)
                    nc.vector.tensor_copy(hT[:].rearrange("p (a b) n -> p a (b n)", a=2), psH[:, :, 0:D_IN]).then_inc(hT_ready, 1)

                nc.vector.memset(xT[HD:HD + 1, :, :, :], 1.0).then_inc(ones_ready, 1)
                each_tile(dve, step, lambda n: hidden(n - 1))

            @block.scalar
            def _(act):
                def load_down(i, p):
                    e = act.value_load(tile_expert[0:1, bass.ds(i, 1)], min_val=0, max_val=E - 1)
                    act.dma_start(wd[:, p, :], w_down[bass.ds(e, 1), :, :].rearrange("o p f -> (o p) f")).then_inc(down_in[p], 16)
                    if b_down is not None:
                        act.dma_start(wb[:, p, :], b_down[bass.ds(e, 1), :]).then_inc(down_in[p], 16)

                def result(i, p, u):
                    act.wait_ge(down_done, i + 1)
                    act.wait_ge(aside, i + 1)
                    wait_past(act, y_out[p], u * 16)
                    nc.scalar.activation(ys[:, p, :], psD[:, 0:D], ACT.Copy, scale=gate[:, p:p + 1]).then_inc(y_ready, 1)

                def step(i, p, u, first):
                    load_down(i, p)
                    act.wait_ge(up_done, i + 1)
                    wait_past(act, h_turned, i)
                    nc.scalar.activation(hm[:].rearrange("p (a n) -> p a n", a=2), psU[:, :, 0:D_IN], func).then_inc(hm_ready, 1)
                    if not first:
                        result(i - 1, 1 - p, u - 1 + p)

                each_tile(act, step, lambda n: result(n - 1, 1, n // 2 - 1))

            @block.gpsimd
            def _(pool):
                pool.wait_ge(cleared, 16)
                for t in range(TILES):
                    for r in range(ranks):
                        nc.gpsimd.indirect_dma_start(
                            out=x_dram[:, :], out_offset=bass.IndirectOffsetOnAxis(ap=slot[:, t, r:r + 1], axis=0),
                            in_=rows[:, t, r, :], in_offset=None).then_inc(scattered, 16)

                def send(first, last):
                    for i in range(first, last):
                        p = i % 2
                        pool.wait_ge(y_ready, i + 1)
                        nc.gpsimd.indirect_dma_start(
                            out=y_dram[:, :], out_offset=bass.IndirectOffsetOnAxis(ap=target[:, p:p + 1], axis=0),
                            in_=ys[:, p, :], in_offset=None, bounds_check=tokens_in - 1, oob_is_err=False).then_inc(y_out[p], 16)
                    for q in y_out:
                        pool.wait_ge(q, 16 * (last // 2))

                send(0, usual)
                with pool.If(more > 0):
                    send(usual, NT)


def combine_stage(nc, W, name, ranks, y_dram, dst, plus=None):
    with Stage(nc, name) as s:
        y = s.sb("y", [PAIR, TILES, ranks, D])
        got = s.sem("got")
        vec = Step(s.sem("vec"))
        with nc.Block() as block:
            @block.sync
            def _(sp):
                sp.dma_start(y[:].rearrange("p t r d -> p t (r d)"),
                             y_dram.rearrange("(t p r) d -> p t (r d)", p=PAIR, r=ranks)).then_inc(got, 16)

            @block.vector
            def _(dve):
                if plus is not None:
                    link(dve, vec, nc.vector.tensor_tensor(dst[:], dst[:], plus[:], ALU.add))
                dve.wait_ge(got, 16)
                for r in range(ranks):
                    link(dve, vec, nc.vector.tensor_tensor(dst[:], dst[:], y[:, :, r, :], ALU.add))


def mamba_layer(nc, W, x, xn, xT, H):
    ZD = D_IN + M_HEADS
    with Stage(nc, "mb") as s:
        z = s.sb("z", [PAIR, TILES, ZD])
        xh = s.sb("xh", [PAIR, TILES, D_IN])
        L = s.sb("L", [PAIR, TILES * M_HEADS, PAIR])
        cc = s.sb("cc", [128, 5, TOK])
        dt = s.sb("dt", [PAIR, TILES, M_HEADS])
        dec = s.sb("dec", [PAIR, TILES, M_HEADS])
        with Stage(nc, "mc") as p:
            xbc = p.sb("xbc", [128, 5, IMAGES, PADSEQ])
            raw = p.sb("raw", [128, 5, TOK])
            prods = []
            for c in range(5):
                rows = 128 if c < 3 else D_ST
                w0 = ZD + (c * 128 if c < 3 else D_IN + (c - 3) * D_ST)
                for g in range(2):
                    prods.append(([(xbc[0:rows, c, 8 * g:8 * g + 8, KCONV - 1:PADSEQ], 0, None)],
                                  [(W["win"][:, k, w0:w0 + rows], xT[:, k, g * HALF_TOK:(g + 1) * HALF_TOK]) for k in range(2)]))
            for t in range(TILES):
                prods.append(([(z[:, t, :], 0, None)], [(xT[:, k, tokens(t)], W["win"][:, k, 0:ZD]) for k in range(2)]))
            product_stage(nc, W, "mp", prods, ["win"])

            t1, t2, t3 = (p.sb(n, [PAIR, TILES * M_HEADS]) for n in ("t1", "t2", "t3"))
            A = p.sb("A", [PAIR, M_HEADS])
            vec, conv = Step(p.sem("vec")), Step(p.sem("conv"))
            conv_done, silus = p.sem("conv_done"), p.sem("silus")
            a_ready, z_done, dt_absd, dt_exp, dec_in, dec_out = (
                p.sem(n) for n in ("a_ready", "z_done", "dt_absd", "dt_exp", "dec_in", "dec_out"))
            dtf = dt[:].rearrange("p t h -> p (t h)")
            decf = dec[:].rearrange("p t h -> p (t h)")
            with nc.Block() as block:
                @block.vector
                def _(dve):
                    def do(ins):
                        link(dve, vec, ins)

                    for n in ("mvec", "colb"):
                        dve.wait_ge(W["sem"][n], 16)
                    do(nc.vector.tensor_tensor(dt[:], z[:, :, D_IN:ZD], bcast(W["colb"][:, 16:22], 1, TILES), ALU.add))
                    do(nc.vector.tensor_scalar(t1[:], dtf, -1.0, None, ALU.mult))
                    nc.vector.tensor_tensor(t1[:], t1[:], dtf, ALU.min).then_inc(dt_absd, 1)
                    do(nc.vector.memset(xbc[:, :, :, 0:KCONV - 1], 0.0))
                    dve.wait_ge(dt_exp, 1)
                    do(nc.vector.tensor_scalar(t2[:], t1[:], 2.0, None, ALU.add))
                    do(nc.vector.reciprocal(t2[:], t2[:]))
                    do(nc.vector.tensor_tensor(t1[:], t1[:], t2[:], ALU.mult))
                    do(nc.vector.tensor_tensor(t2[:], t1[:], t1[:], ALU.mult))
                    do(nc.vector.tensor_scalar(t3[:], t2[:], 1.0 / 17, 1.0 / 15, ALU.mult, ALU.add))
                    for odd in (13, 11, 9, 7, 5, 3, 1):
                        do(nc.vector.tensor_tensor(t3[:], t3[:], t2[:], ALU.mult))
                        do(nc.vector.tensor_scalar(t3[:], t3[:], 1.0 / odd, None, ALU.add))
                    do(nc.vector.scalar_tensor_tensor(t3[:], t3[:], 2.0, t1[:], ALU.mult, ALU.mult))
                    do(nc.vector.scalar_tensor_tensor(dtf, dtf, 0.0, t3[:], ALU.max, ALU.add))
                    dve.wait_ge(a_ready, 1)
                    nc.vector.scalar_tensor_tensor(dec[:], dt[:], -1.0, bcast(A[:], 1, TILES), ALU.mult, ALU.mult).then_inc(dec_in, 1)
                    for k in range(KCONV):
                        for c in range(5):
                            r = 128 if c < 3 else D_ST
                            src = xbc[0:r, c, :, k:k + SEQ]
                            dst = raw[0:r, c, :].rearrange("p (b q) -> p b q", b=IMAGES)
                            tap = W["mvec"][0:r, c, k:k + 1]
                            if k:
                                dve.wait_ge(conv.sem, 5 * (k - 1) + c + 1)
                            conv.add(nc.vector.tensor_scalar(dst, src, tap, None, ALU.mult) if k == 0 else
                                     nc.vector.scalar_tensor_tensor(dst, src, tap, dst, ALU.mult, ALU.add))

                @block.scalar
                def _(act):
                    act.wait_ge(W["sem"]["colb"], 16)
                    nc.scalar.activation(A[:], W["colb"][:, 24:30], ACT.Exp).then_inc(a_ready, 1)
                    act.wait_ge(dt_absd, 1)
                    nc.scalar.activation(t1[:], t1[:], ACT.Exp).then_inc(dt_exp, 1)
                    act.wait_ge(dec_in, 1)
                    nc.scalar.activation(decf, decf, ACT.Exp).then_inc(dec_out, 1)
                    for t in range(TILES):
                        nc.scalar.activation(z[:, t, 0:D_IN], z[:, t, 0:D_IN], ACT.Silu).then_inc(z_done, 1)
                    for c in range(5):
                        r = 128 if c < 3 else D_ST
                        act.wait_ge(conv.sem, 5 * (KCONV - 1) + c + 1)
                        nc.scalar.activation(cc[0:r, c, :], raw[0:r, c, :], ACT.Silu, bias=W["mvec"][0:r, c, 4:5], scale=1.0).then_inc(silus, 1)

        with Stage(nc, "md") as p:
            decT = p.sb("decT", [M_HEADS, TOK])
            d0 = p.sb("d0", [PAIR, TILES, M_HEADS, PAIR])
            d1 = p.sb("d1", [PAIR, TILES * M_HEADS, PAIR])
            psD = p.ps("psD", [M_HEADS, 2, BANK])
            psB = p.ps("psB", [PAIR, 2, BANK])
            psX = p.ps("psX", [PAIR, 2, BANK])
            psG = p.ps("psG", [PAIR, 2, BANK])
            dec_turned, decT_ready, spread, masked, scanned = (p.sem(n) for n in ("dec_turned", "decT_ready", "spread", "masked", "scanned"))
            x_turned, x_kept, g_ready, d1_ready, weighted = (p.sem(n) for n in ("x_turned", "x_kept", "g_ready", "d1_ready", "weighted"))
            with nc.Block() as block:
                @block.tensor
                def _(pe):
                    for t in range(TILES):
                        mm = nc.tensor.transpose(psD[:, t // 4, (t % 4) * PAIR:(t % 4 + 1) * PAIR], dec[:, t, :], W["ident"][0:PAIR, 0:PAIR])
                    mm.then_inc(dec_turned, 1)
                    for t in range(TILES):
                        mm = nc.tensor.matmul(psG[:, t // 4, (t % 4) * PAIR:(t % 4 + 1) * PAIR], cc[0:D_ST, 3, tokens(t)],
                                              cc[0:D_ST, 4, tokens(t)], start=True, stop=True)
                    mm.then_inc(g_ready, 1)
                    pe.wait_ge(decT_ready, 2)
                    pe.wait_ge(W["sem"]["sel"], 16)
                    for hd in range(M_HEADS):
                        for g in range(2):
                            n = 2 * hd + g
                            if n >= 2:
                                pe.wait_ge(masked, n - 1)
                            nc.tensor.matmul(psB[:, g, 0:HALF_TOK], W["sel"][:, hd, :], decT[:, g * HALF_TOK:(g + 1) * HALF_TOK],
                                             start=True, stop=True).then_inc(spread, 1)
                    for t in range(TILES):
                        if t >= 2:
                            pe.wait_ge(x_kept, t - 1)
                        for c in range(3):
                            mm = nc.tensor.transpose(psX[:, t % 2, c * 128:(c + 1) * 128], cc[:, c, tokens(t)], W["ident"][:])
                        mm.then_inc(x_turned, 1)

                @block.scalar
                def _(act):
                    act.wait_ge(dec_turned, 1)
                    for g in range(2):
                        nc.scalar.copy(decT[:, g * HALF_TOK:(g + 1) * HALF_TOK], psD[:, g, 0:HALF_TOK]).then_inc(decT_ready, 1)
                    for t in range(TILES):
                        act.wait_ge(x_turned, t + 1)
                        nc.scalar.copy(xh[:, t, :], psX[:, t % 2, 0:D_IN]).then_inc(x_kept, 1)

                @block.gpsimd
                def _(pool):
                    nc.gpsimd.tensor_tensor(d1[:], bcast(W["ident"][0:PAIR, 0:PAIR], 1, TILES * M_HEADS),
                                            bcast(dt[:].rearrange("p t h -> p (t h)"), 2, PAIR), ALU.mult).then_inc(d1_ready, 1)

                @block.vector
                def _(dve):
                    dve.wait_ge(W["sem"]["lmask"], 16)
                    for hd in range(M_HEADS):
                        for g in range(2):
                            n = 2 * hd + g
                            dve.wait_ge(spread, n + 1)
                            nc.vector.tensor_tensor(d0[:, 4 * g:4 * g + 4, hd, :], psB[:, g, 0:HALF_TOK].rearrange("p (t i) -> p t i", t=4),
                                                    bcast(W["lmask"][:], 1, 4), ALU.mult).then_inc(masked, 1)
                    dve.wait_ge(masked, 2 * M_HEADS)
                    dve.wait_ge(d1_ready, 1)
                    nc.vector.tensor_tensor_scan(L[:].rearrange("p a i -> p (a i)"), d0[:].rearrange("p t h i -> p (t h i)"),
                                                 d1[:].rearrange("p a i -> p (a i)"), 0.0, ALU.mult, ALU.add).then_inc(scanned, 1)
                    dve.wait_ge(scanned, 1)
                    dve.wait_ge(g_ready, 1)
                    for t in range(TILES):
                        Lt = L[:, t * M_HEADS:(t + 1) * M_HEADS, :]
                        nc.vector.tensor_tensor(Lt, bcast(psG[:, t // 4, (t % 4) * PAIR:(t % 4 + 1) * PAIR], 1, M_HEADS), Lt,
                                                ALU.mult).then_inc(weighted, 1)

        with Stage(nc, "me") as p:
            g = p.sb("g", [PAIR, TILES, D_IN])
            sq = p.sb("sq", [PAIR, TILES, D_IN])
            ms = p.sb("ms", [PAIR, 3, TILES])
            gT = p.sb("gT", [128, 3, TOK])
            y_ready, y_read, vec = p.sem("y_ready"), p.sem("y_read"), Step(p.sem("vec"))
            dx_ready, var_ready, rstd_ready = p.sem("dx_ready"), p.sem("var_ready"), p.sem("rstd_ready")
            with Stage(nc, "my") as q:
                psY = q.ps("psY", [PAIR, 4, BANK])
                with nc.Block() as block:
                    @block.tensor
                    def _(pe):
                        for t in range(TILES):
                            if t >= 4:
                                pe.wait_ge(y_read, t - 3)
                            for hd in range(M_HEADS):
                                mm = nc.tensor.matmul(psY[:, t % 4, hd * DH:(hd + 1) * DH], L[:, t * M_HEADS + hd, :],
                                                      xh[:, t, hd * DH:(hd + 1) * DH], start=True, stop=True)
                            mm.then_inc(y_ready, 1)

                    @block.gpsimd
                    def _(pool):
                        pool.wait_ge(var_ready, 1)
                        nc.gpsimd.tensor_tensor(ms[:, 2, :], ms[:, 1, :], W["mhalf"][0:PAIR, 0:TILES], ALU.pow).then_inc(rstd_ready, 1)

                    @block.vector
                    def _(dve):
                        dve.wait_ge(W["sem"]["rowp"], 16)
                        link(dve, vec, nc.vector.tensor_tensor(g[:], xh[:], bcast(W["rowp"][:, 0, :], 1, TILES), ALU.mult))
                        for t in range(TILES):
                            dve.wait_ge(y_ready, t + 1)
                            nc.vector.tensor_tensor(g[:, t, :], psY[:, t % 4, 0:D_IN], g[:, t, :], ALU.add).then_inc(y_read, 1)
                        dve.wait_ge(y_read, TILES)
                        link(dve, vec, nc.vector.tensor_tensor(g[:], g[:], z[:, :, 0:D_IN], ALU.mult))
                        link(dve, vec, nc.vector.tensor_tensor(sq[:], g[:], g[:], ALU.mult))
                        link(dve, vec, nc.vector.tensor_reduce(ms[:, 0, :], sq[:], AX.X, ALU.add))
                        nc.vector.tensor_scalar(ms[:, 1, :], ms[:, 0, :], 1.0 / D_IN, 1e-5, ALU.mult, ALU.add).then_inc(var_ready, 1)
                        dve.wait_ge(rstd_ready, 1)
                        for t in range(TILES):
                            vec.add(nc.vector.scalar_tensor_tensor(g[:, t, :], g[:, t, :], ms[:, 2, t:t + 1], W["rowp"][:, 1, :], ALU.mult, ALU.mult))
                        dve.wait_ge(vec.sem, vec.n)
                        vec.add(nc.vector.tensor_tensor(H[:], H[:], x[:], ALU.add))
            channels_stage(nc, W, "mf", g, gT)
            prods = [([(H[:, t, :], 0, None)], [(gT[:, k, tokens(t)], W["wout"][:, k, :]) for k in range(3)]) for t in range(TILES)]
            product_stage(nc, W, "mg", prods, ["wout"], add=True)


E0, E1 = 8, 16
NT0 = expert_tiles(E0, 2 * TOK) // 2 * 2 + 2 * (expert_tiles(E0, 2 * TOK) % 2)
NT1 = expert_tiles(E1, TOK) // 2 * 2 + 2 * (expert_tiles(E1, TOK) % 2)
USUAL0, USUAL1 = 2 * TOK // SLOT + 2, E1 + 2

RESIDENT = {
    "stem_w": (96, 2, C1), "chan": (C1, 6, 3), "tabs": (128, 72), "ident": (128, 128), "off_w": (C1, TAPS, 32), "stack4": (128, 32),
    "dcn_w": (C1, TAPS, D), "wq": (HD, 2, HEADS * DH), "wk": (HD, 2, HEADS * DH), "qkvb": (128, 3, 6),
    "amask": (PAIR, PAIR), "wv": (HD, 2, HEADS * DH), "wo": (128, 6, D), "rowb": (1, 2, D), "w1": (HD + 1, 2, 3 * D),
    "cmask": (HD, HD), "w2": (HD, 2, D), "imean": (PAIR, PAIR), "before": (PAIR, PAIR), "iota": (128, 82 + TILES),
    "wr0": (HD, 2, E0), "sel": (M_HEADS, M_HEADS, PAIR), "lmask": (PAIR, PAIR), "mvec": (128, 5, 5),
    "wr1": (HD, 2, E1), "win": (HD, 2, 2 * D_IN + 2 * D_ST + M_HEADS), "wout": (128, 3, D),
}
LATE = {"w1", "w2", "win", "wout", "mvec", "rowd", "rowp", "cmask", "imean", "before", "iota", "wr0", "wr1", "sel", "lmask"}
SPREAD = {"colb": 32, "rowd": 7 * D, "rowp": 2 * D_IN}
STREAMED = {"x": (96, IMAGES // 2 * PIX), "up0": (E0, HD + 1, 2 * F), "down0": (E0, 128, FC * D), "bdown0": (E0, D),
            "up1": (E1, HD + 1, 2 * F), "down1": (E1, 128, FC * D)}


def vit_tower(nc, K, out):
    W = {"sem": {}}
    with ExitStack() as top:
        def sb(name, shape, dt=F32):
            return top.enter_context(nc.sbuf_tensor(name, list(shape), dt))

        def place(late):
            for name, shape in RESIDENT.items():
                if (name in LATE) == late:
                    W[name] = sb(name, shape)
                    W["sem"][name] = nc.alloc_semaphore(f"in_{name}")
            for name, n in SPREAD.items():
                if (name in LATE) == late:
                    W[name] = sb(name, (PAIR, n))
                    W["sem"][name] = nc.alloc_semaphore(f"in_{name}")

        def fetch(act, late):
            for name in RESIDENT:
                if (name in LATE) == late:
                    act.dma_start(W[name][:], K[name]).then_inc(W["sem"][name], 16)
            for name in SPREAD:
                if (name in LATE) == late:
                    act.dma_start(W[name][:], K[name].partition_broadcast(PAIR)).then_inc(W["sem"][name], 16)

        place(False)
        W["mhalf"], W["ones"], W["bnv"] = sb("mhalf", (128, 8)), sb("ones", (128, 128)), sb("bnv", (C1, 3, 3))
        H = sb("H", (PAIR, TILES, D))
        off_dram = nc.dram_tensor("points", (IMAGES, 32, POS), F32, kind="Internal").ap()
        a_dram = nc.dram_tensor("channel_rows", (IMAGES, D, SEQ), F32, kind="Internal").ap()
        xs0, xs1 = (nc.dram_tensor(n, (t * SLOT, ROW), F32, kind="Internal").ap() for n, t in (("rows0", NT0), ("rows1", NT1)))
        ys0, ys1 = (nc.dram_tensor(n, (t, D), F32, kind="Internal").ap() for n, t in (("results0", 2 * TOK), ("results1", TOK)))
        zrow = sb("zrow", (SLOT, ROW))
        zeroed, cleared0, cleared1 = (nc.alloc_semaphore(n) for n in ("zeroed", "cleared0", "cleared1"))
        ones_done = nc.alloc_semaphore("ones_done")

        with nc.Block() as block:
            @block.scalar
            def _(act):
                fetch(act, False)

            @block.vector
            def _(dve):
                nc.vector.memset(zrow[:], 0.0).then_inc(zeroed, 1)
                nc.vector.memset(W["ones"][:], 1.0).then_inc(ones_done, 1)
                dve.wait_ge(ones_done, 1)

        with nc.cleanup_on_exit(), Stage(nc, "pe") as s:
            h = s.sb("h", [C1, IMAGES, PIX])
            samp = s.sb("samp", [C1, TAPS, IMAGES * POS])
            hc = s.sb("hc", [HD, 2, IMAGES, SEQ])
            all_near = s.sb("all_near", [1, 1], I32)
            stem_stage(nc, K, W, h, samp, off_dram, all_near)
            near = nc.values_load(all_near[0:1, 0:1], min_val=0, max_val=1)
            with nc.If(near > 0):
                near_sampling_stage(nc, K, W, h, samp, off_dram, hc)
            with nc.Else():
                sampling_stage(nc, K, W, h, samp, off_dram)
                patch_stage(nc, K, W, samp, hc)
            token_stage(nc, W, hc, H)
        with nc.cleanup_on_exit():
            attention_layer(nc, W, H)
        place(True)
        with nc.Block() as block:
            @block.sync
            def _(sp):
                sp.wait_ge(zeroed, 1)
                for xd, n, cleared in ((xs0, NT0, cleared0), (xs1, NT1, cleared1)):
                    sp.dma_start(xd.rearrange("(n p) d -> p n d", p=SLOT), bcast(zrow[:], 1, n)).then_inc(cleared, 16)

            @block.scalar
            def _(act):
                fetch(act, True)
        W["rowd"] = W["rowd"][:].rearrange("p (a d) -> p a d", d=D)
        W["rowp"] = W["rowp"][:].rearrange("p (a d) -> p a d", d=D_IN)
        with nc.cleanup_on_exit(), Stage(nc, "l0") as s:
            X = s.sb("X", [PAIR, TILES, D])
            xT = s.sb("xT", [HD + 1, 2, TOK])
            Y = s.sb("Y", [PAIR, TILES, D])
            YT = s.sb("YT", [HD, 2, TOK])
            rows, slot, te = s.sb("rows", [PAIR, TILES, 2, ROW]), s.sb("slot", [PAIR, TILES, 2], U32), s.sb("te", [1, 32], I32)
            ones_row = s.sem("ones_row")
            norm_stage(nc, W, "l0_n", H, X, 1e-5)
            channels_stage(nc, W, "l0_c", X, xT[0:HD, :, :])
            with nc.Block() as block:
                @block.vector
                def _(dve):
                    nc.vector.memset(xT[HD:HD + 1, :, :], 1.0).then_inc(ones_row, 1)
                    dve.wait_ge(ones_row, 1)
                    dve.wait_ge(W["sem"]["rowd"], 16)
            channel_attention(nc, W, xT, X, a_dram, Y, YT)
            global_norm_stage(nc, W, "l0_g", X, Y, W["rowd"][:, 0, :], W["rowd"][:, 1, :])
            channels_stage(nc, W, "l0_d", Y, YT)
            routing_stage(nc, W, "l0_r", E0, 2, NT0, USUAL0, YT, W["wr0"], "wr0", True, Y, rows, slot, te)
            expert_stage(nc, W, "l0_e", E0, 2, NT0, USUAL0, ACT.Gelu_apprx_tanh, K["up0"], K["down0"], K["bdown0"], te,
                         rows, slot, xs0, cleared0, ys0)
            combine_stage(nc, W, "l0_m", 2, ys0, Y)
            global_norm_stage(nc, W, "l0_h", Y, X, W["rowd"][:, 2, :], W["rowd"][:, 3, :], add_to=H)
        with nc.cleanup_on_exit(), Stage(nc, "l1") as s:
            X = s.sb("X", [PAIR, TILES, D])
            XN = s.sb("XN", [PAIR, TILES, D])
            xT = s.sb("xT", [HD, 2, TOK])
            norm_stage(nc, W, "l1_a", H, X, 1e-5)
            norm_stage(nc, W, "l1_b", X, XN, 1e-5, gain=W["rowd"][:, 4, :], shift=W["rowd"][:, 5, :])
            channels_stage(nc, W, "l1_c", XN, xT)
            mamba_layer(nc, W, X, XN, xT, H)
        with nc.cleanup_on_exit(), Stage(nc, "l2") as s:
            X = s.sb("X", [PAIR, TILES, D])
            XN = s.sb("XN", [PAIR, TILES, D])
            xT = s.sb("xT", [HD, 2, TOK])
            rows, slot, te = s.sb("rows", [PAIR, TILES, 1, ROW]), s.sb("slot", [PAIR, TILES, 2], U32), s.sb("te", [1, 32], I32)
            norm_stage(nc, W, "l2_a", H, X, 1e-5)
            norm_stage(nc, W, "l2_b", X, XN, 1e-6, rms=True, gain=W["rowd"][:, 6, :])
            channels_stage(nc, W, "l2_c", XN, xT)
            routing_stage(nc, W, "l2_r", E1, 1, NT1, USUAL1, xT, W["wr1"], "wr1", False, XN, rows, slot, te)
            expert_stage(nc, W, "l2_e", E1, 1, NT1, USUAL1, ACT.Relu, K["up1"], K["down1"], None, te, rows, slot, xs1, cleared1, ys1)
            combine_stage(nc, W, "l2_m", 1, ys1, H, plus=X)
        out_done = nc.alloc_semaphore("out_done")
        with nc.Block() as block:
            @block.sync
            def _(sp):
                for q in W["sem"].values():
                    sp.wait_ge(q, 16)
                sp.dma_start(out.rearrange("(t o) q d -> (o q) t d", o=2), H[:]).then_inc(out_done, 16)
                sp.wait_ge(out_done, 16)


def layouts(a):
    f = np.float32

    def halves(w):
        return w.reshape(2, HD, -1).transpose(1, 0, 2)

    def biased(w, b):
        lo = np.concatenate([w[:HD], b[None]], 0)
        hi = np.concatenate([w[HD:], np.zeros_like(b)[None]], 0)
        return np.stack([lo, hi], 1)

    K = {}
    x = a["x"].reshape(2, IMAGES // 2, 3, SIDE, 4, SIDE, 4)
    K["x"] = x.transpose(0, 2, 4, 6, 1, 3, 5).reshape(96, IMAGES // 2 * PIX)
    K["stem_w"] = np.zeros((96, 2, C1), f)
    K["stem_w"][0:48, 0] = K["stem_w"][48:96, 1] = a["L0_tok_stem_w"].reshape(C1, 48).T
    K["stack4"] = np.tile(np.eye(32, dtype=f), (4, 1))
    chan = np.zeros((C1, 6, 3), f)
    for i, n in enumerate("gbmv"):
        chan[:, i, 0] = a[f"L0_tok_bn1_{n}"]
        chan[:, i, 1:] = a[f"L0_tok_bn2_{n}"].reshape(2, HD).T
    chan[:, 4, 0] = a["L0_tok_stem_b"]
    chan[:, 4, 1:] = a["L0_tok_dcn_b"].reshape(2, HD).T
    chan[:, 5, 0:2] = a["cls_tok"].reshape(2, HD).T
    K["chan"] = chan
    by_axis = lambda v: np.ascontiguousarray(v.reshape((TAPS, 2) + v.shape[1:]).swapaxes(0, 1)).reshape(v.shape)
    K["off_w"] = by_axis(a["L0_tok_off_w"]).reshape(32, C1, TAPS).transpose(1, 2, 0)
    tabs = np.zeros((128, 72), f)
    p = np.arange(CHUNK)
    for c in range(CHUNKS):
        tabs[:CHUNK, c] = -(ROWS * c + p // SIDE)
    tabs[:CHUNK, 7] = -(p % SIDE)
    tabs[:32, 8] = by_axis(a["L0_tok_off_b"])
    pos, tap = np.arange(POS), np.arange(TAPS)
    tabs[0:16, 16:16 + POS] = 4 * (pos // OUT_SIDE)[None] + (tap // 4)[:, None]
    tabs[16:32, 16:16 + POS] = 4 * (pos % OUT_SIDE)[None] + (tap % 4)[:, None]
    K["tabs"] = tabs
    K["ident"] = np.eye(128, dtype=f)
    K["dcn_w"] = a["L0_tok_dcn_w"].reshape(D, C1, TAPS).transpose(1, 2, 0)
    for n, w in (("wq", "Q"), ("wk", "K"), ("wv", "V")):
        K[n] = halves(a[f"L0_attn_W_{w}"].transpose(1, 0, 2).reshape(D, HEADS * DH))
    K["qkvb"] = np.stack([a[f"L0_attn_b_{n}"].reshape(6, 128).T for n in "QKV"], 1)
    K["wo"] = a["L0_attn_W_O"].reshape(6, 128, D).transpose(1, 0, 2)
    K["rowb"] = np.stack([a["L0_attn_b_O"], a["L0_ffn_W2_b"]])[None]
    K["w1"] = biased(a["L0_ffn_W1_w"], a["L0_ffn_W1_b"])
    K["w2"] = halves(a["L0_ffn_W2_w"])
    q = np.arange(PAIR)
    same = q[:, None] // SEQ == q[None] // SEQ
    K["amask"] = np.where(same & (q[None] <= q[:, None]), 0, NEG).astype(f)
    c = np.arange(HD)
    K["cmask"] = np.where(c[:, None] // 16 == c[None] // 16, 0, NEG).astype(f)
    K["imean"] = (same / SEQ).astype(f)
    K["before"] = (q[:, None] < q[None]).astype(f)
    iota = np.zeros((128, 82 + TILES), f)
    iota[:PAIR, 80:80 + TILES] = np.arange(TOK).reshape(TILES, PAIR).T
    iota[:, 80 + TILES:] = np.arange(2) - NO_ROW
    iota[:, 0:32] = np.arange(32)
    iota[:, 32:40] = SLOT * np.arange(8)
    iota[:, 48:80] = np.arange(32)
    K["iota"] = iota
    K["wr0"], K["wr1"] = halves(a["L0_ffn_r_w"]), halves(a["L1_ffn_w_router"])
    K["sel"] = np.repeat(np.eye(M_HEADS, dtype=f)[:, :, None], PAIR, 2)
    K["lmask"] = (same & (q[None] > q[:, None])).astype(f)
    conv = np.concatenate([a["L1_attn_conv_w"], a["L1_attn_conv_b"][:, None]], 1)
    mvec = np.zeros((128, 5, 5), f)
    mvec[:, 0:3] = conv[:D_IN].reshape(3, 128, 5).transpose(1, 0, 2)
    mvec[:D_ST, 3:5] = conv[D_IN:].reshape(2, D_ST, 5).transpose(1, 0, 2)
    K["mvec"] = mvec
    w = a["L1_attn_W_in"]
    K["win"] = halves(np.concatenate([w[:, :D_IN], w[:, -M_HEADS:], w[:, D_IN:-M_HEADS]], 1))
    K["wout"] = a["L1_attn_W_out"].reshape(3, 128, D).transpose(1, 0, 2)
    colb = np.zeros(32, f)
    colb[0:8], colb[16:22], colb[24:30] = a["L0_ffn_r_b"], a["L1_attn_dt_bias"], a["L1_attn_A_log"]
    K["colb"] = colb
    K["rowd"] = np.concatenate([a[n] for n in ("L0_ffn_ln1_w", "L0_ffn_ln1_b", "L0_ffn_ln2_w", "L0_ffn_ln2_b",
                                               "L1_attn_ln_w", "L1_attn_ln_b", "L1_ffn_ln_w")])
    K["rowp"] = np.concatenate([np.repeat(a["L1_attn_D"], DH), a["L1_attn_rms_w"]])

    def up(w, b):
        w = w.reshape(-1, 2, HD, F).transpose(0, 2, 1, 3)
        row = np.stack([b, np.zeros_like(b)], 1)[:, None]
        return np.concatenate([w, row], 1).reshape(-1, HD + 1, 2 * F)

    def down(w):
        return w.reshape(-1, FC, 128, D).transpose(0, 2, 1, 3).reshape(-1, 128, FC * D)

    K["up0"], K["down0"], K["bdown0"] = up(a["L0_ffn_fc_w"], a["L0_ffn_fc_b"]), down(a["L0_ffn_proj_w"]), a["L0_ffn_proj_b"]
    K["up1"], K["down1"] = up(a["L1_ffn_wi"], np.zeros((E1, F), f)), down(a["L1_ffn_wo"])
    return {n: np.ascontiguousarray(v) for n, v in K.items()}


def kernel(**inputs):
    import concourse.bacc as bacc
    from concourse.bass_utils import run_bass_kernel_spmd

    nc = bacc.Bacc("TRN2", target_bir_lowering=False, num_devices=1)
    arrays = layouts({n: np.asarray(v) for n, v in inputs.items()})
    K = {n: nc.dram_tensor(f"in_{n}", v.shape, mybir.dt.from_np(v.dtype), kind="ExternalInput").ap() for n, v in arrays.items()}
    out = nc.dram_tensor("out", (IMAGES, SEQ, D), F32, kind="ExternalOutput").ap()
    vit_tower(nc, K, out)
    r = run_bass_kernel_spmd(nc, [{f"in_{n}": v for n, v in arrays.items()}], core_ids=[0])
    return r.results[0]["out"]
```

```python
from contextlib import ExitStack

import numpy as np

import concourse.bass as bass
from concourse import mybir

F32 = mybir.dt.float32
I32 = mybir.dt.int32
U32 = mybir.dt.uint32
ALU = mybir.AluOpType
ACT = mybir.ActivationFunctionType
AX = mybir.AxisListType

IMAGES = 16
SIDE = 28
PIX = SIDE * SIDE
TAPS = 16
OUT_SIDE = 7
POS = OUT_SIDE * OUT_SIDE
SEQ = POS + 1
C1 = 96
D = 192
HD = 96
TOK = IMAGES * SEQ
PAIR = 2 * SEQ
TILES = TOK // PAIR
HALF_TOK = TOK // 2
ROWS = 4
CHUNK = ROWS * SIDE
CHUNKS = PIX // CHUNK
HALF = PIX // 2
HEADS = 12
DH = 64
F = 768
FC = F // 128
SLOT = 128
BANK = 512
D_IN = 384
D_ST = 64
M_HEADS = 6
KCONV = 4
PADSEQ = SEQ + KCONV - 1
ROW = D + 2
NO_ROW = 4096
NEG = -1e30


def expert_tiles(experts, assignments):
    return (assignments + experts * (SLOT - 1)) // SLOT


class Stage:

    def __init__(self, nc, name):
        self.nc, self.name, self.stack = nc, name, ExitStack()

    def __enter__(self):
        self.stack.__enter__()
        return self

    def __exit__(self, *a):
        return self.stack.__exit__(*a)

    def sb(self, name, shape, dt=F32):
        return self.stack.enter_context(self.nc.sbuf_tensor(f"{self.name}_{name}", shape, dt))

    def ps(self, name, shape, dt=F32):
        return self.stack.enter_context(self.nc.psum_tensor(f"{self.name}_{name}", shape, dt))

    def sem(self, name):
        return self.nc.alloc_semaphore(f"{self.name}_{name}")


class Step:

    def __init__(self, sem):
        self.sem, self.n = sem, 0

    def add(self, ins):
        ins.then_inc(self.sem, 1)
        self.n += 1
        return self.n


def link(eng, step, ins):
    eng.wait_ge(step.sem, step.add(ins))


def bcast(ap, axis, n):
    a = ap.unsqueeze(axis)
    shape = list(a.shape)
    shape[axis] = n
    return a.broadcast_to(shape)


def stem_stage(nc, K, W, h, samp, off_dram, all_near, fetch_more):
    NCH = 2 * IMAGES
    with Stage(nc, "stem") as s:
        im2col = samp[:].rearrange("p a b -> p (a b)")[:, 0:IMAGES // 2 * PIX]
        tmp = s.sb("tmp", [C1, 3, HALF])
        offs = s.sb("offs", [32, IMAGES, POS])
        ps = s.ps("ps", [C1, 4, BANK])
        pso = s.ps("pso", [128, BANK])
        psum4 = s.ps("psum4", [32, BANK])
        parts = s.sb("parts", [128, 8 * POS])
        starts = [0, 1, 2, 4, IMAGES // 2]
        x_in = [s.sem(f"x_in{i}") for i in range(4)]
        off_part, off_kept = s.sem("off_part"), s.sem("off_kept")
        near = s.sb("near", [32, 8 * POS])
        near_n = s.sb("near_n", [32, 2])
        psn = s.ps("psn", [1, BANK])
        near_ready, near_summed, near_out = s.sem("near_ready"), s.sem("near_summed"), s.sem("near_out")
        vec = Step(s.sem("vec"))
        var_ready, rstd_ready, bn_ready = s.sem("var_ready"), s.sem("rstd_ready"), s.sem("bn_ready")
        conv_ready, scaled, leaky = s.sem("conv_ready"), s.sem("scaled"), s.sem("leaky")
        off_ready, off_based, off_out = s.sem("off_ready"), s.sem("off_based"), s.sem("off_out")
        cv, bnv = W["chan"], W["bnv"]
        with nc.Block() as block:
            @block.sync
            def _(sp):
                for i in range(4):
                    c = slice(starts[i] * PIX, starts[i + 1] * PIX)
                    sp.dma_start(im2col[:, c], K["x"][:, c]).then_inc(x_in[i], 16)
                fetch_more(sp)
                sp.wait_ge(off_based, 2)
                sp.dma_start(off_dram.rearrange("b c p -> c b p"), offs[:]).then_inc(off_out, 16)
                sp.wait_ge(off_out, 16)

            @block.gpsimd
            def _(pool):
                pool.wait_ge(var_ready, 1)
                nc.gpsimd.tensor_tensor(bnv[:, 0, :], bnv[:, 0, :], W["mhalf"][0:C1, 0:3], ALU.pow).then_inc(rstd_ready, 1)

            @block.tensor
            def _(pe):
                pe.wait_ge(W["sem"]["stem_w"], 16)
                for n in range(NCH):
                    if n < IMAGES and n % 2 == 0 and n // 2 in starts:
                        pe.wait_ge(x_in[starts.index(n // 2)], 16)
                    if n >= 4:
                        pe.wait_ge(scaled, n - 3)
                    nc.tensor.matmul(ps[:, n % 4, 0:HALF], W["stem_w"][:, n // IMAGES, :],
                                     im2col[:, n % IMAGES * HALF:(n % IMAGES + 1) * HALF],
                                     start=True, stop=True).then_inc(conv_ready, 1)
                for name in ("off_w", "stack4"):
                    pe.wait_ge(W["sem"][name], 16)
                for half in range(2):
                    pe.wait_ge(leaky, (half + 1) * NCH // 2)
                    grid = h[:, half * 8:(half + 1) * 8, :].rearrange(
                        "p b (i r j s) -> p b i r j s", i=OUT_SIDE, r=4, j=OUT_SIDE)
                    if half:
                        pe.wait_ge(off_part, 1)
                    for tap in range(TAPS):
                        q = 32 * (tap % 4)
                        mm = nc.tensor.matmul(pso[q:q + 32, 0:8 * POS].rearrange("p (b i j) -> p b i j", b=8, i=OUT_SIDE),
                                              W["off_w"][:, tap, :], grid[:, :, :, tap // 4, :, tap % 4],
                                              start=tap < 4, stop=tap >= TAPS - 4)
                    mm.then_inc(off_ready, 1)
                    pe.wait_ge(off_part, half + 1)
                    if half:
                        pe.wait_ge(near_ready, 1)
                    nc.tensor.matmul(psum4[:, 0:8 * POS], W["stack4"][:], parts[:], start=True, stop=True).then_inc(off_kept, 1)
                pe.wait_ge(near_ready, 2)
                for half in range(2):
                    mm = nc.tensor.matmul(psn[:, 0:1], near_n[:, half:half + 1], W["ones"][0:32, 0:1], start=half == 0, stop=half == 1)
                mm.then_inc(near_summed, 1)

            @block.scalar
            def _(act):
                act.wait_ge(bn_ready, 1)
                for n in range(NCH):
                    act.wait_ge(conv_ready, n + 1)
                    if n >= 3:
                        act.wait_ge(leaky, n - 2)
                    nc.scalar.activation(tmp[:, n % 3, :], ps[:, n % 4, 0:HALF], ACT.Identity,
                                         bias=bnv[:, 2, 0:1], scale=bnv[:, 1, 0:1]).then_inc(scaled, 1)
                for half in range(2):
                    act.wait_ge(off_ready, half + 1)
                    if half:
                        act.wait_ge(off_kept, 1)
                    nc.scalar.copy(parts[:], pso[:, 0:8 * POS]).then_inc(off_part, 1)

            @block.vector
            def _(dve):
                for name in ("chan", "tabs"):
                    dve.wait_ge(W["sem"][name], 16)
                nc.vector.memset(W["mhalf"][:], -0.5).then_inc(vec.sem, 1)
                vec.n += 1
                dve.wait_ge(vec.sem, vec.n)
                nc.vector.tensor_scalar(bnv[:, 0, :], cv[:, 3, :], 1e-5, None, ALU.add).then_inc(var_ready, 1)
                dve.wait_ge(rstd_ready, 1)
                link(dve, vec, nc.vector.tensor_tensor(bnv[:, 1, :], bnv[:, 0, :], cv[:, 0, :], ALU.mult))
                link(dve, vec, nc.vector.tensor_tensor(bnv[:, 2, :], cv[:, 4, :], cv[:, 2, :], ALU.subtract))
                link(dve, vec, nc.vector.tensor_tensor(bnv[:, 2, :], bnv[:, 2, :], bnv[:, 1, :], ALU.mult))
                nc.vector.tensor_tensor(bnv[:, 2, :], bnv[:, 2, :], cv[:, 1, :], ALU.add).then_inc(bn_ready, 1)
                for n in range(NCH):
                    dve.wait_ge(scaled, n + 1)
                    t = tmp[:, n % 3, :]
                    nc.vector.scalar_tensor_tensor(h[:, n // 2, (n % 2) * HALF:(n % 2 + 1) * HALF], t, 0.01, t,
                                                   ALU.mult, ALU.max).then_inc(leaky, 1)
                for half in range(2):
                    dve.wait_ge(off_kept, half + 1)
                    nc.vector.scalar_tensor_tensor(
                        offs[:, half * 8:(half + 1) * 8, :],
                        psum4[:, 0:8 * POS].rearrange("p (b q) -> p b q", b=8), W["tabs"][0:32, 8:9],
                        bcast(W["tabs"][0:32, 16:16 + POS], 1, 8), ALU.add, ALU.add).then_inc(off_based, 1)
                    link(dve, vec, nc.vector.tensor_scalar(near[:], psum4[:, 0:8 * POS], W["tabs"][0:32, 8:9], None, ALU.add))
                    link(dve, vec, nc.vector.tensor_tensor(near[:], near[:], near[:], ALU.mult))
                    link(dve, vec, nc.vector.tensor_scalar(near[:], near[:], float(ROWS) ** 2, None, ALU.is_lt))
                    nc.vector.tensor_reduce(near_n[:, half:half + 1], near[:], AX.X, ALU.add).then_inc(near_ready, 1)
                    if half == 0:
                        dve.wait_ge(near_ready, 1)
                dve.wait_ge(near_summed, 1)
                nc.vector.tensor_scalar(all_near[:], psn[:, 0:1], 32.0 * IMAGES * POS, None, ALU.is_ge).then_inc(near_out, 1)
                dve.wait_ge(near_out, 1)


def sampling_stage(nc, K, W, h, samp, off_dram):
    RING = 4
    with Stage(nc, "smp") as s:
        pxy = s.sb("pxy", [CHUNK, 2, 2, PIX])
        xw = s.sb("xw", [CHUNK, 2, PIX])
        dist = s.sb("dist", [CHUNK, 2, PIX])
        rest = s.sb("rest", [CHUNK, PIX])
        S = s.sb("S", [CHUNK, RING, PIX])
        hT = s.sb("hT", [CHUNK, 2, CHUNKS, C1])
        psT = s.ps("psT", [CHUNK, 2, BANK])
        acc = s.ps("acc", [C1, 2, 2, BANK])
        loaded = [s.sem(f"loaded{i}") for i in range(2)]
        turned, hT_ready = s.sem("turned"), s.sem("hT_ready")
        dist_ready, S_ready, S_used = s.sem("dist_ready"), s.sem("S_ready"), s.sem("S_used")
        rest_ready, dist_used = s.sem("rest_ready"), s.sem("dist_used")
        sampled, kept = s.sem("sampled"), s.sem("kept")
        xlink = Step(s.sem("xlink"))
        tabs = W["tabs"]
        PER = CHUNKS + 1
        with nc.Block() as block:
            @block.sync
            def _(sp):
                for b in range(IMAGES):
                    if b >= 2:
                        sp.wait_ge(dist_ready, (b - 1) * PER)
                    sp.dma_start(pxy[:, b % 2, :, :].rearrange("p a q -> p (a q)"),
                                 off_dram[b].rearrange("c p -> (c p)").partition_broadcast(CHUNK)).then_inc(loaded[b % 2], 16)

            @block.tensor
            def _(pe):
                def turn(b):
                    if b >= 1:
                        pe.wait_ge(hT_ready, b * 2)
                    for c in range(CHUNKS):
                        mm = nc.tensor.transpose(psT[:, c // 4, (c % 4) * C1:(c % 4 + 1) * C1],
                                                 h[:, b, c * CHUNK:(c + 1) * CHUNK], W["ident"][0:C1, 0:C1])
                    mm.then_inc(turned, 1)

                pe.wait_ge(W["sem"]["ident"], 16)
                turn(0)
                for b in range(IMAGES):
                    if b + 1 < IMAGES:
                        turn(b + 1)
                    pe.wait_ge(hT_ready, 2 * (b + 1))
                    if b >= 2:
                        pe.wait_ge(kept, 2 * (b - 1))
                    for c in range(CHUNKS):
                        n = b * CHUNKS + c
                        pe.wait_ge(S_ready, n + 1)
                        for half in range(2):
                            mm = nc.tensor.matmul(acc[:, b % 2, half, 0:HALF], hT[:, b % 2, c, :],
                                                  S[:, n % RING, half * HALF:(half + 1) * HALF],
                                                  start=c == 0, stop=c == CHUNKS - 1)
                        mm.then_inc(S_used, 1)

            @block.scalar
            def _(act):
                def keep(b):
                    act.wait_ge(S_used, (b + 1) * CHUNKS)
                    for half in range(2):
                        nc.scalar.copy(samp[:, half * 8:(half + 1) * 8, b * POS:(b + 1) * POS],
                                       acc[:, b % 2, half, 0:HALF].rearrange("p (k q) -> p k q", k=8)).then_inc(kept, 1)

                def turned_back(b):
                    act.wait_ge(turned, b + 1)
                    if b >= 2:
                        act.wait_ge(S_used, (b - 1) * CHUNKS)
                    nc.scalar.copy(hT[:, b % 2, 0:4, :], psT[:, 0, 0:4 * C1].rearrange("p (c n) -> p c n", c=4)).then_inc(hT_ready, 1)
                    nc.scalar.copy(hT[:, b % 2, 4:7, :], psT[:, 1, 0:3 * C1].rearrange("p (c n) -> p c n", c=3)).then_inc(hT_ready, 1)

                turned_back(0)
                for b in range(IMAGES):
                    act.wait_ge(loaded[b % 2], 16 * (b // 2 + 1))
                    for j in range(PER):
                        n = b * PER + j
                        if n >= 2:
                            act.wait_ge(dist_used, n - 1)
                        axis, col = (1, 7) if j == 0 else (0, j - 1)
                        nc.scalar.activation(dist[:, n % 2, :], pxy[:, b % 2, axis, :], ACT.Abs,
                                             bias=tabs[0:CHUNK, col:col + 1], scale=1.0).then_inc(dist_ready, 1)
                        if j == 3 and b + 1 < IMAGES:
                            turned_back(b + 1)
                        if j == 4 and b >= 1:
                            keep(b - 1)
                keep(IMAGES - 1)

            @block.vector
            def _(dve):
                for b in range(IMAGES):
                    for j in range(PER):
                        n = b * PER + j
                        dve.wait_ge(dist_ready, n + 1)
                        d = dist[:, n % 2, :]
                        dst = xw[:, b % 2, :] if j == 0 else rest[:, :]
                        nc.vector.tensor_scalar(dst, d, -1.0, 1.0, ALU.mult, ALU.add).then_inc(dist_used, 1)
                        dve.wait_ge(dist_used, n + 1)
                        if j == 0:
                            link(dve, xlink, nc.vector.tensor_scalar(dst, dst, 0.0, None, ALU.max))
                        else:
                            m = b * CHUNKS + j - 1
                            if m >= RING:
                                dve.wait_ge(S_used, m - RING + 1)
                            nc.vector.scalar_tensor_tensor(S[:, m % RING, :], rest[:, :], 0.0, xw[:, b % 2, :],
                                                           ALU.max, ALU.mult).then_inc(S_ready, 1)
                            dve.wait_ge(S_ready, m + 1)


def near_sampling_stage(nc, K, W, h, samp, off_dram, hc):
    GROUP = 4
    PART = 2 * TAPS // GROUP
    RING = 6
    near = lambda c: range(max(c - 1, 0), min(c + 2, CHUNKS))
    cols = lambda c: slice(near(c)[0] * OUT_SIDE, (near(c)[-1] + 1) * OUT_SIDE)
    with Stage(nc, "nsm") as s:
        pxy = s.sb("pxy", [CHUNK, 3, 2, TAPS, POS])
        xw = s.sb("xw", [CHUNK, 2, TAPS, POS])
        xdist = s.sb("xdist", [CHUNK, TAPS, POS])
        dist = s.sb("dist", [CHUNK, 4, TAPS, 3 * OUT_SIDE])
        rest = s.sb("rest", [CHUNK, 3, TAPS, 3 * OUT_SIDE])
        S = s.sb("S", [CHUNK, RING, TAPS, 3 * OUT_SIDE])
        hT = s.sb("hT", [CHUNK, 2, CHUNKS, C1])
        psT = s.ps("psT", [CHUNK, 2, BANK])
        acc = s.ps("acc", [C1, 2, 2, BANK])
        psD = s.ps("psD", [C1, 2, BANK])
        tmp = s.sb("tmp", [C1, 2, GROUP * POS])
        row = TAPS * OUT_SIDE
        loaded = [s.sem(f"loaded{i}") for i in range(3)]
        turned, hT_act, hT_dve = s.sem("turned"), s.sem("hT_act"), s.sem("hT_dve")
        xdist_ready, xrest_ready, xw_ready = s.sem("xdist_ready"), s.sem("xrest_ready"), s.sem("xw_ready")
        dist_ready, rest_ready, S_ready, row_done, kept = (
            s.sem(x) for x in ("dist_ready", "rest_ready", "S_ready", "row_done", "kept"))
        mm_ready, scaled, leaky = s.sem("mm_ready"), s.sem("scaled"), s.sem("leaky")
        tabs = W["tabs"]
        with nc.Block() as block:
            @block.sync
            def _(sp):
                for b in range(IMAGES):
                    if b >= 3:
                        sp.wait_ge(dist_ready, (b - 2) * CHUNKS)
                        sp.wait_ge(xdist_ready, b - 2)
                    sp.dma_start(pxy[:, b % 3].rearrange("p a k q -> p (a k q)"),
                                 off_dram[b].rearrange("c p -> (c p)").partition_broadcast(CHUNK)).then_inc(loaded[b % 3], 16)

            @block.tensor
            def _(pe):
                def turn(b):
                    if b >= 1:
                        pe.wait_ge(hT_act, b)
                        pe.wait_ge(hT_dve, b)
                    for c in range(CHUNKS):
                        mm = nc.tensor.transpose(psT[:, c // 4, (c % 4) * C1:(c % 4 + 1) * C1],
                                                 h[:, b, c * CHUNK:(c + 1) * CHUNK], W["ident"][0:C1, 0:C1])
                    mm.then_inc(turned, 1)

                def patch(g, first, last):
                    pe.wait_ge(kept, 2 * GROUP * (g + 1))
                    for n in range(first, last):
                        m, tap = n // TAPS, n % TAPS
                        if tap == 0 and g:
                            pe.wait_ge(scaled, 2 * (g - 1) + m + 1)
                        mm = nc.tensor.matmul(psD[:, m, 0:GROUP * POS], W["dcn_w"][:, tap, m * HD:(m + 1) * HD],
                                              samp[:, tap, g * GROUP * POS:(g + 1) * GROUP * POS], start=tap == 0, stop=tap == TAPS - 1)
                        if tap == TAPS - 1:
                            mm.then_inc(mm_ready, 1)

                for name in ("ident", "dcn_w"):
                    pe.wait_ge(W["sem"][name], 16)
                turn(0)
                for b in range(IMAGES):
                    if b + 1 < IMAGES:
                        turn(b + 1)
                    pe.wait_ge(hT_act, b + 1)
                    pe.wait_ge(hT_dve, b + 1)
                    if b >= 2:
                        pe.wait_ge(kept, 2 * (b - 1))
                    for i in range(OUT_SIDE):
                        pe.wait_ge(S_ready, b * CHUNKS + near(i)[-1] + 1)
                        for c in near(i):
                            q = (i - near(c)[0]) * OUT_SIDE
                            mm = nc.tensor.matmul(acc[:, b % 2, i // 4, (i % 4) * row:(i % 4 + 1) * row], hT[:, b % 2, c, :],
                                                  S[:, (b * CHUNKS + c) % RING, :, q:q + OUT_SIDE],
                                                  start=c == near(i)[0], stop=c == near(i)[-1])
                        mm.then_inc(row_done, 1)
                        if b >= GROUP:
                            n = b % GROUP * PART
                            patch(b // GROUP - 1, n + PART * i // OUT_SIDE, n + PART * (i + 1) // OUT_SIDE)
                patch(IMAGES // GROUP - 1, 0, 2 * TAPS)

            @block.scalar
            def _(act):
                def keep(b, half):
                    rows = 4 - half
                    act.wait_ge(row_done, b * CHUNKS + 4 + 3 * half)
                    nc.scalar.copy(samp[:, :, b * POS + 4 * half * OUT_SIDE:b * POS + (4 * half + rows) * OUT_SIDE].rearrange("p k (i j) -> p i k j", i=rows),
                                   acc[:, b % 2, half, 0:rows * row].rearrange("p (i k j) -> p i k j", i=rows, k=TAPS)).then_inc(kept, 1)

                def turned_back(b):
                    act.wait_ge(turned, b + 1)
                    if b >= 2:
                        act.wait_ge(row_done, (b - 1) * CHUNKS)
                    nc.scalar.copy(hT[:, b % 2, 0:4, :], psT[:, 0, 0:4 * C1].rearrange("p (c n) -> p c n", c=4)).then_inc(hT_act, 1)

                def xpart(b):
                    act.wait_ge(loaded[b % 3], 16 * (b // 3 + 1))
                    if b >= 1:
                        act.wait_ge(xw_ready, b)
                    nc.scalar.activation(xdist[:], pxy[:, b % 3, 1], ACT.Abs, bias=tabs[0:CHUNK, 7:8], scale=1.0).then_inc(xdist_ready, 1)

                turned_back(0)
                xpart(0)
                for b in range(IMAGES):
                    for c in range(CHUNKS):
                        n = b * CHUNKS + c
                        if n >= 4:
                            act.wait_ge(rest_ready, n - 3)
                        w = cols(c)
                        nc.scalar.activation(dist[:, n % 4, :, 0:w.stop - w.start], pxy[:, b % 3, 0, :, w], ACT.Abs,
                                             bias=tabs[0:CHUNK, c:c + 1], scale=1.0).then_inc(dist_ready, 1)
                        if c == 1 and b + 1 < IMAGES:
                            xpart(b + 1)
                        if c == 5 and b + 1 < IMAGES:
                            turned_back(b + 1)
                        if c == 5 and b >= 1:
                            keep(b - 1, 0)
                        if c == 6 and b >= 1:
                            keep(b - 1, 1)
                keep(IMAGES - 1, 0)
                keep(IMAGES - 1, 1)

            @block.gpsimd
            def _(pool):
                for b in range(IMAGES):
                    pool.wait_ge(xdist_ready, b + 1)
                    if b >= 2:
                        pool.wait_ge(S_ready, (b - 1) * CHUNKS)
                    nc.gpsimd.tensor_scalar(xw[:, b % 2], xdist[:], -1.0, 1.0, ALU.mult, ALU.add).then_inc(xrest_ready, 1)
                    pool.wait_ge(xrest_ready, b + 1)
                    nc.gpsimd.tensor_scalar(xw[:, b % 2], xw[:, b % 2], 0.0, None, ALU.max).then_inc(xw_ready, 1)

            @block.vector
            def _(dve):
                def turned_back(b):
                    dve.wait_ge(turned, b + 1)
                    if b >= 2:
                        dve.wait_ge(row_done, (b - 1) * CHUNKS)
                    nc.vector.tensor_copy(hT[:, b % 2, 4:7, :], psT[:, 1, 0:3 * C1].rearrange("p (c n) -> p c n", c=3)).then_inc(hT_dve, 1)

                def remainder(n):
                    c = n % CHUNKS
                    w = cols(c).stop - cols(c).start
                    dve.wait_ge(dist_ready, n + 1)
                    if n >= 3:
                        dve.wait_ge(S_ready, n - 2)
                    nc.vector.tensor_scalar(rest[:, n % 3, :, 0:w], dist[:, n % 4, :, 0:w], -1.0, 1.0, ALU.mult, ALU.add).then_inc(rest_ready, 1)

                def activate(j):
                    g, m = j // 2, j % 2
                    dve.wait_ge(mm_ready, j + 1)
                    nc.vector.tensor_scalar(tmp[:, m, :], psD[:, m, 0:GROUP * POS], W["bnv"][:, 1, 1 + m:2 + m], W["bnv"][:, 2, 1 + m:2 + m],
                                            ALU.mult, ALU.add).then_inc(scaled, 1)
                    dve.wait_ge(scaled, j + 1)
                    v = tmp[:, m, :].rearrange("p (b q) -> p b q", b=GROUP)
                    nc.vector.scalar_tensor_tensor(hc[:, m, g * GROUP:(g + 1) * GROUP, 1:SEQ], v, 0.01, v, ALU.mult, ALU.max).then_inc(leaky, 1)
                    dve.wait_ge(leaky, j + 1)

                turned_back(0)
                remainder(0)
                remainder(1)
                for n in range(IMAGES * CHUNKS):
                    b, c = n // CHUNKS, n % CHUNKS
                    if n + 2 < IMAGES * CHUNKS:
                        remainder(n + 2)
                    if c == 0:
                        dve.wait_ge(xw_ready, b + 1)
                    if n >= RING:
                        dve.wait_ge(row_done, min(n - RING + 1, (n - RING) // CHUNKS * CHUNKS + CHUNKS - 1) + 1)
                    dve.wait_ge(rest_ready, n + 1)
                    w = cols(c)
                    nc.vector.scalar_tensor_tensor(S[:, n % RING, :, 0:w.stop - w.start], rest[:, n % 3, :, 0:w.stop - w.start], 0.0,
                                                   xw[:, b % 2, :, w], ALU.max, ALU.mult).then_inc(S_ready, 1)
                    if c == 4 and b + 1 < IMAGES:
                        turned_back(b + 1)
                    if c == 5 and b > GROUP and b % 2 == 0:
                        activate(b // 2 - GROUP // 2 - 1)
                for j in range((IMAGES - GROUP) // 2 - 1, 2 * IMAGES // GROUP):
                    activate(j)


def patch_stage(nc, K, W, samp, hc):
    with Stage(nc, "dcn") as s:
        tmp = s.sb("tmp", [C1, 4, HALF])
        ps = s.ps("ps", [C1, 4, BANK])
        mm_ready, scaled, leaky = s.sem("mm_ready"), s.sem("scaled"), s.sem("leaky")
        with nc.Block() as block:
            @block.tensor
            def _(pe):
                pe.wait_ge(W["sem"]["dcn_w"], 16)
                for n in range(4):
                    half, m = n // 2, n % 2
                    for tap in range(TAPS):
                        mm = nc.tensor.matmul(ps[:, n, 0:HALF], W["dcn_w"][:, tap, m * HD:(m + 1) * HD],
                                              samp[:, tap, half * HALF:(half + 1) * HALF],
                                              start=tap == 0, stop=tap == TAPS - 1)
                    mm.then_inc(mm_ready, 1)

            @block.scalar
            def _(act):
                for n in range(4):
                    act.wait_ge(mm_ready, n + 1)
                    m = n % 2
                    nc.scalar.activation(tmp[:, n, :], ps[:, n, 0:HALF], ACT.Identity,
                                         bias=W["bnv"][:, 2, 1 + m:2 + m], scale=W["bnv"][:, 1, 1 + m:2 + m]).then_inc(scaled, 1)

            @block.vector
            def _(dve):
                for n in range(4):
                    half, m = n // 2, n % 2
                    dve.wait_ge(scaled, n + 1)
                    t = tmp[:, n, :].rearrange("p (b q) -> p b q", b=8)
                    nc.vector.scalar_tensor_tensor(hc[:, m, half * 8:(half + 1) * 8, 1:SEQ], t, 0.01, t,
                                                   ALU.mult, ALU.max).then_inc(leaky, 1)


def token_stage(nc, W, hc, H):
    with Stage(nc, "tok") as s:
        psT = s.ps("psT", [PAIR, 4, BANK])
        cls, turned, kept, kept_v = s.sem("cls"), s.sem("turned"), s.sem("kept"), s.sem("kept_v")
        with nc.Block() as block:
            @block.tensor
            def _(pe):
                pe.wait_ge(W["sem"]["ident"], 16)
                pe.wait_ge(cls, 1)
                for t in range(TILES):
                    for m in range(2):
                        mm = nc.tensor.transpose(psT[:, t // 2, (t % 2) * D + m * HD:(t % 2) * D + (m + 1) * HD],
                                                 hc[:, m, 2 * t:2 * t + 2, :].rearrange("p b q -> p (b q)"), W["ident"][0:HD, 0:HD])
                    mm.then_inc(turned, 1)

            @block.scalar
            def _(act):
                for j in (0, 2):
                    act.wait_ge(turned, 2 * j + 2)
                    nc.scalar.copy(H[:, 2 * j:2 * j + 2, :], psT[:, j, 0:2 * D].rearrange("p (t d) -> p t d", t=2)).then_inc(kept, 1)

            @block.vector
            def _(dve):
                dve.wait_ge(W["sem"]["chan"], 16)
                nc.vector.tensor_copy(hc[:, :, :, 0], bcast(W["chan"][:, 5, 0:2], 2, IMAGES)).then_inc(cls, 1)
                for j in (1, 3):
                    dve.wait_ge(turned, 2 * j + 2)
                    nc.vector.tensor_copy(H[:, 2 * j:2 * j + 2, :], psT[:, j, 0:2 * D].rearrange("p (t d) -> p t d", t=2)).then_inc(kept_v, 1)


class Turn:

    def __init__(self, nc, W, s, src, dst, gain=None, shift=None, ready=None):
        self.nc, self.W, self.src, self.dst, self.gain, self.shift = nc, W, src, dst, gain, shift
        self.ps = s.ps("psT", [HD, 4, BANK])
        self.normed, self.turned, self.kept = s.sem("normed"), s.sem("turned"), s.sem("kept")
        self.ready = ready or [(self.normed, 4), (self.normed, 8)]

    def half_on_tensor(self, pe, g):
        nc = self.nc
        sem, value = self.ready[g]
        pe.wait_ge(sem, value)
        for m in range(2):
            for i in range(4):
                mm = nc.tensor.transpose(self.ps[:, 2 * g + m, i * PAIR:(i + 1) * PAIR],
                                         self.src[:, 4 * g + i, m * HD:(m + 1) * HD], self.W["ident"][0:PAIR, 0:PAIR])
            mm.then_inc(self.turned, 1)

    def on_tensor(self, pe):
        pe.wait_ge(self.W["sem"]["ident"], 16)
        for g in range(2):
            self.half_on_tensor(pe, g)

    def on_scalar(self, act):
        nc = self.nc
        if self.gain is not None:
            act.wait_ge(self.W["sem"]["lncol"], 16)
        for g in range(2):
            for m in range(2):
                act.wait_ge(self.turned, 2 * g + m + 1)
                dst, src = self.dst[:, m, g * HALF_TOK:(g + 1) * HALF_TOK], self.ps[:, 2 * g + m, 0:HALF_TOK]
                if self.gain is None:
                    nc.scalar.copy(dst, src).then_inc(self.kept, 1)
                elif self.shift is None:
                    nc.scalar.activation(dst, src, ACT.Copy, scale=self.gain[:, m:m + 1]).then_inc(self.kept, 1)
                else:
                    nc.scalar.activation(dst, src, ACT.Identity, bias=self.shift[:, m:m + 1], scale=self.gain[:, m:m + 1]).then_inc(self.kept, 1)


def norm_stage(nc, W, name, norms, dst, gain=None, shift=None, on_sync=None, ones=None):
    with Stage(nc, name) as s:
        levels = len(norms)
        stat = s.sb("stat", [PAIR, TILES, 6])
        mv = s.sb("mv", [PAIR, TILES, 2])
        sq = s.sb("sq", [PAIR, TILES])
        rstd = s.sb("rstd", [PAIR, levels, TILES])
        vec, half_done = Step(s.sem("vec")), [s.sem(f"half_done{g}") for g in range(2)]
        var_ready, rstd_ready, ones_ready = s.sem("var_ready"), s.sem("rstd_ready"), s.sem("ones_ready")
        turn = Turn(nc, W, s, norms[-1][1], dst, gain, shift)
        order = [(lev, g) for lev in range(levels) for g in range(2)]
        with nc.Block() as block:
            if on_sync is not None:
                block.sync(on_sync)
            block.tensor(turn.on_tensor)
            block.scalar(turn.on_scalar)

            @block.vector
            def _(dve):
                def statistics(lev, g):
                    src, _, eps, rms = norms[lev]
                    i = slice(4 * g, 4 * g + 4)
                    if lev:
                        dve.wait_ge(half_done[g], 4 * lev)
                    for t in range(4 * g, 4 * g + 4):
                        vec.add(nc.vector.bn_stats(stat[:, t, :], src[:, t, :]))
                    dve.wait_ge(vec.sem, vec.n)
                    for t in range(4 * g, 4 * g + 4):
                        vec.add(nc.vector.bn_aggr(mv[:, t, :], stat[:, t, :]))
                    dve.wait_ge(vec.sem, vec.n)
                    if rms:
                        link(dve, vec, nc.vector.tensor_tensor(sq[:, i], mv[:, i, 0], mv[:, i, 0], ALU.mult))
                        link(dve, vec, nc.vector.tensor_tensor(sq[:, i], sq[:, i], mv[:, i, 1], ALU.add))
                        nc.vector.tensor_scalar(sq[:, i], sq[:, i], eps, None, ALU.add).then_inc(var_ready, 1)
                    else:
                        nc.vector.tensor_scalar(sq[:, i], mv[:, i, 1], eps, None, ALU.add).then_inc(var_ready, 1)

                def normalise(lev, g):
                    src, out, _, rms = norms[lev]
                    dve.wait_ge(rstd_ready, order.index((lev, g)) + 1)
                    for t in range(4 * g, 4 * g + 4):
                        if rms:
                            ins = nc.vector.tensor_scalar(out[:, t, :], src[:, t, :], rstd[:, lev, t:t + 1], None, ALU.mult)
                        else:
                            ins = nc.vector.tensor_scalar(out[:, t, :], src[:, t, :], mv[:, t, 0:1], rstd[:, lev, t:t + 1],
                                                          ALU.subtract, ALU.mult)
                        ins.then_inc(turn.normed if lev == levels - 1 else half_done[g], 1)

                statistics(0, 0)
                statistics(0, 1)
                for lev in range(levels):
                    for g in range(2):
                        normalise(lev, g)
                        if lev + 1 < levels:
                            statistics(lev + 1, g)

            @block.gpsimd
            def _(pool):
                if ones is not None:
                    nc.gpsimd.memset(ones, 1.0).then_inc(ones_ready, 1)
                    pool.wait_ge(ones_ready, 1)
                for n, (lev, g) in enumerate(order):
                    i = slice(4 * g, 4 * g + 4)
                    pool.wait_ge(var_ready, n + 1)
                    nc.gpsimd.tensor_tensor(rstd[:, lev, i], sq[:, i], W["mhalf"][0:PAIR, i], ALU.pow).then_inc(rstd_ready, 1)


def global_norm_stage(nc, W, name, src, dst, dst_turned=None, gain_turned=None, shift_turned=None, gain=None, add_to=None, y_dram=None):
    N = TOK * D
    with Stage(nc, name) as s:
        y = s.sb("y", [PAIR, TILES, 2, D]) if y_dram is not None else None
        stat = s.sb("stat", [PAIR, TILES, 6])
        mv = s.sb("mv", [PAIR, 2])
        m = s.sb("m", [PAIR, 4])
        ps = s.ps("ps", [PAIR, 2, BANK])
        vec = Step(s.sem("vec"))
        mean_in, mean_out, var_in, var_out = (s.sem(x) for x in ("mean_in", "mean_out", "var_in", "var_out"))
        sq_ready, rstd_ready = s.sem("sq_ready"), s.sem("rstd_ready")
        got = [s.sem(f"got{i}") for i in range(2)]
        turn = Turn(nc, W, s, dst, dst_turned, gain_turned, shift_turned) if dst_turned is not None else None
        with nc.Block() as block:
            if y is not None:
                @block.sync
                def _(sp):
                    for half in range(2):
                        t = slice(4 * half, 4 * half + 4)
                        sp.dma_start(y[:, t].rearrange("p t r d -> p t (r d)"),
                                     y_dram.rearrange("(t p r) d -> p t (r d)", p=PAIR, r=2)[:, t]).then_inc(got[half], 16)

            if turn is not None:
                block.scalar(turn.on_scalar)

            @block.tensor
            def _(pe):
                pe.wait_ge(mean_in, 1)
                nc.tensor.matmul(ps[:, 0, 0:1], W["ones"][0:PAIR, 0:PAIR], mv[:, 0:1], start=True, stop=True).then_inc(mean_out, 1)
                pe.wait_ge(var_in, 1)
                nc.tensor.matmul(ps[:, 1, 0:1], W["ones"][0:PAIR, 0:PAIR], m[:, 2:3], start=True, stop=True).then_inc(var_out, 1)
                if turn is not None:
                    turn.on_tensor(pe)

            @block.gpsimd
            def _(pool):
                pool.wait_ge(sq_ready, 1)
                nc.gpsimd.tensor_tensor(m[:, 3:4], m[:, 1:2], W["mhalf"][0:PAIR, 0:1], ALU.pow).then_inc(rstd_ready, 1)

            @block.vector
            def _(dve):
                for half in range(2):
                    t4 = slice(4 * half, 4 * half + 4)
                    if y is not None:
                        dve.wait_ge(got[half], 16)
                        for r in range(2):
                            link(dve, vec, nc.vector.tensor_tensor(src[:, t4, :], src[:, t4, :], y[:, t4, r, :], ALU.add))
                    for t in range(4 * half, 4 * half + 4):
                        vec.add(nc.vector.bn_stats(stat[:, t, :], src[:, t, :]))
                dve.wait_ge(vec.sem, vec.n)
                nc.vector.bn_aggr(mv[:], stat[:].rearrange("p t c -> p (t c)")).then_inc(mean_in, 1)
                dve.wait_ge(mean_out, 1)
                link(dve, vec, nc.vector.tensor_scalar(m[:, 0:1], ps[:, 0, 0:1], 1.0 / PAIR, None, ALU.mult))
                link(dve, vec, nc.vector.tensor_tensor(m[:, 1:2], mv[:, 0:1], m[:, 0:1], ALU.subtract))
                link(dve, vec, nc.vector.tensor_tensor(m[:, 1:2], m[:, 1:2], m[:, 1:2], ALU.mult))
                nc.vector.tensor_tensor(m[:, 2:3], mv[:, 1:2], m[:, 1:2], ALU.add).then_inc(var_in, 1)
                dve.wait_ge(var_out, 1)
                nc.vector.tensor_scalar(m[:, 1:2], ps[:, 1, 0:1], N / (N - 1.0) / PAIR, 1e-12, ALU.mult, ALU.add).then_inc(sq_ready, 1)
                if turn is not None:
                    dve.wait_ge(rstd_ready, 1)
                    for t in range(TILES):
                        nc.vector.tensor_scalar(dst[:, t, :], src[:, t, :], m[:, 0:1], m[:, 3:4], ALU.subtract, ALU.mult).then_inc(turn.normed, 1)
                else:
                    for t in range(TILES):
                        vec.add(nc.vector.scalar_tensor_tensor(dst[:, t, :], src[:, t, :], m[:, 0:1], gain, ALU.subtract, ALU.mult))
                    dve.wait_ge(vec.sem, vec.n)
                    dve.wait_ge(rstd_ready, 1)
                    for t in range(TILES):
                        vec.add(nc.vector.scalar_tensor_tensor(add_to[:, t, :], dst[:, t, :], m[:, 3:4], add_to[:, t, :],
                                                               ALU.mult, ALU.add))


def product_stage(nc, W, name, products, weights, add=False, on_pool=None):
    with Stage(nc, name) as s:
        ps = s.ps("ps", [128, 8, BANK])
        ready, kept_a, kept_v = s.sem("ready"), s.sem("kept_a"), s.sem("kept_v")

        def bank(j, dst, row, col=0):
            free = dst.shape[1:]
            v = ps[row:row + dst.shape[0], j % 8, col:col + int(np.prod(free))]
            return v if len(free) == 1 else v.rearrange("p (a b) -> p a b", a=free[0])

        def by_act(j):
            return j % 2 == 0 and not add

        with nc.Block() as block:
            if on_pool is not None:
                block.gpsimd(on_pool)

            @block.tensor
            def _(pe):
                for w in weights:
                    pe.wait_ge(W["sem"][w], 16)
                for j, (results, terms) in enumerate(products):
                    if j >= 8 and by_act(j):
                        pe.wait_ge(kept_a, (j - 8) // 2 + 1)
                    elif j >= 8:
                        pe.wait_ge(kept_v, j - 7 if add else (j - 8) // 2 + 1)
                    order = [lo for lo, _, _ in terms]
                    for i, (lo, lhsT, rhs) in enumerate(terms):
                        m, n = int(np.prod(lhsT.shape[1:])), int(np.prod(rhs.shape[1:]))
                        mm = nc.tensor.matmul(ps[lo:lo + m, j % 8, 0:n], lhsT, rhs,
                                              start=lo not in order[:i], stop=lo not in order[i + 1:])
                    mm.then_inc(ready, 1)

            @block.scalar
            def _(act):
                for j, (results, _) in enumerate(products):
                    if by_act(j):
                        act.wait_ge(ready, j + 1)
                        for dst, row, bias, *part in results:
                            if part and part[0][1] is not None:
                                last = nc.scalar.activation(dst, bank(j, dst, row, part[0][0]), ACT.Copy, scale=part[0][1])
                            elif bias is None:
                                last = nc.scalar.copy(dst, bank(j, dst, row, part[0][0] if part else 0))
                            else:
                                last = nc.scalar.activation(dst, bank(j, dst, row), ACT.Identity, bias=bias, scale=1.0)
                        last.then_inc(kept_a, 1)

            @block.vector
            def _(dve):
                for j, (results, _) in enumerate(products):
                    if not by_act(j):
                        dve.wait_ge(ready, j + 1)
                        for dst, row, bias, *part in results:
                            if part and part[0][1] is not None:
                                last = nc.vector.tensor_scalar(dst, bank(j, dst, row, part[0][0]), part[0][1], None, ALU.mult)
                            elif part:
                                last = nc.vector.tensor_copy(dst, bank(j, dst, row, part[0][0]))
                            elif add:
                                last = nc.vector.tensor_tensor(dst, bank(j, dst, row), dst, ALU.add)
                            elif bias is None:
                                last = nc.vector.tensor_copy(dst, bank(j, dst, row))
                            else:
                                last = nc.vector.tensor_scalar(dst, bank(j, dst, row), bias, None, ALU.add)
                        last.then_inc(kept_v, 1)


def attention_core(nc, W, xT, QT, KT, V, zT, H):
    G, AHEAD, BUF = 3, 2, 4
    with Stage(nc, "att") as s:
        sc = s.sb("sc", [PAIR, BUF, HEADS, PAIR])
        pt = s.sb("pt", [PAIR, 2, HEADS, PAIR])
        mx = s.sb("mx", [PAIR, BUF, HEADS])
        sm = s.sb("sm", [PAIR, BUF, HEADS])
        psS = s.ps("psS", [PAIR, G, BANK])
        psP = s.ps("psP", [PAIR, G, BANK])
        psZ = s.ps("psZ", [128, 2, BANK])
        scores, masked, vec, shifted = s.sem("scores"), s.sem("masked"), Step(s.sem("vec")), s.sem("shifted")
        exps, rec, probs, turned, pt_ready = (s.sem(x) for x in ("exps", "rec", "probs", "turned", "pt_ready"))
        v_ready, v_kept, z_ready, z_kept = (s.sem(x) for x in ("v_ready", "v_kept", "z_ready", "z_kept"))

        OUT = 3 * PAIR

        def kept(t):
            return 3 * t + 2

        def staged(first, later):
            for t in range(TILES + AHEAD):
                if t < TILES:
                    first(t)
                if t >= AHEAD:
                    later(t - AHEAD)

        with nc.Block() as block:
            @block.tensor
            def _(pe):
                def score(t):
                    for g in range(G):
                        if t >= 1:
                            pe.wait_ge(masked, G * (t - 1) + g + 1)
                        for i in (0, 2):
                            hd = 4 * g + i
                            mm = nc.tensor.matmul(psS[:, g, i * PAIR:(i + 2) * PAIR].rearrange("p (h k) -> p h k", h=2),
                                                  QT[:, hd // 2, tokens(t)], KT[:, hd:hd + 2, tokens(t)], start=True, stop=True)
                        mm.then_inc(scores, 1)
                    if t > AHEAD:
                        pe.wait_ge(z_kept, kept(t - AHEAD - 1))
                    elif t >= 1:
                        pe.wait_ge(v_kept, 2 * t)
                    for j in range(2):
                        for k in range(2):
                            mm = nc.tensor.matmul(psZ[0:PAIR, j, 0:D_IN], xT[:, k, tokens(t)], W["wv"][:, k, j * D_IN:(j + 1) * D_IN],
                                                  start=k == 0, stop=k == 1)
                        mm.then_inc(v_ready, 1)

                def finish(t):
                    pe.wait_ge(probs, t + 1)
                    for g in range(G):
                        if t >= 1:
                            pe.wait_ge(pt_ready, G * (t - 1) + g + 1)
                        for i in range(4):
                            mm = nc.tensor.transpose(psP[:, g, i * PAIR:(i + 1) * PAIR], sc[:, t % BUF, 4 * g + i, :],
                                                     W["ident"][0:PAIR, 0:PAIR])
                        mm.then_inc(turned, 1)
                    pe.wait_ge(v_kept, 2 * min(t + AHEAD + 1, TILES))
                    if t >= 1:
                        pe.wait_ge(z_kept, kept(t - 1))
                    for hd in range(HEADS):
                        if hd % 4 == 0:
                            pe.wait_ge(pt_ready, G * t + hd // 4 + 1)
                        r, pr = 64 * (hd % 2), hd // 2
                        mm = nc.tensor.matmul(psZ[r:r + 64, pr // 3, (pr % 3) * PAIR:(pr % 3 + 1) * PAIR],
                                              V[:, t, hd * DH:(hd + 1) * DH], pt[:, t % 2, hd, :], start=True, stop=True)
                    if t >= 1:
                        mm = out(t - 1)
                    mm.then_inc(z_ready, 1)

                def out(t):
                    for p in range(6):
                        mm = nc.tensor.matmul(psZ[0:PAIR, 1, OUT:OUT + D], zT[:, p, tokens(t)], W["wo"][:, p, :], start=p == 0, stop=p == 5)
                    return mm

                for name in ("wv", "wo"):
                    pe.wait_ge(W["sem"][name], 16)
                staged(score, finish)
                pe.wait_ge(z_kept, kept(TILES - 1))
                out(TILES - 1).then_inc(z_ready, 1)

            @block.vector
            def _(dve):
                def open_(t):
                    b = t % BUF
                    for g in range(G):
                        dve.wait_ge(scores, G * t + g + 1)
                        if t >= BUF:
                            dve.wait_ge(turned, G * (t - BUF + 1))
                        nc.vector.tensor_tensor(sc[:, b, 4 * g:4 * g + 4, :],
                                                psS[:, g, 0:4 * PAIR].rearrange("p (h k) -> p h k", h=4),
                                                bcast(W["amask"][:], 1, 4), ALU.add).then_inc(masked, 1)
                    for j in range(2):
                        dve.wait_ge(v_ready, 2 * t + j + 1)
                        nc.vector.tensor_copy(V[:, t, j * D_IN:(j + 1) * D_IN], psZ[0:PAIR, j, 0:D_IN]).then_inc(v_kept, 1)
                    dve.wait_ge(masked, G * (t + 1))
                    link(dve, vec, nc.vector.tensor_reduce(mx[:, b, :], sc[:, b, :, :], AX.X, ALU.max))
                    nc.vector.tensor_scalar(mx[:, b, :], mx[:, b, :], -(DH ** -0.5), None, ALU.mult).then_inc(shifted, 1)

                def sums(t):
                    b = t % BUF
                    dve.wait_ge(exps, HEADS * (t + 1))
                    nc.vector.reciprocal(sm[:, b, :], sm[:, b, :]).then_inc(rec, 1)

                def keep(t):
                    dve.wait_ge(z_ready, t + 1)
                    for j in range(2):
                        nc.vector.tensor_tensor(zT[:, 3 * j:3 * j + 3, tokens(t)],
                                                psZ[:, j, 0:3 * PAIR].rearrange("p (h q) -> p h q", h=3),
                                                bcast(W["qkvb"][:, 2, 3 * j:3 * j + 3], 2, PAIR), ALU.add).then_inc(z_kept, 1)
                    if t >= 1:
                        add_out(t - 1)

                def add_out(t):
                    nc.vector.tensor_tensor(H[:, t, :], psZ[0:PAIR, 1, OUT:OUT + D], H[:, t, :], ALU.add).then_inc(z_kept, 1)

                dve.wait_ge(W["sem"]["amask"], 16)
                for t in range(TILES + AHEAD + 1):
                    if t > AHEAD:
                        keep(t - AHEAD - 1)
                    if t < TILES:
                        open_(t)
                    if 1 <= t <= TILES:
                        sums(t - 1)
                dve.wait_ge(z_ready, TILES + 1)
                add_out(TILES - 1)

            @block.gpsimd
            def _(pool):
                for t in range(TILES):
                    pool.wait_ge(rec, t + 1)
                    b = t % BUF
                    nc.gpsimd.tensor_tensor(sc[:, b, :, :], sc[:, b, :, :], bcast(sm[:, b, :], 2, PAIR),
                                            ALU.mult).then_inc(probs, 1)

            @block.scalar
            def _(act):
                def exp(t):
                    act.wait_ge(shifted, t + 1)
                    b = t % BUF
                    for hd in range(HEADS):
                        nc.scalar.activation(sc[:, b, hd, :], sc[:, b, hd, :], ACT.Exp, bias=mx[:, b, hd:hd + 1], scale=DH ** -0.5,
                                             accum_out=sm[:, b, hd:hd + 1]).then_inc(exps, 1)

                def keep(t):
                    for g in range(G):
                        act.wait_ge(turned, G * t + g + 1)
                        if t >= 2:
                            act.wait_ge(z_ready, t - 1)
                        nc.scalar.copy(pt[:, t % 2, 4 * g:4 * g + 4, :],
                                       psP[:, g, 0:4 * PAIR].rearrange("p (h k) -> p h k", h=4)).then_inc(pt_ready, 1)

                for t in range(TILES + AHEAD):
                    if t >= AHEAD:
                        keep(t - AHEAD)
                    if t < TILES:
                        exp(t)


def tokens(t):
    return slice(t * PAIR, (t + 1) * PAIR)


def attention_layer(nc, W, H):
    with Stage(nc, "at") as s:
        xn = s.sb("xn", [PAIR, TILES, D])
        xT = s.sb("xT", [HD, 2, TOK])
        QT = s.sb("QT", [128, 6, TOK])
        KT = s.sb("KT", [128, HEADS, TOK])
        zeroed = s.sem("zeroed")
        V = s.sb("V", [PAIR, TILES, HEADS * DH])
        zT = s.sb("zT", [128, 6, TOK])

        def zero_other_heads(pool):
            for hd in range(HEADS):
                r = 64 * (1 - hd % 2)
                nc.gpsimd.memset(KT[r:r + 64, hd, :], 0.0).then_inc(zeroed, 1)
            pool.wait_ge(zeroed, HEADS)
            pool.wait_ge(W["sem"]["rowb"], 16)
            nc.gpsimd.tensor_tensor(H[:], H[:], bcast(W["rowb"][:, 0:D], 1, TILES), ALU.add).then_inc(zeroed, 1)
            pool.wait_ge(zeroed, HEADS + 1)

        norm_stage(nc, W, "at_n", [(H, xn, 1e-5, False)], xT)
        prods = []
        for m in range(6):
            for g in range(2):
                c = slice(g * HALF_TOK, (g + 1) * HALF_TOK)
                w = slice(m * 128, (m + 1) * 128)
                prods.append(([(QT[:, m, c], 0, W["qkvb"][:, 0, m:m + 1])], [(0, W["wq"][:, k, w], xT[:, k, c]) for k in range(2)]))
                prods.append(([(KT[r:r + 64, 2 * m + r // 64, c], r, W["qkvb"][r:r + 64, 1, m:m + 1]) for r in (0, 64)],
                              [(0, W["wk"][:, k, w], xT[:, k, c]) for k in range(2)]))
        product_stage(nc, W, "at_p", prods, ["wq", "wk", "qkvb"], on_pool=zero_other_heads)
        attention_core(nc, W, xT, QT, KT, V, zT, H)


def channel_attention(nc, W, xT, X, a_dram, Y, YT):
    IN = 2
    with Stage(nc, "ca") as s:
        Q = s.sb("Q", [PAIR, IN, TILES, D])
        Kt = s.sb("K", [PAIR, TILES, D])
        VT = s.sb("VT", [HD, 2, TOK])
        sc = s.sb("sc", [HD, TILES, 4, HD])
        wT = s.sb("wT", [HD, TILES, 4, HD])
        mx = s.sb("mx", [HD, TILES, 4])
        sm = s.sb("sm", [HD, TILES, 4])
        A = s.sb("A", [HD, 2, IMAGES, SEQ])
        biased = s.sem("biased")
        only = W["iota"][0:PAIR, 82 + TILES:84 + TILES]
        prods = [([(Q[:, o, t, :], 0, None, (0, only[:, o:o + 1])) for o in range(IN)] + [(Kt[:, t, :], 0, None, (D, None))],
                  [(0, xT[:, 0, tokens(t)], W["w1"][:, 0, 0:2 * D]), (0, xT[0:HD, 1, tokens(t)], W["w1"][0:HD, 1, 0:2 * D])])
                 for t in range(TILES)]
        for m in range(2):
            for g in range(2):
                c = slice(g * HALF_TOK, (g + 1) * HALF_TOK)
                v = slice(2 * D + m * HD, 2 * D + (m + 1) * HD)
                prods.append(([(VT[:, m, c], 0, None)],
                              [(0, W["w1"][:, 0, v], xT[:, 0, c]), (0, W["w1"][0:HD, 1, v], xT[0:HD, 1, c])]))

        def bias(pool):
            nc.gpsimd.tensor_tensor(X[:], X[:], bcast(W["rowb"][:, D:2 * D], 1, TILES), ALU.add).then_inc(biased, 1)
            pool.wait_ge(biased, 1)

        product_stage(nc, W, "ca_p", prods, ["w1", "iota"], on_pool=bias)
        with Stage(nc, "cb") as p:
            psS = p.ps("psS", [HD, 3, BANK])
            psT = p.ps("psT", [HD, 2, BANK])
            psA = p.ps("psA", [HD, 2, BANK])
            scores, masked, vec = s.sem("scores"), s.sem("masked"), Step(s.sem("vec"))
            bounded, exps, divided, probs, turned, wT_ready, a_ready, a_kept = (
                s.sem(x) for x in ("bounded", "exps", "divided", "probs", "turned", "wT_ready", "a_ready", "a_kept"))
            a_out, a_in = ([s.sem(f"{n}{part}") for part in range(2)] for n in ("a_out", "a_in"))

            def four(bank, n=HD):
                return bank[:, 0:4 * n].rearrange("p (h k) -> p h k", h=4)

            with nc.Block() as block:
                @block.tensor
                def _(pe):
                    for n in range(TILES + 3):
                        t = n
                        if t < TILES:
                            if t >= 3:
                                pe.wait_ge(masked, t - 2)
                            for i in range(4):
                                c = (i % 2) * HD
                                mm = nc.tensor.matmul(psS[:, t % 3, i * HD:(i + 1) * HD], Q[:, i // 2, t, c:c + HD], Kt[:, t, c:c + HD],
                                                      start=True, stop=True)
                            mm.then_inc(scores, 1)
                        t = n - 2
                        if 0 <= t < TILES:
                            pe.wait_ge(probs, t + 1)
                            if t >= 2:
                                pe.wait_ge(wT_ready, t - 1)
                            for i in range(4):
                                mm = nc.tensor.transpose(psT[:, t % 2, i * HD:(i + 1) * HD], sc[:, t, i, :], W["ident"][0:HD, 0:HD])
                            mm.then_inc(turned, 1)
                        t = n - 3
                        if t >= 0:
                            pe.wait_ge(wT_ready, t + 1)
                            if t >= 2:
                                pe.wait_ge(a_kept, t - 1)
                            for i in range(4):
                                b = 2 * t + i // 2
                                mm = nc.tensor.matmul(psA[:, t % 2, i * SEQ:(i + 1) * SEQ], wT[:, t, i, :],
                                                      VT[:, i % 2, b * SEQ:(b + 1) * SEQ], start=True, stop=True)
                            mm.then_inc(a_ready, 1)

                @block.vector
                def _(dve):
                    dve.wait_ge(W["sem"]["cmask"], 16)
                    for n in range(TILES + 3):
                        t = n
                        if t < TILES:
                            dve.wait_ge(scores, t + 1)
                            nc.vector.tensor_tensor(sc[:, t], four(psS[:, t % 3]), bcast(W["cmask"][:], 1, 4), ALU.add).then_inc(masked, 1)
                            dve.wait_ge(masked, t + 1)
                            link(dve, vec, nc.vector.tensor_reduce(mx[:, t, :], sc[:, t], AX.X, ALU.max))
                            nc.vector.tensor_scalar(mx[:, t, :], mx[:, t, :], -(float(SEQ) ** -0.5), None, ALU.mult).then_inc(bounded, 1)
                        t = n - 1
                        if 0 <= t < TILES:
                            dve.wait_ge(exps, 4 * (t + 1))
                            nc.vector.reciprocal(sm[:, t, :], sm[:, t, :]).then_inc(divided, 1)
                            dve.wait_ge(divided, t + 1)
                            nc.vector.tensor_tensor(sc[:, t], sc[:, t], bcast(sm[:, t, :], 2, HD), ALU.mult).then_inc(probs, 1)
                        t = n - 2
                        if 0 <= t < TILES:
                            dve.wait_ge(turned, t + 1)
                            nc.vector.tensor_copy(wT[:, t], four(psT[:, t % 2])).then_inc(wT_ready, 1)

                @block.scalar
                def _(act):
                    for n in range(TILES + 3):
                        t = n
                        if t < TILES:
                            act.wait_ge(bounded, t + 1)
                            for i in range(4):
                                nc.scalar.activation(sc[:, t, i, :], sc[:, t, i, :], ACT.Exp, bias=mx[:, t, i:i + 1], scale=float(SEQ) ** -0.5,
                                                     accum_out=sm[:, t, i:i + 1]).then_inc(exps, 1)
                        t = n - 3
                        if t >= 0:
                            act.wait_ge(a_ready, t + 1)
                            nc.scalar.copy(A[:, :, 2 * t:2 * t + 2, :].rearrange("p h b q -> p b h q"),
                                           psA[:, t % 2, 0:4 * SEQ].rearrange("p (b h q) -> p b h q", b=IN, h=2)).then_inc(a_kept, 1)

                @block.sync
                def _(sp):
                    for part in range(2):
                        b = slice(8 * part, 8 * part + 8)
                        sp.wait_ge(a_kept, 4 * (part + 1))
                        for half in range(2):
                            sp.dma_start(a_dram.rearrange("b (h c) q -> h c b q", h=2)[half][:, b, :], A[:, half, b, :]).then_inc(a_out[part], 16)
                    for part in range(2):
                        sp.wait_ge(a_out[part], 32)
                        sp.dma_start(Y[:, 4 * part:4 * part + 4, :],
                                     a_dram[8 * part:8 * part + 8].rearrange("b c q -> (b c q)").rearrange("(t p d) -> p t d", p=PAIR, d=D)).then_inc(a_in[part], 16)
    with Stage(nc, "cd") as s:
        turn = Turn(nc, W, s, Y, YT, ready=[(a_in[part], 16) for part in range(2)])
        psO = s.ps("psO", [PAIR, 4, BANK])
        out_ready, added = s.sem("out_ready"), s.sem("added")
        with nc.Block() as block:
            block.scalar(turn.on_scalar)

            @block.tensor
            def _(pe):
                for name in ("ident", "w2"):
                    pe.wait_ge(W["sem"][name], 16)
                for half in range(2):
                    turn.half_on_tensor(pe, half)
                    pe.wait_ge(turn.kept, 2 * (half + 1))
                    for t in range(4 * half, 4 * half + 4):
                        if t >= 4:
                            pe.wait_ge(added, t - 3)
                        for k in range(2):
                            mm = nc.tensor.matmul(psO[:, t % 4, 0:D], YT[:, k, tokens(t)], W["w2"][:, k, :], start=k == 0, stop=k == 1)
                        mm.then_inc(out_ready, 1)

            @block.vector
            def _(dve):
                for t in range(TILES):
                    dve.wait_ge(out_ready, t + 1)
                    nc.vector.tensor_tensor(X[:, t, :], psO[:, t % 4, 0:D], X[:, t, :], ALU.add).then_inc(added, 1)


def routing_stage(nc, W, name, E, ranks, NT, usual, xT, wr, wr_name, by_image, x, gain, shift, rows, slot, tile_expert,
                  total, more):
    TE = TILES * E
    MAXM = (TOK + SLOT - 1) // SLOT
    with Stage(nc, name) as s:
        lg = s.sb("lg", [PAIR, TILES, E])
        lr = s.sb("lr", [PAIR, TILES, E])
        ex = s.sb("ex", [PAIR, TILES, E])
        key = s.sb("key", [PAIR, TILES, E])
        oh = s.sb("oh", [PAIR, 2, TILES, E])
        pre = s.sb("pre", [PAIR, 2, 2 * TILES + 1, E])
        both = pre[:, 0, TILES + 1:, :]
        pre2 = s.sb("pre2", [PAIR, 2 * TILES + 1, E])
        st = s.sb("st", [PAIR, 6, TILES])
        cnt = s.sb("cnt", [PAIR, E, MAXM])
        ne = s.sb("ne", [PAIR, 4, E])
        zero = s.sb("zero", [PAIR, E])
        place = s.sb("place", [PAIR, TILES, E])
        slotf = s.sb("slotf", [PAIR, TILES, 2])
        te = s.sb("te", [1, NT, E])
        tef = s.sb("tef", [1, NT])
        psL = s.ps("psL", [PAIR, BANK])
        psM = s.ps("psM", [PAIR, BANK])
        psP = s.ps("psP", [PAIR, BANK])
        logits, raw_kept, mean_ready, shifted, exps = (s.sem(x) for x in ("logits", "raw_kept", "mean_ready", "shifted", "exps"))
        chosen, counted, slots_ready, copied, x_done, total_done = (
            s.sem(x) for x in ("chosen", "counted", "slots_ready", "copied", "x_done", "total_done"))
        x_steps = 1 if shift is None else 2
        vec = Step(s.sem("vec"))
        with nc.Block() as block:
            @block.tensor
            def _(pe):
                for n in (wr_name, "imean", "before"):
                    pe.wait_ge(W["sem"][n], 16)
                for t in range(TILES):
                    for k in range(2):
                        mm = nc.tensor.matmul(psL[:, t * E:(t + 1) * E], xT[0:HD, k, tokens(t)], wr[:, k, :],
                                              start=k == 0, stop=k == 1)
                mm.then_inc(logits, 1)
                if by_image:
                    pe.wait_ge(raw_kept, 1)
                    nc.tensor.matmul(psM[:, 0:TE], W["imean"][:], lr[:].rearrange("p t e -> p (t e)"),
                                     start=True, stop=True).then_inc(mean_ready, 1)
                pe.wait_ge(chosen, 1)
                nc.tensor.matmul(psP[:, 0:TE + E], W["ones"][0:PAIR, 0:PAIR], pre[:, 1, TILES:, :].rearrange("p t e -> p (t e)"),
                                 start=True, stop=False)
                mm = nc.tensor.matmul(psP[:, 0:TE], W["before"][:], both.rearrange("p t e -> p (t e)"), start=False, stop=True)
                mm.then_inc(counted, 1)

            @block.gpsimd
            def _(pool):
                pool.wait_ge(W["sem"]["rowd"], 16)
                nc.gpsimd.tensor_tensor(x[:], x[:], bcast(gain, 1, TILES), ALU.mult).then_inc(x_done, 1)
                pool.wait_ge(x_done, 1)
                if shift is not None:
                    nc.gpsimd.tensor_tensor(x[:], x[:], bcast(shift, 1, TILES), ALU.add).then_inc(x_done, 1)
                    pool.wait_ge(x_done, 2)
                nc.gpsimd.tensor_tensor(total[:], total[:], more[:] if len(more.shape) == 3 else bcast(more, 1, TILES),
                                        ALU.add).then_inc(total_done, 1)
                pool.wait_ge(total_done, 1)

            @block.scalar
            def _(act):
                act.wait_ge(shifted, 1)
                nc.scalar.activation(ex[:], lg[:], ACT.Exp, scale=1.0).then_inc(exps, 1)
                act.wait_ge(W["sem"]["iota"], 16)
                act.wait_ge(x_done, x_steps)
                for k in range(ranks):
                    nc.scalar.copy(rows[:, :, k, 0:D], x[:]).then_inc(copied, 1)
                    nc.scalar.activation(rows[:, :, k, D], W["iota"][0:PAIR, 80:80 + TILES], ACT.Identity,
                                         bias=W["iota"][0:PAIR, 80 + TILES + k:81 + TILES + k], scale=float(ranks)).then_inc(copied, 1)

            @block.vector
            def _(dve):
                def do(ins):
                    link(dve, vec, ins)

                v3 = lambda p: p[:, 0:TE].rearrange("p (t e) -> p t e", t=TILES)
                do(nc.vector.memset(pre[:], 0.0))
                do(nc.vector.memset(pre2[:], 0.0))
                do(nc.vector.memset(zero[:], 0.0))
                dve.wait_ge(W["sem"]["iota"], 16)
                dve.wait_ge(logits, 1)
                if by_image:
                    nc.vector.tensor_copy(lr[:], v3(psL)).then_inc(raw_kept, 1)
                    dve.wait_ge(W["sem"]["colb"], 16)
                    dve.wait_ge(mean_ready, 1)
                    do(nc.vector.tensor_tensor(lr[:], v3(psM), bcast(W["colb"][:, 0:E], 1, TILES), ALU.add))
                else:
                    do(nc.vector.tensor_copy(lr[:], v3(psL)))
                do(nc.vector.tensor_reduce(st[:, 0, :], lr[:], AX.X, ALU.max))
                nc.vector.tensor_tensor(lg[:], lr[:], bcast(st[:, 0, :], 2, E), ALU.subtract).then_inc(shifted, 1)
                dve.wait_ge(exps, 1)
                do(nc.vector.tensor_reduce(st[:, 1, :], ex[:], AX.X, ALU.add))
                do(nc.vector.reciprocal(st[:, 2, :], st[:, 1, :]))
                iota = bcast(W["iota"][0:PAIR, 0:E], 1, TILES)
                for r in range(ranks):
                    if r:
                        do(nc.vector.tensor_reduce(st[:, 0, :], lr[:], AX.X, ALU.max))
                    do(nc.vector.tensor_tensor(key[:], lr[:], bcast(st[:, 0, :], 2, E), ALU.is_lt))
                    do(nc.vector.scalar_tensor_tensor(key[:], key[:], 1000.0, iota, ALU.mult, ALU.add))
                    do(nc.vector.tensor_reduce(st[:, 3, :], key[:], AX.X, ALU.min))
                    do(nc.vector.tensor_tensor(oh[:, r, :, :], iota, bcast(st[:, 3, :], 2, E), ALU.is_equal))
                    do(nc.vector.tensor_tensor(key[:], oh[:, r, :, :], ex[:], ALU.mult))
                    do(nc.vector.tensor_reduce(st[:, 4, :], key[:], AX.X, ALU.add))
                    do(nc.vector.tensor_tensor(rows[:, :, r, D + 1], st[:, 4, :], st[:, 2, :], ALU.mult))
                    if r + 1 < ranks:
                        do(nc.vector.scalar_tensor_tensor(lr[:], oh[:, r, :, :], NEG, lr[:], ALU.mult, ALU.add))
                if ranks == 2:
                    do(nc.vector.tensor_tensor(both, oh[:, 0, :, :], oh[:, 1, :, :], ALU.add))
                else:
                    do(nc.vector.tensor_copy(both, oh[:, 0, :, :]))
                a = [pre[:, 0], pre[:, 1], pre2[:], pre[:, 1]]
                for n, shift in enumerate((1, 2, 4)):
                    low = lambda v, k: v[:, TILES - k:2 * TILES + 1 - k, :]
                    ins = nc.vector.tensor_tensor(low(a[n + 1], 0), low(a[n], 0), low(a[n], shift), ALU.add)
                    if n < 2:
                        do(ins)
                ins.then_inc(chosen, 1)
                dve.wait_ge(counted, 1)
                do(nc.vector.tensor_copy(ne[:, 0, :], psP[:, TE:TE + E]))
                do(nc.vector.tensor_tensor(cnt[:], bcast(ne[:, 0, :], 2, MAXM), bcast(W["iota"][0:PAIR, 32:32 + MAXM], 1, E), ALU.is_gt))
                do(nc.vector.tensor_reduce(ne[:, 1, :], cnt[:], AX.X, ALU.add))
                do(nc.vector.tensor_tensor_scan(ne[:, 2, :], ne[:, 1, :], zero[:], 0.0, ALU.add, ALU.add))
                do(nc.vector.tensor_tensor(ne[:, 3, :], ne[:, 2, :], ne[:, 1, :], ALU.subtract))
                do(nc.vector.tensor_scalar(ne[:, 3, :], ne[:, 3, :], float(SLOT), None, ALU.mult))
                do(nc.vector.tensor_tensor(place[:], v3(psP), bcast(ne[:, 3, :], 1, TILES), ALU.add))
                for r in range(ranks):
                    do(nc.vector.tensor_tensor(key[:], place[:], oh[:, r, :, :], ALU.mult))
                    do(nc.vector.tensor_reduce(slotf[:, :, r], key[:], AX.X, ALU.add))
                do(nc.vector.tensor_tensor(te[:], bcast(W["iota"][0:1, 48:48 + NT], 2, E), bcast(ne[0:1, 2, :], 1, NT), ALU.is_ge))
                do(nc.vector.tensor_reduce(tef[:], te[:], AX.X, ALU.add))
                do(nc.vector.tensor_scalar(tile_expert[:, 0:NT], tef[:], float(E - 1), None, ALU.min))
                do(nc.vector.tensor_scalar(tile_expert[:, NT:NT + 1], ne[0:1, 2, E - 1:E], usual + 0.5, None, ALU.is_gt))
                nc.vector.tensor_copy(slot[:, :, 0:ranks], slotf[:, :, 0:ranks]).then_inc(slots_ready, 1)


def expert_stage(nc, W, name, E, ranks, NT, usual, func, w_up, w_down, b_down, tile_expert, rows, slot, x_dram, cleared, y_dram):
    tokens_in = ranks * TOK
    with Stage(nc, name) as s:
        wu = s.sb("wu", [HD + 1, 2, 2 * F])
        wd = s.sb("wd", [128, 2, FC * D])
        wb = s.sb("wb", [1, 2, D]) if b_down is not None else None
        xs = s.sb("xs", [SLOT, 2, ROW])
        gate = s.sb("gate", [SLOT, 2])
        target = s.sb("target", [SLOT, 2], U32)
        xT = s.sb("xT", [HD + 1, 2, 2, SLOT])
        hm = s.sb("hm", [SLOT, F])
        hT = s.sb("hT", [128, FC, SLOT])
        ys = s.sb("ys", [SLOT, 2, D])
        psX = s.ps("psX", [HD, BANK])
        psU = s.ps("psU", [SLOT, 2, BANK])
        psH = s.ps("psH", [128, 2, BANK])
        psD = s.ps("psD", [SLOT, BANK])
        up_in, down_in, x_in, y_out = ([s.sem(f"{n}{i}") for i in range(2)] for n in ("up_in", "down_in", "x_in", "y_out"))
        ones_ready, x_turned, xT_ready, up_done, hm_ready = (
            s.sem(x) for x in ("ones_ready", "x_turned", "xT_ready", "up_done", "hm_ready"))
        h_turned, hT_ready, down_done, y_ready = (s.sem(x) for x in ("h_turned", "hT_ready", "down_done", "y_ready"))
        scattered, aside = s.sem("scattered"), s.sem("aside")
        down_parts = 2 if b_down is not None else 1
        xd = x_dram.rearrange("(n p) d -> n p d", p=SLOT)
        more = nc.values_load(tile_expert[0:1, NT:NT + 1], min_val=0, max_val=1)

        def each_tile(eng, step, finish):
            def run(a, b):
                with eng.Fori(a // 2, a // 2 + (b - a) // 2) as k:
                    for i, p, u in ((2 * k + 1, 1, k), (2 * k + 2, 0, k + 1)) if a % 2 else ((2 * k, 0, k), (2 * k + 1, 1, k)):
                        step(i, p, u, False)
                if (b - a) % 2:
                    step(b - 1, (b - 1) % 2, (b - 1) // 2, False)

            for i in range(3):
                step(i, i % 2, i // 2, i == 0)
            run(3, usual)
            with eng.If(more > 0):
                run(usual, NT)
                finish(NT)
            with eng.Else():
                finish(usual)

        def wait_past(eng, sem, n):
            if not (isinstance(n, int) and n <= 0):
                eng.wait_ge(sem, n)

        with nc.Block() as block:
            @block.sync
            def _(sp):
                def load(i, p, u, first):
                    e = sp.value_load(tile_expert[0:1, bass.ds(i, 1)], min_val=0, max_val=E - 1)
                    if first:
                        sp.dma_start(wu[:, p, :], w_up[bass.ds(e, 1), :, :].rearrange("o p f -> (o p) f")).then_inc(up_in[p], 16)
                        sp.wait_ge(scattered, 16 * TILES * ranks)
                        sp.dma_start(xs[:, p, :], xd[bass.ds(i, 1), :, :].rearrange("o p f -> (o p) f")).then_inc(x_in[p], 16)
                    else:
                        wait_past(sp, up_done, i - 1)
                        wait_past(sp, aside, i - 1)
                        sp.dma_start(xs[:, p, :], xd[bass.ds(i, 1), :, :].rearrange("o p f -> (o p) f")).then_inc(x_in[p], 16)
                        sp.dma_start(wu[:, p, :], w_up[bass.ds(e, 1), :, :].rearrange("o p f -> (o p) f")).then_inc(up_in[p], 16)

                each_tile(sp, load, lambda n: None)

            @block.tensor
            def _(pe):
                def turn_hidden(i):
                    pe.wait_ge(hm_ready, i + 1)
                    wait_past(pe, hT_ready, i)
                    for c in range(FC):
                        mm = nc.tensor.transpose(psH[:, c // 3, (c % 3) * SLOT:(c % 3 + 1) * SLOT],
                                                 hm[:, c * 128:(c + 1) * 128], W["ident"][:])
                    mm.then_inc(h_turned, 1)

                def down(i, p, u):
                    pe.wait_ge(down_in[p], (u + 1) * (16 * down_parts))
                    pe.wait_ge(hT_ready, i + 1)
                    wait_past(pe, y_ready, i)
                    for c in range(FC):
                        mm = nc.tensor.matmul(psD[:, 0:D], hT[:, c, :], wd[:, p, c * D:(c + 1) * D],
                                              start=c == 0, stop=c == FC - 1 and b_down is None)
                    if b_down is not None:
                        mm = nc.tensor.matmul(psD[:, 0:D], W["ones"][0:1, 0:SLOT], wb[:, p, :], start=False, stop=True)
                    mm.then_inc(down_done, 1)

                def step(i, p, u, first):
                    pe.wait_ge(x_in[p], (u + 1) * 16)
                    if not first:
                        pe.wait_ge(xT_ready, i)
                    for k in range(2):
                        mm = nc.tensor.transpose(psX[:, k * SLOT:(k + 1) * SLOT], xs[:, p, k * HD:(k + 1) * HD], W["ident"][:])
                    mm.then_inc(x_turned, 1)
                    if not first:
                        turn_hidden(i - 1)
                    pe.wait_ge(up_in[p], (u + 1) * 16)
                    pe.wait_ge(xT_ready, i + 1)
                    for j in range(2):
                        c = j * D_IN
                        nc.tensor.matmul(psU[:, j, 0:D_IN], xT[:, p, 0, :], wu[:, p, c:c + D_IN], start=True, stop=False)
                        mm = nc.tensor.matmul(psU[:, j, 0:D_IN], xT[0:HD, p, 1, :], wu[0:HD, p, F + c:F + c + D_IN],
                                              start=False, stop=True)
                    mm.then_inc(up_done, 1)
                    if not first:
                        down(i - 1, 1 - p, u - 1 + p)

                pe.wait_ge(ones_ready, 1)
                def finish(n):
                    turn_hidden(n - 1)
                    down(n - 1, (n - 1) % 2, (n - 1) // 2)

                each_tile(pe, step, finish)

            @block.vector
            def _(dve):
                def step(i, p, u, first):
                    dve.wait_ge(x_turned, i + 1)
                    if not first:
                        wait_past(dve, up_done, i - 1)
                    nc.vector.tensor_copy(xT[0:HD, p, :, :], psX[:, 0:2 * SLOT].rearrange("p (k n) -> p k n", k=2)).then_inc(xT_ready, 1)
                    if not first:
                        hidden(i - 1)
                    wait_past(dve, y_out[p], u * 16)
                    nc.vector.tensor_scalar(target[:, p:p + 1], xs[:, p, D:D + 1], float(NO_ROW), None, ALU.add)
                    nc.vector.tensor_copy(gate[:, p:p + 1], xs[:, p, D + 1:D + 2]).then_inc(aside, 1)

                def hidden(i):
                    dve.wait_ge(h_turned, i + 1)
                    wait_past(dve, down_done, i)
                    nc.vector.tensor_copy(hT[:].rearrange("p (a b) n -> p a (b n)", a=2), psH[:, :, 0:D_IN]).then_inc(hT_ready, 1)

                nc.vector.memset(xT[HD:HD + 1, :, :, :], 1.0).then_inc(ones_ready, 1)
                each_tile(dve, step, lambda n: hidden(n - 1))

            @block.scalar
            def _(act):
                def load_down(i, p):
                    e = act.value_load(tile_expert[0:1, bass.ds(i, 1)], min_val=0, max_val=E - 1)
                    act.dma_start(wd[:, p, :], w_down[bass.ds(e, 1), :, :].rearrange("o p f -> (o p) f")).then_inc(down_in[p], 16)
                    if b_down is not None:
                        act.dma_start(wb[:, p, :], b_down[bass.ds(e, 1), :]).then_inc(down_in[p], 16)

                def result(i, p, u):
                    act.wait_ge(down_done, i + 1)
                    act.wait_ge(aside, i + 1)
                    wait_past(act, y_out[p], u * 16)
                    nc.scalar.activation(ys[:, p, :], psD[:, 0:D], ACT.Copy, scale=gate[:, p:p + 1]).then_inc(y_ready, 1)

                def step(i, p, u, first):
                    load_down(i, p)
                    act.wait_ge(up_done, i + 1)
                    wait_past(act, h_turned, i)
                    nc.scalar.activation(hm[:].rearrange("p (a n) -> p a n", a=2), psU[:, :, 0:D_IN], func).then_inc(hm_ready, 1)
                    if not first:
                        result(i - 1, 1 - p, u - 1 + p)

                each_tile(act, step, lambda n: result(n - 1, (n - 1) % 2, (n - 1) // 2))

            @block.gpsimd
            def _(pool):
                pool.wait_ge(cleared, 16)
                for t in range(TILES):
                    for r in range(ranks):
                        nc.gpsimd.indirect_dma_start(
                            out=x_dram[:, :], out_offset=bass.IndirectOffsetOnAxis(ap=slot[:, t, r:r + 1], axis=0),
                            in_=rows[:, t, r, :], in_offset=None).then_inc(scattered, 16)

                def send(first, last):
                    for i in range(first, last):
                        p = i % 2
                        pool.wait_ge(y_ready, i + 1)
                        nc.gpsimd.indirect_dma_start(
                            out=y_dram[:, :], out_offset=bass.IndirectOffsetOnAxis(ap=target[:, p:p + 1], axis=0),
                            in_=ys[:, p, :], in_offset=None, bounds_check=tokens_in - 1, oob_is_err=False).then_inc(y_out[p], 16)
                    for p in range(2):
                        pool.wait_ge(y_out[p], 16 * ((last + 1 - p) // 2))

                send(0, usual)
                with pool.If(more > 0):
                    send(usual, NT)


def combine_stage(nc, W, name, y_dram, H, out):
    with Stage(nc, name) as s:
        y = s.sb("y", [PAIR, TILES, D])
        got, stored = [s.sem(f"got{i}") for i in range(2)], s.sem("stored")
        added = s.sem("added")
        with nc.Block() as block:
            @block.sync
            def _(sp):
                for half in range(2):
                    t = slice(4 * half, 4 * half + 4)
                    sp.dma_start(y[:, t], y_dram.rearrange("(t p) d -> p t d", p=PAIR)[:, t]).then_inc(got[half], 16)
                for loaded in W["sem"].values():
                    sp.wait_ge(loaded, 16)
                for half in range(2):
                    t = slice(4 * half, 4 * half + 4)
                    sp.wait_ge(added, half + 1)
                    sp.dma_start(out.rearrange("(t o) q d -> (o q) t d", o=2)[:, t], H[:, t]).then_inc(stored, 16)
                sp.wait_ge(stored, 32)

            @block.vector
            def _(dve):
                for half in range(2):
                    t = slice(4 * half, 4 * half + 4)
                    dve.wait_ge(got[half], 16)
                    nc.vector.tensor_tensor(H[:, t], H[:, t], y[:, t], ALU.add).then_inc(added, 1)


def mamba_layer(nc, W, x, xT, H, dec_dram):
    ZD = D_IN + M_HEADS
    TH = TILES * M_HEADS
    with Stage(nc, "mb") as s:
        z = s.sb("z", [128, 3, TOK])
        cc = s.sb("cc", [128, 4, TOK])
        xh = s.sb("xh", [PAIR, TILES, D_IN])
        L = s.sb("L", [PAIR, TH, PAIR])
        wout = s.sb("wout", [128, 3, D])
        with Stage(nc, "mc") as p:
            ORDER = (3, 0, 1, 2)
            xbc = p.sb("xbc", [128, 4, IMAGES, PADSEQ])
            BC = p.sb("BC", [D_ST, 2, TOK])
            dt = p.sb("dt", [PAIR, TILES, M_HEADS])
            dec = p.sb("dec", [PAIR, TILES, M_HEADS])
            decT = p.sb("decT", [TH, 2, SEQ])
            d0 = p.sb("d0", [PAIR, TH * PAIR])
            d1 = p.sb("d1", [PAIR, TH, PAIR])
            t1, t2, t3 = (p.sb(n, [PAIR, TH]) for n in ("t1", "t2", "t3"))
            A = p.sb("A", [PAIR, M_HEADS])
            ring = p.ps("ring", [128, 4, BANK])
            psD = p.ps("psD", [TH, BANK])
            psV = p.ps("psV", [PAIR, BANK])
            psG = p.ps("psG", [PAIR, 2, BANK])
            v_ready, ring_ready, ring_kept, padded, weighed = (
                p.sem(n) for n in ("v_ready", "ring_ready", "ring_kept", "padded", "weighed"))
            vec, first_tap, conv = Step(p.sem("vec")), p.sem("first_tap"), Step(p.sem("conv"))
            a_ready, dt_absd, dt_exp, dt_ready, dec_in, dec_out = (
                p.sem(n) for n in ("a_ready", "dt_absd", "dt_exp", "dt_ready", "dec_in", "dec_out"))
            dec_turned, decT_zero, decT_ready, dec_stored, d0_ready, d1_ready = (
                p.sem(n) for n in ("dec_turned", "decT_zero", "decT_ready", "dec_stored", "d0_ready", "d1_ready"))
            silus, g_ready, x_turned, x_kept, scanned, weighted, added = (
                p.sem(n) for n in ("silus", "g_ready", "x_turned", "x_kept", "scanned", "weighted", "added"))
            dtf = dt[:].rearrange("p t h -> p (t h)")
            decf = dec[:].rearrange("p t h -> p (t h)")
            with nc.Block() as block:
                @block.tensor
                def _(pe):
                    pe.wait_ge(W["sem"]["win"], 16)
                    for t in range(TILES):
                        for k in range(2):
                            mm = nc.tensor.matmul(psV[:, t * M_HEADS:(t + 1) * M_HEADS], xT[:, k, tokens(t)], W["win"][:, k, D_IN:ZD],
                                                  start=k == 0, stop=k == 1)
                    mm.then_inc(v_ready, 1)

                    def project(n, w0):
                        if n >= 4:
                            pe.wait_ge(ring_kept, n - 3)
                        for k in range(2):
                            mm = nc.tensor.matmul(ring[:, n % 4, 0:HALF_TOK], W["win"][:, k, w0:w0 + 128],
                                                  xT[:, k, (n % 2) * HALF_TOK:(n % 2 + 1) * HALF_TOK], start=k == 0, stop=k == 1)
                        mm.then_inc(ring_ready, 1)

                    for n in range(8):
                        project(n, ZD + ORDER[n // 2] * 128)
                        if n == 5:
                            pe.wait_ge(dec_out, 1)
                            nc.tensor.transpose(psD[:, 0:PAIR], decf, W["ident"][0:PAIR, 0:PAIR]).then_inc(dec_turned, 1)
                    for n in range(8, 14):
                        project(n, (n - 8) // 2 * 128)
                    pe.wait_ge(silus, 2)
                    for t in range(TILES):
                        mm = nc.tensor.matmul(psG[:, t // 4, (t % 4) * PAIR:(t % 4 + 1) * PAIR], BC[:, 0, tokens(t)],
                                              BC[:, 1, tokens(t)], start=True, stop=True)
                    mm.then_inc(g_ready, 1)
                    pe.wait_ge(silus, 5)
                    pe.wait_ge(ring_kept, 14)
                    for t in range(TILES):
                        if t >= 4:
                            pe.wait_ge(x_kept, t - 3)
                        for c in range(3):
                            mm = nc.tensor.transpose(ring[0:PAIR, t % 4, c * 128:(c + 1) * 128], cc[:, c, tokens(t)], W["ident"][:])
                        mm.then_inc(x_turned, 1)

                @block.scalar
                def _(act):
                    def keep(q):
                        c = ORDER[q]
                        for g in range(2):
                            act.wait_ge(ring_ready, 2 * q + g + 1)
                            nc.scalar.copy(xbc[:, c, 8 * g:8 * g + 8, KCONV - 1:PADSEQ],
                                           ring[:, (2 * q + g) % 4, 0:HALF_TOK].rearrange("p (b q) -> p b q", b=8)).then_inc(ring_kept, 1)
                        act.wait_ge(ring_kept, 2 * q + 2)
                        nc.scalar.activation(cc[:, c, :].rearrange("p (b q) -> p b q", b=IMAGES), xbc[:, c, :, 0:SEQ], ACT.Identity,
                                             bias=W["mvec"][:, c, 4:5], scale=W["mvec"][:, c, 0:1]).then_inc(first_tap, 1)

                    for n in ("mvec", "colb"):
                        act.wait_ge(W["sem"][n], 16)
                    nc.scalar.activation(A[:], W["colb"][:, 24:30], ACT.Exp).then_inc(a_ready, 1)
                    act.wait_ge(padded, 1)
                    act.wait_ge(dt_absd, 1)
                    nc.scalar.activation(t1[:], t1[:], ACT.Exp).then_inc(dt_exp, 1)
                    keep(0)
                    keep(1)
                    act.wait_ge(dec_in, 1)
                    nc.scalar.activation(decf, decf, ACT.Exp).then_inc(dec_out, 1)
                    keep(2)
                    keep(3)
                    act.wait_ge(conv.sem, 3)
                    for i in range(2):
                        nc.scalar.activation(BC[:, i, :], cc[64 * i:64 * i + D_ST, 3, :], ACT.Silu).then_inc(silus, 1)
                    for n in range(8, 14):
                        act.wait_ge(ring_ready, n + 1)
                        nc.scalar.activation(z[:, (n - 8) // 2, (n % 2) * HALF_TOK:(n % 2 + 1) * HALF_TOK], ring[:, n % 4, 0:HALF_TOK],
                                             ACT.Silu).then_inc(ring_kept, 1)
                    for q in range(1, 4):
                        act.wait_ge(conv.sem, 3 * (q + 1))
                        nc.scalar.activation(cc[:, ORDER[q], :], cc[:, ORDER[q], :], ACT.Silu).then_inc(silus, 1)
                    for t in range(TILES):
                        act.wait_ge(x_turned, t + 1)
                        nc.scalar.copy(xh[:, t, :], ring[0:PAIR, t % 4, 0:D_IN]).then_inc(x_kept, 1)

                @block.gpsimd
                def _(pool):
                    nc.gpsimd.memset(xbc[:, :, :, 0:KCONV - 1], 0.0).then_inc(padded, 1)
                    nc.gpsimd.memset(decT[:], 0.0).then_inc(decT_zero, 1)
                    nc.gpsimd.tensor_tensor(H[:], H[:], x[:], ALU.add).then_inc(added, 1)
                    pool.wait_ge(dt_ready, 1)
                    nc.gpsimd.tensor_tensor(d1[:], bcast(W["ident"][0:PAIR, 0:PAIR], 1, TH), bcast(dtf, 2, PAIR), ALU.mult).then_inc(d1_ready, 1)
                    for name in ("wout", "mvec"):
                        pool.wait_ge(W["sem"][name], 16)
                    nc.gpsimd.tensor_tensor(wout[:], W["wout"][:], bcast(W["mvec"][:, 0:3, 5], 2, D), ALU.mult).then_inc(weighed, 1)

                @block.sync
                def _(sp):
                    sp.wait_ge(decT_ready, 1)
                    sp.dma_start(dec_dram, decT[:].rearrange("p o i -> p (o i)")).then_inc(dec_stored, 16)
                    sp.wait_ge(dec_stored, 16)
                    sp.dma_start(d0[:], dec_dram.rearrange("a i -> (a i)").partition_broadcast(PAIR)).then_inc(d0_ready, 16)

                @block.vector
                def _(dve):
                    def do(ins):
                        link(dve, vec, ins)

                    dve.wait_ge(W["sem"]["colb"], 16)
                    dve.wait_ge(v_ready, 1)
                    do(nc.vector.tensor_tensor(dt[:], psV[:, 0:TH].rearrange("p (t h) -> p t h", t=TILES), bcast(W["colb"][:, 16:22], 1, TILES), ALU.add))
                    do(nc.vector.tensor_scalar(t1[:], dtf, -1.0, None, ALU.mult))
                    nc.vector.tensor_tensor(t1[:], t1[:], dtf, ALU.min).then_inc(dt_absd, 1)
                    dve.wait_ge(dt_exp, 1)
                    do(nc.vector.tensor_scalar(t2[:], t1[:], 2.0, None, ALU.add))
                    do(nc.vector.reciprocal(t2[:], t2[:]))
                    do(nc.vector.tensor_tensor(t1[:], t1[:], t2[:], ALU.mult))
                    do(nc.vector.tensor_tensor(t2[:], t1[:], t1[:], ALU.mult))
                    do(nc.vector.tensor_scalar(t3[:], t2[:], 1.0 / 17, 1.0 / 15, ALU.mult, ALU.add))
                    for odd in (13, 11, 9, 7, 5, 3, 1):
                        do(nc.vector.tensor_tensor(t3[:], t3[:], t2[:], ALU.mult))
                        do(nc.vector.tensor_scalar(t3[:], t3[:], 1.0 / odd, None, ALU.add))
                    do(nc.vector.scalar_tensor_tensor(t3[:], t3[:], 2.0, t1[:], ALU.mult, ALU.mult))
                    nc.vector.scalar_tensor_tensor(dtf, dtf, 0.0, t3[:], ALU.max, ALU.add).then_inc(dt_ready, 1)
                    dve.wait_ge(dt_ready, 1)
                    dve.wait_ge(a_ready, 1)
                    nc.vector.scalar_tensor_tensor(dec[:], dt[:], -1.0, bcast(A[:], 1, TILES), ALU.mult, ALU.mult).then_inc(dec_in, 1)
                    for q, c in enumerate(ORDER):
                        dve.wait_ge(first_tap, q + 1)
                        dst = cc[:, c, :].rearrange("p (b q) -> p b q", b=IMAGES)
                        for k in range(1, KCONV):
                            link(dve, conv, nc.vector.scalar_tensor_tensor(dst, xbc[:, c, :, k:k + SEQ], W["mvec"][:, c, k:k + 1], dst,
                                                                           ALU.mult, ALU.add))
                        if q == 0:
                            dve.wait_ge(dec_turned, 1)
                            dve.wait_ge(decT_zero, 1)
                            nc.vector.tensor_copy(decT[:, :, 1:SEQ],
                                                  psD[:, 0:PAIR].rearrange("p (o i) -> p o i", o=2)[:, :, 1:SEQ]).then_inc(decT_ready, 1)
                    dve.wait_ge(d0_ready, 16)
                    dve.wait_ge(d1_ready, 1)
                    nc.vector.tensor_tensor_scan(L[:].rearrange("p a i -> p (a i)"), d0[:], d1[:].rearrange("p a i -> p (a i)"),
                                                 0.0, ALU.mult, ALU.add).then_inc(scanned, 1)
                    dve.wait_ge(scanned, 1)
                    dve.wait_ge(g_ready, 1)
                    for t in range(TILES):
                        Lt = L[:, t * M_HEADS:(t + 1) * M_HEADS, :]
                        nc.vector.tensor_tensor(Lt, bcast(psG[:, t // 4, (t % 4) * PAIR:(t % 4 + 1) * PAIR], 1, M_HEADS), Lt,
                                                ALU.mult).then_inc(weighted, 1)

        with Stage(nc, "me") as p:
            STEPS = 6
            g = p.sb("g", [128, 3, TOK])
            sq = p.sb("sq", [128, 3, TOK])
            ms = p.sb("ms", [PAIR, 2, TILES])
            psY = p.ps("psY", [128, 3, BANK])
            psQ = p.ps("psQ", [PAIR, 2, BANK])
            psO = p.ps("psO", [PAIR, 3, BANK])
            folded = p.sem("folded")
            y_ready, y_read, gated, squared, summed, var_ready, rstd_ready, out_ready, out_kept = (
                p.sem(n) for n in ("y_ready", "y_read", "gated", "squared", "summed", "var_ready", "rstd_ready", "out_ready", "out_kept"))
            cols = lambda n: slice(n // 3 * HALF_TOK, (n // 3 + 1) * HALF_TOK)
            with nc.Block() as block:
                @block.tensor
                def _(pe):
                    def y(n):
                        if n >= 3:
                            pe.wait_ge(y_read, n - 2)
                        for i in range(4):
                            t = 4 * (n // 3) + i
                            for o in range(2):
                                hd = 2 * (n % 3) + o
                                mm = nc.tensor.matmul(psY[64 * o:64 * o + DH, n % 3, i * PAIR:(i + 1) * PAIR],
                                                      xh[:, t, hd * DH:(hd + 1) * DH], L[:, t * M_HEADS + hd, :], start=True, stop=True)
                        mm.then_inc(y_ready, 1)

                    def out(half):
                        pe.wait_ge(folded, 2 * (half + 1))
                        for i in range(4):
                            mm = nc.tensor.matmul(psQ[:, half, i:i + 1], sq[:, 0, tokens(4 * half + i)], W["ones"][:, 0:1],
                                                  start=True, stop=True)
                        mm.then_inc(summed, 1)
                        for t in range(4 * half, 4 * half + 4):
                            if t >= 3:
                                pe.wait_ge(out_kept, t - 2)
                            for c in range(3):
                                mm = nc.tensor.matmul(psO[:, t % 3, 0:D], g[:, c, tokens(t)], wout[:, c, :], start=c == 0, stop=c == 2)
                            mm.then_inc(out_ready, 1)

                    for n in range(STEPS):
                        y(n)
                    out(0)
                    out(1)

                @block.vector
                def _(dve):
                    def fold(half):
                        i = slice(half * HALF_TOK, (half + 1) * HALF_TOK)
                        for c in (1, 2):
                            dve.wait_ge(squared, 3 * half + c + 1)
                            link(dve, folded_step, nc.vector.tensor_tensor(sq[:, 0, i], sq[:, 0, i], sq[:, c, i], ALU.add))

                    folded_step = Step(folded)
                    for n in range(STEPS):
                        c = n % 3
                        dve.wait_ge(y_ready, n + 1)
                        nc.vector.scalar_tensor_tensor(g[:, c, cols(n)], cc[:, c, cols(n)], W["mvec"][:, c, 6:7], psY[:, c, 0:HALF_TOK],
                                                       ALU.mult, ALU.add).then_inc(y_read, 1)
                        dve.wait_ge(y_read, n + 1)
                        nc.vector.tensor_tensor(g[:, c, cols(n)], g[:, c, cols(n)], z[:, c, cols(n)], ALU.mult).then_inc(gated, 1)
                        if c == 0 and n:
                            fold(n // 3 - 1)
                    fold(1)
                    for half in range(2):
                        dve.wait_ge(summed, half + 1)
                        nc.vector.tensor_scalar(ms[:, 0, 4 * half:4 * half + 4], psQ[:, half, 0:4], 1.0 / D_IN, 1e-5,
                                                ALU.mult, ALU.add).then_inc(var_ready, 1)
                        dve.wait_ge(rstd_ready, half + 1)
                        for t in range(4 * half, 4 * half + 4):
                            dve.wait_ge(out_ready, t + 1)
                            nc.vector.scalar_tensor_tensor(H[:, t, :], psO[:, t % 3, 0:D], ms[:, 1, t:t + 1], H[:, t, :],
                                                           ALU.mult, ALU.add).then_inc(out_kept, 1)

                @block.scalar
                def _(act):
                    for n in range(STEPS):
                        act.wait_ge(gated, n + 1)
                        nc.scalar.activation(sq[:, n % 3, cols(n)], g[:, n % 3, cols(n)], ACT.Square).then_inc(squared, 1)

                @block.gpsimd
                def _(pool):
                    for half in range(2):
                        i = slice(4 * half, 4 * half + 4)
                        pool.wait_ge(var_ready, half + 1)
                        nc.gpsimd.tensor_tensor(ms[:, 1, i], ms[:, 0, i], W["mhalf"][0:PAIR, i], ALU.pow).then_inc(rstd_ready, 1)


E0, E1 = 8, 16
NT0, NT1 = expert_tiles(E0, 2 * TOK), expert_tiles(E1, TOK)
USUAL0, USUAL1 = 2 * TOK // SLOT + 2, E1 + 1

RESIDENT = {
    "stem_w": (96, 2, C1), "chan": (C1, 6, 3), "tabs": (128, 72), "ident": (128, 128), "off_w": (C1, TAPS, 32), "stack4": (128, 32),
    "dcn_w": (C1, TAPS, D), "wq": (HD, 2, HEADS * DH), "wk": (HD, 2, HEADS * DH), "qkvb": (128, 3, 6),
    "amask": (PAIR, PAIR), "wv": (HD, 2, HEADS * DH), "wo": (128, 6, D), "w1": (HD + 1, 2, 3 * D),
    "cmask": (HD, HD), "w2": (HD, 2, D), "imean": (PAIR, PAIR), "before": (PAIR, PAIR), "iota": (128, 84 + TILES),
    "wr0": (HD, 2, E0), "mvec": (128, 4, 7),
    "wr1": (HD, 2, E1), "lncol": (HD, 2, 5), "win": (HD, 2, 2 * D_IN + 2 * D_ST + M_HEADS), "wout": (128, 3, D),
}
FIRST = {"stem_w", "chan", "tabs", "off_w", "stack4", "ident"}
KEPT = {"ident", "rowb"}
LATE = {"colb", "lncol", "w1", "w2", "win", "wout", "mvec", "rowd", "cmask", "imean", "before", "iota", "wr0", "wr1"}
SPREAD = {"rowb": 2 * D, "colb": 32, "rowd": 7 * D}
STREAMED = {"x": (96, IMAGES // 2 * PIX), "up0": (E0, HD + 1, 2 * F), "down0": (E0, 128, FC * D), "bdown0": (E0, D),
            "up1": (E1, HD + 1, 2 * F), "down1": (E1, 128, FC * D)}


def vit_tower(nc, K, out):
    W = {"sem": {}}
    with ExitStack() as top:
        def sb(name, shape, dt=F32):
            return top.enter_context(nc.sbuf_tensor(name, list(shape), dt))

        def place(stack, wanted):
            for name, shape in list(RESIDENT.items()) + [(n, (PAIR, length)) for n, length in SPREAD.items()]:
                if wanted(name):
                    W[name] = stack.enter_context(nc.sbuf_tensor(name, list(shape), F32))
                    W["sem"][name] = nc.alloc_semaphore(f"in_{name}")

        def fetch(eng, wanted):
            for name in RESIDENT:
                if wanted(name):
                    eng.dma_start(W[name][:], K[name]).then_inc(W["sem"][name], 16)
            for name in SPREAD:
                if wanted(name):
                    eng.dma_start(W[name][:], K[name].partition_broadcast(PAIR)).then_inc(W["sem"][name], 16)

        W["mhalf"], W["ones"], W["bnv"] = sb("mhalf", (128, 8)), sb("ones", (128, 128)), sb("bnv", (C1, 3, 3))
        H = sb("H", (PAIR, TILES, D))
        off_dram = nc.dram_tensor("points", (IMAGES, 32, POS), F32, kind="Internal").ap()
        dec_dram = nc.dram_tensor("decays", (TILES * M_HEADS, PAIR), F32, kind="Internal").ap()
        a_dram = nc.dram_tensor("channel_rows", (IMAGES, D, SEQ), F32, kind="Internal").ap()
        xs0, xs1 = (nc.dram_tensor(n, (t * SLOT, ROW), F32, kind="Internal").ap() for n, t in (("rows0", NT0), ("rows1", NT1)))
        ys0, ys1 = (nc.dram_tensor(n, (t, D), F32, kind="Internal").ap() for n, t in (("results0", 2 * TOK), ("results1", TOK)))
        zrow = sb("zrow", (SLOT, ROW))
        zeroed, cleared0, cleared1 = (nc.alloc_semaphore(n) for n in ("zeroed", "cleared0", "cleared1"))
        ones_done = nc.alloc_semaphore("ones_done")

        place(top, lambda name: name in KEPT)
        early = ExitStack()
        place(early, lambda name: name not in LATE and name not in KEPT)
        with nc.Block() as block:
            @block.scalar
            def _(act):
                fetch(act, lambda name: name in FIRST)

            @block.vector
            def _(dve):
                nc.vector.memset(zrow[:], 0.0).then_inc(zeroed, 1)
                nc.vector.memset(W["ones"][:], 1.0).then_inc(ones_done, 1)
                dve.wait_ge(ones_done, 1)

        with nc.cleanup_on_exit(), Stage(nc, "pe") as s:
            h = s.sb("h", [C1, IMAGES, PIX])
            samp = s.sb("samp", [C1, TAPS, IMAGES * POS])
            hc = s.sb("hc", [HD, 2, IMAGES, SEQ])
            all_near = s.sb("all_near", [1, 1], I32)
            stem_stage(nc, K, W, h, samp, off_dram, all_near,
                       lambda sp: fetch(sp, lambda name: name not in FIRST and name not in LATE))
            near = nc.values_load(all_near[0:1, 0:1], min_val=0, max_val=1)
            with nc.If(near > 0):
                near_sampling_stage(nc, K, W, h, samp, off_dram, hc)
            with nc.Else():
                sampling_stage(nc, K, W, h, samp, off_dram)
                patch_stage(nc, K, W, samp, hc)
            token_stage(nc, W, hc, H)
        with nc.cleanup_on_exit():
            attention_layer(nc, W, H)
        early.close()
        place(top, lambda name: name in LATE)

        def fetch_late(sp):
            fetch(sp, lambda name: name in LATE)
            sp.wait_ge(zeroed, 1)
            for xd, n, cleared in ((xs0, NT0, cleared0), (xs1, NT1, cleared1)):
                sp.dma_start(xd.rearrange("(n p) d -> p n d", p=SLOT), bcast(zrow[:], 1, n)).then_inc(cleared, 16)

        W["rowd"] = W["rowd"][:].rearrange("p (a d) -> p a d", d=D)
        with nc.cleanup_on_exit(), Stage(nc, "l0") as s:
            X = s.sb("X", [PAIR, TILES, D])
            xT = s.sb("xT", [HD + 1, 2, TOK])
            Y = s.sb("Y", [PAIR, TILES, D])
            YT = s.sb("YT", [HD, 2, TOK])
            rows, slot, te = s.sb("rows", [PAIR, TILES, 2, ROW]), s.sb("slot", [PAIR, TILES, 2], U32), s.sb("te", [1, 32], I32)
            norm_stage(nc, W, "l0_n", [(H, X, 1e-5, False)], xT[0:HD, :, :], on_sync=fetch_late, ones=xT[HD:HD + 1, :, :])
            channel_attention(nc, W, xT, X, a_dram, Y, YT)
            global_norm_stage(nc, W, "l0_g", X, Y, YT, W["lncol"][:, :, 0], W["lncol"][:, :, 1])
            routing_stage(nc, W, "l0_r", E0, 2, NT0, USUAL0, YT, W["wr0"], "wr0", True, Y,
                          W["rowd"][:, 0, :], W["rowd"][:, 1, :], rows, slot, te, H, W["rowd"][:, 3, :])
            expert_stage(nc, W, "l0_e", E0, 2, NT0, USUAL0, ACT.Gelu_apprx_tanh, K["up0"], K["down0"], K["bdown0"], te,
                         rows, slot, xs0, cleared0, ys0)
            global_norm_stage(nc, W, "l0_h", Y, X, gain=W["rowd"][:, 2, :], add_to=H, y_dram=ys0)
        with nc.cleanup_on_exit(), Stage(nc, "l1") as s:
            X = s.sb("X", [PAIR, TILES, D])
            XN = s.sb("XN", [PAIR, TILES, D])
            xT = s.sb("xT", [HD, 2, TOK])
            norm_stage(nc, W, "l1_n", [(H, X, 1e-5, False), (X, XN, 1e-5, False)], xT, W["lncol"][:, :, 2], W["lncol"][:, :, 3])
            mamba_layer(nc, W, X, xT, H, dec_dram)
        with nc.cleanup_on_exit(), Stage(nc, "l2") as s:
            X = s.sb("X", [PAIR, TILES, D])
            XN = s.sb("XN", [PAIR, TILES, D])
            xT = s.sb("xT", [HD, 2, TOK])
            rows, slot, te = s.sb("rows", [PAIR, TILES, 1, ROW]), s.sb("slot", [PAIR, TILES, 2], U32), s.sb("te", [1, 32], I32)
            norm_stage(nc, W, "l2_n", [(H, X, 1e-5, False), (X, XN, 1e-6, True)], xT, W["lncol"][:, :, 4])
            routing_stage(nc, W, "l2_r", E1, 1, NT1, USUAL1, xT, W["wr1"], "wr1", False, XN,
                          W["rowd"][:, 6, :], None, rows, slot, te, H, X)
            expert_stage(nc, W, "l2_e", E1, 1, NT1, USUAL1, ACT.Relu, K["up1"], K["down1"], None, te, rows, slot, xs1, cleared1, ys1)
            combine_stage(nc, W, "l2_m", ys1, H, out)


def layouts(a):
    f = np.float32

    def halves(w):
        return w.reshape(2, HD, -1).transpose(1, 0, 2)

    def biased(w, b):
        lo = np.concatenate([w[:HD], b[None]], 0)
        hi = np.concatenate([w[HD:], np.zeros_like(b)[None]], 0)
        return np.stack([lo, hi], 1)

    K = {}
    x = a["x"].reshape(2, IMAGES // 2, 3, SIDE, 4, SIDE, 4)
    K["x"] = x.transpose(0, 2, 4, 6, 1, 3, 5).reshape(96, IMAGES // 2 * PIX)
    K["stem_w"] = np.zeros((96, 2, C1), f)
    K["stem_w"][0:48, 0] = K["stem_w"][48:96, 1] = a["L0_tok_stem_w"].reshape(C1, 48).T
    K["stack4"] = np.tile(np.eye(32, dtype=f), (4, 1))
    chan = np.zeros((C1, 6, 3), f)
    for i, n in enumerate("gbmv"):
        chan[:, i, 0] = a[f"L0_tok_bn1_{n}"]
        chan[:, i, 1:] = a[f"L0_tok_bn2_{n}"].reshape(2, HD).T
    chan[:, 4, 0] = a["L0_tok_stem_b"]
    chan[:, 4, 1:] = a["L0_tok_dcn_b"].reshape(2, HD).T
    chan[:, 5, 0:2] = a["cls_tok"].reshape(2, HD).T
    K["chan"] = chan
    by_axis = lambda v: np.ascontiguousarray(v.reshape((TAPS, 2) + v.shape[1:]).swapaxes(0, 1)).reshape(v.shape)
    K["off_w"] = by_axis(a["L0_tok_off_w"]).reshape(32, C1, TAPS).transpose(1, 2, 0)
    tabs = np.zeros((128, 72), f)
    p = np.arange(CHUNK)
    for c in range(CHUNKS):
        tabs[:CHUNK, c] = -(ROWS * c + p // SIDE)
    tabs[:CHUNK, 7] = -(p % SIDE)
    tabs[:32, 8] = by_axis(a["L0_tok_off_b"])
    pos, tap = np.arange(POS), np.arange(TAPS)
    tabs[0:16, 16:16 + POS] = 4 * (pos // OUT_SIDE)[None] + (tap // 4)[:, None]
    tabs[16:32, 16:16 + POS] = 4 * (pos % OUT_SIDE)[None] + (tap % 4)[:, None]
    K["tabs"] = tabs
    K["ident"] = np.eye(128, dtype=f)
    K["dcn_w"] = a["L0_tok_dcn_w"].reshape(D, C1, TAPS).transpose(1, 2, 0)
    for n, w in (("wq", "Q"), ("wk", "K"), ("wv", "V")):
        K[n] = halves(a[f"L0_attn_W_{w}"].transpose(1, 0, 2).reshape(D, HEADS * DH))
    K["qkvb"] = np.stack([a[f"L0_attn_b_{n}"].reshape(6, 128).T for n in "QKV"], 1)
    K["wo"] = a["L0_attn_W_O"].reshape(6, 128, D).transpose(1, 0, 2)
    K["rowb"] = np.concatenate([a["L0_attn_b_O"], a["L0_ffn_W2_b"]])
    K["w1"] = biased(a["L0_ffn_W1_w"], a["L0_ffn_W1_b"])
    K["w2"] = halves(a["L0_ffn_W2_w"])
    q = np.arange(PAIR)
    same = q[:, None] // SEQ == q[None] // SEQ
    K["amask"] = np.where(same & (q[None] <= q[:, None]), 0, NEG).astype(f)
    c = np.arange(HD)
    K["cmask"] = np.where(c[:, None] // 16 == c[None] // 16, 0, NEG).astype(f)
    K["imean"] = (same / SEQ).astype(f)
    K["before"] = (q[:, None] < q[None]).astype(f)
    iota = np.zeros((128, 84 + TILES), f)
    iota[:PAIR, 80:80 + TILES] = np.arange(TOK).reshape(TILES, PAIR).T
    iota[:, 80 + TILES:82 + TILES] = np.arange(2) - NO_ROW
    iota[:PAIR, 82 + TILES:] = np.arange(PAIR)[:, None] // SEQ == np.arange(2)[None]
    iota[:, 0:32] = np.arange(32)
    iota[:, 32:40] = SLOT * np.arange(8)
    iota[:, 48:80] = np.arange(32)
    K["iota"] = iota
    K["lncol"] = np.stack([a[n].reshape(2, HD).T for n in ("L0_ffn_ln1_w", "L0_ffn_ln1_b", "L1_attn_ln_w", "L1_attn_ln_b",
                                                            "L1_ffn_ln_w")], 2)
    K["wr0"], K["wr1"] = halves(a["L0_ffn_r_w"]), halves(a["L1_ffn_w_router"])
    conv = np.concatenate([a["L1_attn_conv_w"], a["L1_attn_conv_b"][:, None]], 1)
    mvec = np.zeros((128, 4, 7), f)
    mvec[:, :, 0:5] = conv.reshape(4, 128, 5).transpose(1, 0, 2)
    mvec[:, 0:3, 6] = np.repeat(a["L1_attn_D"], DH).reshape(3, 128).T
    mvec[:, 0:3, 5] = a["L1_attn_rms_w"].reshape(3, 128).T
    K["mvec"] = mvec
    w = a["L1_attn_W_in"]
    K["win"] = halves(np.concatenate([w[:, :D_IN], w[:, -M_HEADS:], w[:, D_IN:-M_HEADS]], 1))
    K["wout"] = a["L1_attn_W_out"].reshape(3, 128, D).transpose(1, 0, 2)
    colb = np.zeros(32, f)
    colb[0:8], colb[16:22], colb[24:30] = a["L0_ffn_r_b"], a["L1_attn_dt_bias"], a["L1_attn_A_log"]
    K["colb"] = colb
    K["rowd"] = np.concatenate([a[n] for n in ("L0_ffn_ln1_w", "L0_ffn_ln1_b", "L0_ffn_ln2_w", "L0_ffn_ln2_b",
                                               "L1_attn_ln_w", "L1_attn_ln_b", "L1_ffn_ln_w")])

    def up(w, b):
        w = w.reshape(-1, 2, HD, F).transpose(0, 2, 1, 3)
        row = np.stack([b, np.zeros_like(b)], 1)[:, None]
        return np.concatenate([w, row], 1).reshape(-1, HD + 1, 2 * F)

    def down(w):
        return w.reshape(-1, FC, 128, D).transpose(0, 2, 1, 3).reshape(-1, 128, FC * D)

    K["up0"], K["down0"], K["bdown0"] = up(a["L0_ffn_fc_w"], a["L0_ffn_fc_b"]), down(a["L0_ffn_proj_w"]), a["L0_ffn_proj_b"]
    K["up1"], K["down1"] = up(a["L1_ffn_wi"], np.zeros((E1, F), f)), down(a["L1_ffn_wo"])
    return {n: np.ascontiguousarray(v) for n, v in K.items()}


def kernel(**inputs):
    import concourse.bacc as bacc
    from concourse.bass_utils import run_bass_kernel_spmd

    nc = bacc.Bacc("TRN2", target_bir_lowering=False, num_devices=1)
    arrays = layouts({n: np.asarray(v) for n, v in inputs.items()})
    K = {n: nc.dram_tensor(f"in_{n}", v.shape, mybir.dt.from_np(v.dtype), kind="ExternalInput").ap() for n, v in arrays.items()}
    out = nc.dram_tensor("out", (IMAGES, SEQ, D), F32, kind="ExternalOutput").ap()
    vit_tower(nc, K, out)
    r = run_bass_kernel_spmd(nc, [{f"in_{n}": v for n, v in arrays.items()}], core_ids=[0])
    return r.results[0]["out"]
```
